# Optimizing a Trainium2 kernel written in Bass

```python
import numpy as np
import jax
import jax.numpy as jnp

def _softmax(x, axis=-1):
    return jax.nn.softmax(x, axis=axis)

def _gelu(x):
    return jax.nn.gelu(x, approximate=True)

def _silu(x):
    return jax.nn.silu(x)

def _sigmoid(x):
    return jax.nn.sigmoid(x)

def _layernorm(x, axis=-1, eps=1e-05):
    m = jnp.mean(x, axis=axis, keepdims=True)
    v = jnp.var(x, axis=axis, keepdims=True)
    return (x - m) / jnp.sqrt(v + eps)

def _scatter_add(tgt, idx, src, axis=0):
    return tgt.at[idx].add(src)

def _segment_sum(src, seg, n):
    return jax.ops.segment_sum(src, seg, n)
kernel_name = 'mk_adaln_d2_jaxref_r8_73925c'

def setup_inputs(seed: int=0):
    np.random.seed(seed)
    _w = jnp.asarray

    def _L0_attn_setup():
        import jax, jax.numpy as jnp
        import numpy as np
        D_MODEL = 128
        K_HEADS = 32
        ANCHOR = 4
        M_THETA = 4
        CONV_K = 4
        H_DIM = D_MODEL // K_HEADS
        TOTAL = 2 * D_MODEL + K_HEADS
        key = jax.random.key(seed)
        ks = jax.random.split(key, 12)
        B, L = (4, 256)
        x = jax.random.normal(ks[0], (B, L, D_MODEL), dtype=jnp.float32)
        W_in = jax.random.normal(ks[1], (D_MODEL, TOTAL), dtype=jnp.float32) / np.sqrt(D_MODEL)
        w_conv = jax.random.normal(ks[2], (CONV_K, 1, TOTAL), dtype=jnp.float32) / np.sqrt(CONV_K)
        b_conv = jnp.zeros((TOTAL,), dtype=jnp.float32)
        grid = np.linspace(-np.pi / 3, np.pi / 3, M_THETA, dtype=np.float32)
        theta = jnp.asarray(np.tile(grid.reshape(1, 1, 1, 1, M_THETA), (1, 1, K_HEADS, H_DIM, 1)))
        dec_rates = np.geomspace(0.001, 0.1, K_HEADS - ANCHOR).astype(np.float32)
        decay_slopes = jnp.asarray(np.log(np.exp(dec_rates) - 1))
        anc_rates = np.geomspace(0.01, 0.1, ANCHOR).astype(np.float32)
        anchor_slopes = jnp.asarray(np.log(np.exp(anc_rates) - 1))
        score_scale = jnp.ones((K_HEADS,), dtype=jnp.float32)
        deriv_logits = jnp.asarray([5.0, 0.0, 0.0], dtype=jnp.float32)
        norm_scale = jnp.ones((2 * H_DIM * M_THETA,), dtype=jnp.float32)
        lim = np.sqrt(6.0 / (H_DIM * M_THETA + H_DIM))
        W_re = jax.random.uniform(ks[3], (H_DIM * M_THETA, H_DIM), jnp.float32, -lim, lim)
        W_im = jax.random.uniform(ks[4], (H_DIM * M_THETA, H_DIM), jnp.float32, -lim, lim)
        W_out = jax.random.normal(ks[5], (D_MODEL, D_MODEL), dtype=jnp.float32) / np.sqrt(D_MODEL)
        return {'x': x, 'W_in': W_in, 'w_conv': w_conv, 'b_conv': b_conv, 'theta': theta, 'decay_slopes': decay_slopes, 'anchor_slopes': anchor_slopes, 'score_scale': score_scale, 'deriv_logits': deriv_logits, 'norm_scale': norm_scale, 'W_re': W_re, 'W_im': W_im, 'W_out': W_out}
    _L0_attn_in = _L0_attn_setup()

    def _L0_ffn_setup():
        import jax, jax.numpy as jnp
        import numpy as np
        H = 128
        E = 64
        K = 8
        G = 8
        TOPK_GROUP = 4
        I_MOE = 64
        I_SHARED = 256
        SCALE = 2.5

        def relu2(x):
            return jnp.square(jax.nn.relu(x))

        def _route(xf, router_w, correction_bias):
            T = xf.shape[0]
            logits = xf @ router_w.T
            scores = jax.nn.sigmoid(logits)
            sfc = scores + correction_bias[None, :]
            grp = sfc.reshape(T, G, E // G)
            top2, _ = jax.lax.top_k(grp, 2)
            group_scores = top2.sum(-1)
            _, gidx = jax.lax.top_k(group_scores, TOPK_GROUP)
            gmask = jnp.zeros((T, G), sfc.dtype).at[jnp.arange(T)[:, None], gidx].set(1.0)
            emask = jnp.repeat(gmask, E // G, axis=1)
            masked = jnp.where(emask > 0, sfc, 0.0)
            _, tidx = jax.lax.top_k(masked, K)
            tw = jnp.take_along_axis(scores, tidx, axis=1)
            tw = tw / (tw.sum(-1, keepdims=True) + 1e-20)
            return (tidx, tw * SCALE)
        key = jax.random.key(seed)
        ks = jax.random.split(key, 7)
        x = jax.random.normal(ks[0], (2, 128, H), dtype=jnp.float32)
        router_w = jax.random.normal(ks[1], (E, H), dtype=jnp.float32) * 0.02
        correction_bias = jax.random.normal(ks[2], (E,), dtype=jnp.float32) * 0.01
        up_w = jax.random.normal(ks[3], (E, H, I_MOE), dtype=jnp.float32) * 0.02
        down_w = jax.random.normal(ks[4], (E, I_MOE, H), dtype=jnp.float32) * 0.02
        shared_up_w = jax.random.normal(ks[5], (H, I_SHARED), dtype=jnp.float32) * 0.02
        shared_down_w = jax.random.normal(ks[6], (I_SHARED, H), dtype=jnp.float32) * 0.02
        return {'x': x, 'router_w': router_w, 'correction_bias': correction_bias, 'up_w': up_w, 'down_w': down_w, 'shared_up_w': shared_up_w, 'shared_down_w': shared_down_w}
    _L0_ffn_in = _L0_ffn_setup()
    _L0_c = _w((lambda *s: np.random.randn(*s).astype(np.float32) * 0.05)(1, 128))
    _L0_wmod = _w((lambda *s: np.random.randn(*s).astype(np.float32) * 0.05)(128, 6 * 128) * 128 ** (-0.5))

    def _L1_attn_setup():
        import jax, jax.numpy as jnp
        import numpy as np
        B, S, E = (4, 256, 128)
        H, KVH = (16, 4)
        D = E // H
        QL, KVL = (64, 32)
        ROPE_BASE = 10000.0

        def _rope(x):
            d = x.shape[-1]
            inv_freq = 1.0 / ROPE_BASE ** (jnp.arange(0, d, 2, dtype=jnp.float32) / d)
            t = jnp.arange(x.shape[1], dtype=jnp.float32)
            freqs = jnp.outer(t, inv_freq)
            cos = jnp.cos(freqs)[None, :, None, :].astype(x.dtype)
            sin = jnp.sin(freqs)[None, :, None, :].astype(x.dtype)
            x1, x2 = (x[..., ::2], x[..., 1::2])
            r1 = x1 * cos - x2 * sin
            r2 = x1 * sin + x2 * cos
            return jnp.stack([r1, r2], axis=-1).reshape(x.shape)
        key = jax.random.key(seed)
        ks = jax.random.split(key, 7)
        s = 0.02
        return {'x': jax.random.normal(ks[0], (B, S, E), dtype=jnp.float32), 'Wqa': jax.random.normal(ks[1], (E, QL), dtype=jnp.float32) * s, 'Wqb': jax.random.normal(ks[2], (QL, E), dtype=jnp.float32) * s, 'Wkva': jax.random.normal(ks[3], (E, KVL), dtype=jnp.float32) * s, 'Wkvb': jax.random.normal(ks[4], (KVL, KVH * D * 2), dtype=jnp.float32) * s, 'Wout': jax.random.normal(ks[5], (E, E), dtype=jnp.float32) * s, 'bout': jax.random.normal(ks[6], (E,), dtype=jnp.float32) * s}
    _L1_attn_in = _L1_attn_setup()

    def _L1_ffn_setup():
        import jax, jax.numpy as jnp
        import numpy as np
        B, S, H = (2, 128, 128)
        E, F = (8, 512)
        GATE_TEMP = 0.1
        key = jax.random.key(seed)
        ks = jax.random.split(key, 6)
        s_h = 1.0 / np.sqrt(H)
        s_f = 1.0 / np.sqrt(F)
        return {'hidden_states': jax.random.normal(ks[0], (B, S, H), dtype=jnp.float32), 'w_router': jax.random.normal(ks[1], (H, E), dtype=jnp.float32) * s_h, 'w_gating': jax.random.normal(ks[2], (H, E), dtype=jnp.float32) * s_h, 'w_gate': jax.random.normal(ks[3], (E, H, F), dtype=jnp.float32) * s_h, 'w_up': jax.random.normal(ks[4], (E, H, F), dtype=jnp.float32) * s_h, 'w_down': jax.random.normal(ks[5], (E, F, H), dtype=jnp.float32) * s_f}
    _L1_ffn_in = _L1_ffn_setup()
    _L1_c = _w((lambda *s: np.random.randn(*s).astype(np.float32) * 0.05)(1, 128))
    _L1_wmod = _w((lambda *s: np.random.randn(*s).astype(np.float32) * 0.05)(128, 6 * 128) * 128 ** (-0.5))
    _d = {'L0_attn_x': _L0_attn_in['x'], 'L0_attn_W_in': _L0_attn_in['W_in'], 'L0_attn_w_conv': _L0_attn_in['w_conv'], 'L0_attn_b_conv': _L0_attn_in['b_conv'], 'L0_attn_theta': _L0_attn_in['theta'], 'L0_attn_decay_slopes': _L0_attn_in['decay_slopes'], 'L0_attn_anchor_slopes': _L0_attn_in['anchor_slopes'], 'L0_attn_score_scale': _L0_attn_in['score_scale'], 'L0_attn_deriv_logits': _L0_attn_in['deriv_logits'], 'L0_attn_norm_scale': _L0_attn_in['norm_scale'], 'L0_attn_W_re': _L0_attn_in['W_re'], 'L0_attn_W_im': _L0_attn_in['W_im'], 'L0_attn_W_out': _L0_attn_in['W_out'], 'L0_ffn_router_w': _L0_ffn_in['router_w'], 'L0_ffn_correction_bias': _L0_ffn_in['correction_bias'], 'L0_ffn_up_w': _L0_ffn_in['up_w'], 'L0_ffn_down_w': _L0_ffn_in['down_w'], 'L0_ffn_shared_up_w': _L0_ffn_in['shared_up_w'], 'L0_ffn_shared_down_w': _L0_ffn_in['shared_down_w'], 'L0_c': _L0_c, 'L0_wmod': _L0_wmod, 'L1_attn_Wqa': _L1_attn_in['Wqa'], 'L1_attn_Wqb': _L1_attn_in['Wqb'], 'L1_attn_Wkva': _L1_attn_in['Wkva'], 'L1_attn_Wkvb': _L1_attn_in['Wkvb'], 'L1_attn_Wout': _L1_attn_in['Wout'], 'L1_attn_bout': _L1_attn_in['bout'], 'L1_ffn_w_router': _L1_ffn_in['w_router'], 'L1_ffn_w_gating': _L1_ffn_in['w_gating'], 'L1_ffn_w_gate': _L1_ffn_in['w_gate'], 'L1_ffn_w_up': _L1_ffn_in['w_up'], 'L1_ffn_w_down': _L1_ffn_in['w_down'], 'L1_c': _L1_c, 'L1_wmod': _L1_wmod}
    _x0 = _d['L0_attn_x']
    _d['L0_attn_x'] = jax.random.normal(jax.random.fold_in(jax.random.key(seed), 1), (1, 2048, 128), dtype=_x0.dtype)
    del _x0
    return _d

def reference(L0_attn_x, L0_attn_W_in, L0_attn_w_conv, L0_attn_b_conv, L0_attn_theta, L0_attn_decay_slopes, L0_attn_anchor_slopes, L0_attn_score_scale, L0_attn_deriv_logits, L0_attn_norm_scale, L0_attn_W_re, L0_attn_W_im, L0_attn_W_out, L0_ffn_router_w, L0_ffn_correction_bias, L0_ffn_up_w, L0_ffn_down_w, L0_ffn_shared_up_w, L0_ffn_shared_down_w, L0_c, L0_wmod, L1_attn_Wqa, L1_attn_Wqb, L1_attn_Wkva, L1_attn_Wkvb, L1_attn_Wout, L1_attn_bout, L1_ffn_w_router, L1_ffn_w_gating, L1_ffn_w_gate, L1_ffn_w_up, L1_ffn_w_down, L1_c, L1_wmod):

    def _L0_attn_ref(x, W_in, w_conv, b_conv, theta, decay_slopes, anchor_slopes, score_scale, deriv_logits, norm_scale, W_re, W_im, W_out):
        import jax, jax.numpy as jnp
        import numpy as np
        D_MODEL = 128
        K_HEADS = 32
        ANCHOR = 4
        M_THETA = 4
        CONV_K = 4
        H_DIM = D_MODEL // K_HEADS
        TOTAL = 2 * D_MODEL + K_HEADS
        B, L, D = x.shape
        K, H, M = (K_HEADS, H_DIM, M_THETA)
        z = x @ W_in
        z = jax.lax.conv_general_dilated(z, w_conv, window_strides=(1,), padding=[(CONV_K - 1, 0)], feature_group_count=z.shape[-1], dimension_numbers=('NWC', 'WIO', 'NWC')) + b_conv
        x_val = z[..., :D].reshape(B, L, K, H)
        x_gate = jax.nn.silu(z[..., D:2 * D])
        s_raw = z[..., 2 * D:].reshape(B, L, K, 1)
        pos = jnp.arange(L, dtype=jnp.float32)
        sd = jax.nn.softplus(decay_slopes)
        dist = jnp.maximum(L - 1 - pos, 0.0)
        w_dec = jnp.exp(-sd[None, :] * dist[:, None])
        sa = jax.nn.softplus(anchor_slopes)
        w_anc = jnp.exp(-sa[None, :] * pos[:, None])
        time_w = jnp.concatenate([w_dec, w_anc], axis=1)[None, :, :, None]
        p = jnp.exp(jnp.clip(score_scale[None, None, :, None] * s_raw, -20.0, 20.0))
        x5 = x_val[..., None]
        phi = x5 * theta
        cos_b, sin_b = (jnp.cos(phi), jnp.sin(phi))
        w = jax.nn.softmax(deriv_logits)
        poly = w[0] + w[1] * x5 - w[2] * jnp.square(x5)
        re_m = poly * cos_b
        im_m = poly * sin_b
        p_w = (p * time_w)[..., None]
        flat = (B, L, K * H * M)
        merged = jnp.concatenate([(p_w * re_m).reshape(flat), (p_w * im_m).reshape(flat), jnp.broadcast_to(p_w, (B, L, K, H, M)).reshape(flat)], axis=-1)
        cs = jnp.cumsum(merged, axis=1)
        num_re, num_im, den = jnp.split(cs, 3, axis=-1)
        inv_den = 1.0 / jnp.maximum(den, 0.0001)
        re = (num_re * inv_den).reshape(B, L, K, H * M)
        im = (num_im * inv_den).reshape(B, L, K, H * M)
        mean_sq = (jnp.sum(jnp.square(re), -1) + jnp.sum(jnp.square(im), -1)) / (2.0 * H * M)
        rsq = jax.lax.rsqrt(mean_sq[..., None] + 1e-05)
        re_n = re * rsq * norm_scale[:H * M]
        im_n = im * rsq * norm_scale[H * M:]
        y = re_n @ W_re + im_n @ W_im
        y = y.reshape(B, L, D)
        return y * x_gate @ W_out

    def _L0_ffn_ref(x, router_w, correction_bias, up_w, down_w, shared_up_w, shared_down_w):
        import jax, jax.numpy as jnp
        import numpy as np
        H = 128
        E = 64
        K = 8
        G = 8
        TOPK_GROUP = 4
        I_MOE = 64
        I_SHARED = 256
        SCALE = 2.5

        def relu2(x):
            return jnp.square(jax.nn.relu(x))

        def _route(xf, router_w, correction_bias):
            T = xf.shape[0]
            logits = xf @ router_w.T
            scores = jax.nn.sigmoid(logits)
            sfc = scores + correction_bias[None, :]
            grp = sfc.reshape(T, G, E // G)
            top2, _ = jax.lax.top_k(grp, 2)
            group_scores = top2.sum(-1)
            _, gidx = jax.lax.top_k(group_scores, TOPK_GROUP)
            gmask = jnp.zeros((T, G), sfc.dtype).at[jnp.arange(T)[:, None], gidx].set(1.0)
            emask = jnp.repeat(gmask, E // G, axis=1)
            masked = jnp.where(emask > 0, sfc, 0.0)
            _, tidx = jax.lax.top_k(masked, K)
            tw = jnp.take_along_axis(scores, tidx, axis=1)
            tw = tw / (tw.sum(-1, keepdims=True) + 1e-20)
            return (tidx, tw * SCALE)
        B, S, Hd = x.shape
        xf = x.reshape(-1, Hd)
        T = xf.shape[0]
        tidx, tw = _route(xf.astype(jnp.float32), router_w, correction_bias)
        combine = jnp.zeros((T, E), xf.dtype).at[jnp.arange(T)[:, None], tidx].add(tw.astype(xf.dtype))

        def body(acc, ew):
            wu, wd, c = ew
            return (acc + c[:, None] * (relu2(xf @ wu) @ wd), None)
        routed, _ = jax.lax.scan(body, jnp.zeros_like(xf), (up_w, down_w, combine.T))
        shared = relu2(xf @ shared_up_w) @ shared_down_w
        return (routed + shared).reshape(B, S, Hd)

    def _L1_attn_ref(x, Wqa, Wqb, Wkva, Wkvb, Wout, bout):
        import jax, jax.numpy as jnp
        import numpy as np
        B, S, E = (4, 256, 128)
        H, KVH = (16, 4)
        D = E // H
        QL, KVL = (64, 32)
        ROPE_BASE = 10000.0

        def _rope(x):
            d = x.shape[-1]
            inv_freq = 1.0 / ROPE_BASE ** (jnp.arange(0, d, 2, dtype=jnp.float32) / d)
            t = jnp.arange(x.shape[1], dtype=jnp.float32)
            freqs = jnp.outer(t, inv_freq)
            cos = jnp.cos(freqs)[None, :, None, :].astype(x.dtype)
            sin = jnp.sin(freqs)[None, :, None, :].astype(x.dtype)
            x1, x2 = (x[..., ::2], x[..., 1::2])
            r1 = x1 * cos - x2 * sin
            r2 = x1 * sin + x2 * cos
            return jnp.stack([r1, r2], axis=-1).reshape(x.shape)
        b, s, _ = x.shape
        scale = D ** (-0.5)
        q = (x @ Wqa @ Wqb).reshape(b, s, H, D)
        kv = (x @ Wkva @ Wkvb).reshape(b, s, KVH, D, 2)
        k, v = (kv[..., 0], kv[..., 1])
        q = _rope(q)
        k = _rope(k)
        g = H // KVH
        k = jnp.repeat(k, g, axis=2)
        v = jnp.repeat(v, g, axis=2)
        scores = jnp.einsum('bqhd,bkhd->bhqk', q, k) * scale
        causal = jnp.triu(jnp.ones((s, s), dtype=bool), k=1)
        scores = jnp.where(causal[None, None], -jnp.inf, scores)
        w = jax.nn.softmax(scores, axis=-1)
        out = jnp.einsum('bhqk,bkhd->bqhd', w, v).reshape(b, s, E)
        return out @ Wout + bout

    def _L1_ffn_ref(hidden_states, w_router, w_gating, w_gate, w_up, w_down):
        import jax, jax.numpy as jnp
        import numpy as np
        B, S, H = (2, 128, 128)
        E, F = (8, 512)
        GATE_TEMP = 0.1
        x = hidden_states
        router_probs = jax.nn.softmax(jnp.einsum('bsh,he->bse', x, w_router), axis=-1)
        gate_weights = jax.nn.softmax(jnp.einsum('bsh,he->bse', x, w_gating) / GATE_TEMP, axis=-1)
        g = jnp.einsum('bsh,ehf->ebsf', x, w_gate)
        u = jnp.einsum('bsh,ehf->ebsf', x, w_up)
        h = jax.nn.silu(g) * u
        expert_out = jnp.einsum('ebsf,efh->ebsh', h, w_down)
        cw = router_probs * gate_weights
        cw = cw / (jnp.sum(cw, axis=-1, keepdims=True) + 1e-09)
        out = jnp.einsum('ebsh,bse->bsh', expert_out, cw)
        return out
    x = L0_attn_x
    mod = (_silu(L0_c) @ L0_wmod).reshape(L0_c.shape[0], 6, 1, -1)
    sa, ca, ga, sb, cb, gb = (mod[:, 0], mod[:, 1], mod[:, 2], mod[:, 3], mod[:, 4], mod[:, 5])
    ga = (2 * (ga >= 0) - 1) * jnp.maximum(jnp.abs(ga), 0.25)
    gb = (2 * (gb >= 0) - 1) * jnp.maximum(jnp.abs(gb), 0.25)
    h = _layernorm(x, axis=-1) * (1 + ca) + sa
    x = x + ga * _L0_attn_ref(h, L0_attn_W_in, L0_attn_w_conv, L0_attn_b_conv, L0_attn_theta, L0_attn_decay_slopes, L0_attn_anchor_slopes, L0_attn_score_scale, L0_attn_deriv_logits, L0_attn_norm_scale, L0_attn_W_re, L0_attn_W_im, L0_attn_W_out)
    h = _layernorm(x, axis=-1) * (1 + cb) + sb
    x = x + gb * _L0_ffn_ref(h, L0_ffn_router_w, L0_ffn_correction_bias, L0_ffn_up_w, L0_ffn_down_w, L0_ffn_shared_up_w, L0_ffn_shared_down_w)
    mod = (_silu(L1_c) @ L1_wmod).reshape(L1_c.shape[0], 6, 1, -1)
    sa, ca, ga, sb, cb, gb = (mod[:, 0], mod[:, 1], mod[:, 2], mod[:, 3], mod[:, 4], mod[:, 5])
    ga = (2 * (ga >= 0) - 1) * jnp.maximum(jnp.abs(ga), 0.25)
    gb = (2 * (gb >= 0) - 1) * jnp.maximum(jnp.abs(gb), 0.25)
    h = _layernorm(x, axis=-1) * (1 + ca) + sa
    x = x + ga * _L1_attn_ref(h, L1_attn_Wqa, L1_attn_Wqb, L1_attn_Wkva, L1_attn_Wkvb, L1_attn_Wout, L1_attn_bout)
    h = _layernorm(x, axis=-1) * (1 + cb) + sb
    x = x + gb * _L1_ffn_ref(h, L1_ffn_w_router, L1_ffn_w_gating, L1_ffn_w_gate, L1_ffn_w_up, L1_ffn_w_down)
    return x

_drawn_inputs = setup_inputs


def setup_inputs(seed=0):
    import zlib

    import numpy as np

    out = dict(_drawn_inputs(seed))
    spreads = {'L0_attn_b_conv': (0.0, 0.296),
     'L0_attn_score_scale': (1.0, 0.6),
     'L0_attn_norm_scale': (1.0, 0.2)}
    factors = {'L0_attn_anchor_slopes': 60.336,
     'L0_ffn_router_w': 8.0,
     'L0_ffn_correction_bias': 8.0,
     'L0_ffn_up_w': 8.0,
     'L0_ffn_down_w': 8.0,
     'L0_ffn_shared_up_w': 8.0,
     'L0_ffn_shared_down_w': 8.0,
     'L1_attn_Wqa': 8.0,
     'L1_attn_Wqb': 8.0,
     'L1_attn_Wkva': 8.0,
     'L1_attn_Wkvb': 8.0,
     'L1_attn_Wout': 8.0,
     'L1_attn_bout': 32.119,
     'L1_ffn_w_router': 5.85}
    for name, (base, spread) in spreads.items():
        noise = np.random.default_rng([zlib.crc32(name.encode()), seed]).standard_normal(out[name].shape)
        drawn = base * np.exp(spread * noise) if base else spread * noise
        out[name] = jnp.asarray(drawn.astype(out[name].dtype))
    for name, factor in factors.items():
        out[name] = (out[name] * factor).astype(out[name].dtype)
    return out
```

```python
from contextlib import ExitStack

import concourse.bass as bass
from concourse import mybir

F32 = mybir.dt.float32
BF16 = mybir.dt.bfloat16
ALU = mybir.AluOpType
ACT = mybir.ActivationFunctionType
AX_X = mybir.AxisListType.X

P = 128
T = 2048
D = 128
NT = T // P
CW = 512
NC = T // CW
TPC = CW // P
K0, H0, M0 = 32, 4, 4
TAPS = 4
E0, I0, ISH = 64, 64, 256
NG0, GE0, TOPG, TOPK = 8, 8, 4, 8
GP = 4
NPAIR = E0 // 2
NLOAD = NPAIR // GP
NSH = ISH // P
H1, G1, HD = 16, 4, 8
QL, KVL = 64, 32
HPG = H1 // G1
NSPLIT = 3
KROWS = NSPLIT * NSPLIT * HD
E1, F1 = 8, 512
FT = F1 // P

PI = 3.1415925
HALF_PI = 1.5707963267948966
INV_2PI = 0.15915494309189535
TWO_PI_HI = 6.28125
TWO_PI_LO = 0.0019353071795864769
ROUND = 12582912.0
BIG = 1.0e30
EPS = 1e-5


def p1_units():
    return [(t, u) for t in range(NT) for u in range(t // TPC + 1)]


def p2_steps():
    return [(c, j) for c in range(NC) for j in range(TPC * c + TPC)]


def adaln_two_layers(nc, A, out):
    ctx = ExitStack()
    with ctx:
        def sb(name, shape, dt=F32):
            return ctx.enter_context(nc.sbuf_tensor(name, shape, dt))

        def sem(name):
            return ctx.enter_context(nc.semaphore(name))

        xt = sb("xt", [P, NT, D])
        xn = sb("xn", [P, NT, D])
        PAD = TAPS - 1
        hT = sb("hT", [P, PAD + T])
        wslot = sb("wslot", [P, 2, 1536])
        ident = sb("ident", [P, P])
        identb = sb("identb", [P, P], BF16)
        maskqk = sb("maskqk", [P, P], BF16)
        maskkq = sb("maskkq", [P, P], BF16)
        blk = sb("blk", [P, P])
        stats = sb("stats", [P, NT, 6])
        mv = sb("mv", [P, NT, 2])
        sd = sb("sd", [P, NT])
        rstd = sb("rstd", [P, NT])
        modc = sb("modc", [P, 2, 8])
        gar = sb("gar", [P, 2, D])
        wo0 = sb("wo0", [P, D])
        wo1 = sb("wo1", [P, D])
        bo1 = sb("bo1", [P, D])
        wqa = sb("wqa", [P, QL])
        wkva = sb("wkva", [P, KVL])
        wqb = sb("wqb", [QL, 2, D])
        wkvb = sb("wkvb", [KVL, G1 * HD * 2])
        wkk = sb("wkk", [KVL, 3, G1 * HD])
        wr1 = sb("wr1", [P, 2 * E1])
        rwn = sb("rwn", [E0, D])
        rwT = sb("rwT", [P, E0])
        cbias = sb("cbias", [P, E0])
        tri = sb("tri", [P, NG0, NG0])
        tiny = sb("tiny", [P, 64])
        AW = 40000
        arena = sb("arena", [P, AW])
        ps = ctx.enter_context(nc.psum_tensor("ps", [P, 8, CW], F32))

        at = [0]

        def take(shape, dt=F32, parts=P):
            n = 1
            for s in shape:
                n *= s
            words = n if dt == F32 else (n + 1) // 2
            v = arena[0:parts, at[0]:at[0] + words]
            at[0] += words
            assert at[0] <= AW, at[0]
            if dt != F32:
                v = v.bitcast(dt)
            if len(shape) > 1:
                names = "abcd"[:len(shape)]
                v = v.rearrange("p (" + " ".join(names) + ") -> p " + " ".join(names),
                                **{names[i]: shape[i] for i in range(1, len(shape))})
            return v

        wmod = take([2, 6 * D])
        scb = take([2, P])
        win = take([2 * D + K0])
        wcv = take([TAPS, 2 * D + K0])
        wfold = take([TAPS, 3, P])
        wrows = take([2, M0, H0])
        bd = take([2, M0, K0, H0])
        tw = take([T])
        pw = take([T])
        gate = take([T])
        yg = xn[:, :, :].rearrange("p n d -> p (n d)")
        den = take([T])
        xv = take([2, CW])
        phi = take([2, M0, CW])
        ang = take([2, M0, CW])
        nums = take([2, 2 * M0, CW])
        sqs = take([2 * M0, CW])
        pw_poly = take([2, CW])
        tmp = take([3, CW])
        ssq = take([CW])
        fac = take([2, CW])
        at[0] = 0
        scores = take([NT, E0])
        sfc = take([NT, E0])
        msk = take([NT, E0])
        b1 = take([NT, E0])
        b2 = take([NT, E0])
        comb3 = take([NT, 3, E0], BF16)
        combT = take([T], BF16)
        combL = take([T], BF16)
        sel = take([NPAIR, P], BF16)
        gsm = take([10, NT * NG0])
        top8 = take([NT, 8])
        wsum = take([3, NT])
        wsh = take([2, ISH])
        relu = take([2, CW])
        gsq = take([2, CW])
        hid = take([2, CW])
        yT = take([T])
        assert at[0] <= AW
        at[0] = 0
        qst = take([H1, T], BF16)
        kst = take([G1, T], BF16)
        vaug = take([NT, G1, 32])
        ropec = take([T])
        ropes = take([T])
        rope_at = at[0]
        latq = take([2, CW])
        latk = take([2, CW])
        ra = take([2, CW])
        rb = take([2, CW])
        rk = take([2, CW])
        rl = take([2, CW])
        q3 = take([2, NSPLIT, CW], BF16)
        k3 = take([2, NSPLIT, CW], BF16)
        probs = arena[:, rope_at:rope_at + 2 * HPG * CW].rearrange("p (a b c) -> p a b c", a=2, b=HPG)
        mx = take([HPG, NT, NC])
        nmx = take([HPG * NT])
        nres = take([HPG * NT])
        nm2 = take([2, HPG * NT], BF16)
        nrow = take([P], BF16)
        oT = take([CW])
        rden = take([TPC, HPG])
        otok = xn
        oTT = take([2, CW])
        at[0] = 0
        hcw = take([E1, T])
        silg = take([2, CW])
        hid1 = take([2, CW])
        lg = take([NT, 2 * E1])
        ex = take([NT, 2 * E1])
        cw = take([NT, E1])
        sm = take([6, NT * 2])
        y1T = take([T])
        obuf = take([NT, D])

        qs_dram = nc.dram_tensor("q_parts", [NSPLIT, P, T], BF16).ap()
        ks_dram = nc.dram_tensor("k_parts", [NSPLIT, G1 * HD, T], BF16).ap()

        ld_x = [sem(f"ld_x{c}") for c in range(NC)]
        ld_mod = sem("ld_mod")
        ld_a = sem("ld_a")
        ld_const = sem("ld_const")
        ld_small = sem("ld_small")
        ld_b = sem("ld_b")
        ld_c = sem("ld_c")
        ld_sel = sem("ld_sel")
        ld_rope = sem("ld_rope")
        ld_w0 = [sem(f"ld_w0_{i}") for i in range(2)]
        ld_w1 = [sem(f"ld_w1_{i}") for i in range(2)]
        st_qk = [sem(f"st_qk{b}") for b in range(2)]
        ld_kst = sem("ld_kst")
        ld_qst = [sem(f"ld_qst{g}") for g in range(G1)]
        ld_nm = [sem(f"ld_nm{g}") for g in range(G1)]
        st_out = sem("st_out")
        s_v = sem("s_v")
        s_a = sem("s_a")
        pad_zero = sem("pad_zero")
        silu_c = sem("silu_c")
        scb_ready = sem("scb_ready")
        mod_mm = sem("mod_mm")
        mod_ready = sem("mod_ready")
        slope_in = sem("slope_in")
        slope_e = sem("slope_e")
        slope_u = sem("slope_u")
        slope_l = sem("slope_l")
        slope_ready = sem("slope_ready")
        fold_ready = sem("fold_ready")
        tw_ready = sem("tw_ready")
        dl_max = sem("dl_max")
        dl_exp = sem("dl_exp")
        bd_ready = sem("bd_ready")
        wo_ready = sem("wo_ready")
        N_LN = 4
        ln_var = [sem(f"ln_var{i}") for i in range(N_LN)]
        ln_sd = [sem(f"ln_sd{i}") for i in range(N_LN)]
        ln_xn = [sem(f"ln_xn{i}") for i in range(N_LN)]
        ln_tr = [sem(f"ln_tr{i}") for i in range(N_LN)]
        ln_h = [sem(f"ln_h{i}") for i in range(N_LN)]
        zs_mm = sem("zs_mm")
        zs_lin = sem("zs_lin")
        zs_exp = sem("zs_exp")
        pw_ready = sem("pw_ready")
        zv_mm = sem("zv_mm")
        zg_mm = sem("zg_mm")
        xv_ready = sem("xv_ready")
        gate_ready = sem("gate_ready")
        phi_ready = sem("phi_ready")
        trig_ready = sem("trig_ready")
        num_ready = sem("num_ready")
        sq_ready = sem("sq_ready")
        y_mm = sem("y_mm")
        ss_mm = sem("ss_mm")
        q_ready = sem("q_ready")
        rt_ready = sem("rt_ready")
        yg_ready = sem("yg_ready")
        o0_mm = sem("o0_mm")
        x1_ready = sem("x1_ready")
        rw_tr = sem("rw_tr")
        rw_ready = sem("rw_ready")
        lg_mm = sem("lg_mm")
        sig_ready = sem("sig_ready")
        sh_up = sem("sh_up")
        sh_hid = sem("sh_hid")
        sh_down = sem("sh_down")
        comb_ready = sem("comb_ready")
        comb_tr = sem("comb_tr")
        comb_T = sem("comb_T")
        moe_up = sem("moe_up")
        moe_cb = sem("moe_cb")
        moe_relu = sem("moe_relu")
        moe_g = sem("moe_g")
        moe_hid = sem("moe_hid")
        moe_down = sem("moe_down")
        y0_ready = sem("y0_ready")
        y0_tr = sem("y0_tr")
        x2_ready = sem("x2_ready")
        wk_ready = sem("wk_ready")
        kones = sem("kones")
        vzero = sem("vzero")
        mxinit = sem("mxinit")
        lat_mm = sem("lat_mm")
        lat_ready = sem("lat_ready")
        qk_mm = sem("qk_mm")
        v_mm = sem("v_mm")
        v_ready = sem("v_ready")
        rope_done = sem("rope_done")
        split_ready = sem("split_ready")
        x2b_ready = sem("x2b_ready")
        p1_mm = sem("p1_mm")
        p1_max = sem("p1_max")
        nm_ready = sem("nm_ready")
        nm_tr = sem("nm_tr")
        nm_row = sem("nm_row")
        p2_mm = sem("p2_mm")
        p2_exp = sem("p2_exp")
        pv_mm = sem("pv_mm")
        o_copy = sem("o_copy")
        o_tr = sem("o_tr")
        o_norm = sem("o_norm")
        ot_tr = sem("ot_tr")
        ot_ready = sem("ot_ready")
        o1_mm = sem("o1_mm")
        x3_ready = sem("x3_ready")
        lg1_mm = sem("lg1_mm")
        lg1_max = sem("lg1_max")
        lg1_exp = sem("lg1_exp")
        cw_ready = sem("cw_ready")
        cw_tr = sem("cw_tr")
        hcw_ready = sem("hcw_ready")
        ffn_g = sem("ffn_g")
        ffn_u = sem("ffn_u")
        ffn_silu = sem("ffn_silu")
        ffn_hid = sem("ffn_hid")
        ffn_down = sem("ffn_down")
        y1_ready = sem("y1_ready")
        y1_tr = sem("y1_tr")
        out_ready = sem("out_ready")

        UNITS = p1_units()
        STEPS = p2_steps()
        NU, NS = len(UNITS), len(STEPS)
        PER_STEP = 5

        def moe_units(lo, hi):
            return [(k // NC, k % NC) for k in range(lo, hi)]

        MU = 2 * GP * NC
        assert MU == 2 * FT * NC
        N_IT0 = NLOAD // 2
        N_IT1 = E1 // 2

        def up0(slot, pair):
            return wslot[:, slot, pair * P:(pair + 1) * P]

        def down0(slot, pair):
            return wslot[:, slot, GP * P + pair * P:GP * P + (pair + 1) * P]

        def w1(slot, which, ft):
            return wslot[:, slot, which * F1 + ft * P:which * F1 + (ft + 1) * P]

        def tiles(c):
            return range(TPC * c, TPC * c + TPC)

        def chunk(c):
            return slice(c * CW, (c + 1) * CW)

        def bank_of(step_bank, w0, w1_):
            return ps[:, step_bank, w0:w1_]

        col = {n: i for i, n in enumerate(
            "c0 c1 sc0 sc1 bval bgate bs ssb ss slope nabs esl usl dsl msl rsl lsl zsl sp nsd".split())}

        def tc(name, n=1, parts=P):
            return tiny[0:parts, col[name]:col[name] + n]

        theta_c = tiny[:, 20:24]
        theta_n = tiny[:, 24:28]
        dlog = tiny[:, 28:31]
        dmax = tiny[:, 31:32]
        dexp = tiny[:, 32:35]
        dsum = tiny[:, 35:36]
        dw = tiny[:, 36:39]
        nsc = tiny[:, 39:40]
        gcol = tiny[:, 40:44]
        nscale = sb("nscale", [P, 2, M0])
        ones_w = sb("ones_w", [P, 1])

        block = ctx.enter_context(nc.Block())

        @block.sync
        def _(sp):
            sp.dma_start(tc("c0"), A["L0_c"].rearrange("a (p b) -> (a p) b", b=1)).then_inc(ld_mod, 16)
            sp.dma_start(tc("c1"), A["L1_c"].rearrange("a (p b) -> (a p) b", b=1)).then_inc(ld_mod, 16)
            sp.dma_start(wmod[:, 0, :], A["L0_wmod"]).then_inc(ld_mod, 16)
            sp.dma_start(wmod[:, 1, :], A["L1_wmod"]).then_inc(ld_mod, 16)
            x_v = A["L0_attn_x"].rearrange("a (n p) d -> p (a n) d", p=P)
            for c in range(NC):
                sp.dma_start(xt[:, TPC * c:TPC * c + TPC, :], x_v[:, TPC * c:TPC * c + TPC, :])\
                  .then_inc(ld_x[c], 16)
            sp.dma_start(ident[:, :], A["ident"]).then_inc(ld_const, 16)
            sp.dma_start(blk[:, :], A["blk"]).then_inc(ld_const, 16)
            sp.dma_start(win, A["L0_attn_W_in"]).then_inc(ld_a, 16)
            sp.dma_start(wcv, A["L0_attn_w_conv"].rearrange("k a c -> a (k c)").broadcast_to(
                [P, TAPS * (2 * D + K0)]).rearrange("p (k c) -> p k c", k=TAPS))\
              .then_inc(ld_a, 16)
            sp.dma_start(tw, A["dist"]).then_inc(ld_a, 16)
            bc = A["L0_attn_b_conv"]
            sp.dma_start(tc("bval"), bc[0:D].rearrange("(p b) -> p b", b=1)).then_inc(ld_small, 16)
            sp.dma_start(tc("bgate"), bc[D:2 * D].rearrange("(p b) -> p b", b=1)).then_inc(ld_small, 16)

            def by_head(dst, lo, n, src):
                sp.dma_start(dst[H0 * lo:H0 * (lo + n), :],
                             src.rearrange("(k h b) -> k h b", h=1, b=1).broadcast_to([n, H0, 1]))\
                  .then_inc(ld_small, 16)

            by_head(tc("bs"), 0, K0, bc[2 * D:2 * D + K0])
            by_head(tc("ss"), 0, K0, A["L0_attn_score_scale"])
            na = A["L0_attn_anchor_slopes"].shape[0]
            by_head(tc("slope"), 0, K0 - na, A["L0_attn_decay_slopes"])
            by_head(tc("slope"), K0 - na, na, A["L0_attn_anchor_slopes"])
            sp.dma_start(theta_c, A["L0_attn_theta"].rearrange("a b k h m -> (a b k h) m")).then_inc(ld_small, 16)
            sp.dma_start(dlog, A["L0_attn_deriv_logits"].rearrange("(a n) -> a n", a=1).broadcast_to([P, 3]))\
              .then_inc(ld_small, 16)
            for i, name in enumerate(("L0_attn_W_re", "L0_attn_W_im")):
                w = A[name].rearrange("(h m) j -> h (m j)", m=M0)
                sp.dma_start(wrows[:, i].rearrange("p m j -> p (m j)"),
                             w.unsqueeze(0).broadcast_to([K0, H0, M0 * H0])).then_inc(ld_small, 16)
            for i in range(2):
                n_v = A["L0_attn_norm_scale"].rearrange("(i h m) -> i h m", i=2, m=M0)[i]
                sp.dma_start(nscale[:, i, :],
                             n_v.unsqueeze(0).broadcast_to([K0, H0, M0])).then_inc(ld_small, 16)
            sp.dma_start(wo0[:, :], A["L0_attn_W_out"]).then_inc(ld_b, 16)
            sp.dma_start(rwn[:, :], A["L0_ffn_router_w"]).then_inc(ld_b, 16)
            sp.dma_start(cbias[:, :], A["L0_ffn_correction_bias"].rearrange("(a n) -> a n", a=1).broadcast_to([P, E0]))\
              .then_inc(ld_b, 16)
            sp.dma_start(tri[:, :, :].rearrange("p a b -> p (a b)"), A["tri"].rearrange("(a n) -> a n", a=1)
                         .broadcast_to([P, NG0 * NG0])).then_inc(ld_b, 16)
            up_v = A["L0_ffn_up_w"].rearrange("e d f -> d e f")
            down_v = A["L0_ffn_down_w"].rearrange("(n two) f d -> (two f) n d", two=2)

            def load0(slot, n):
                sp.dma_start(wslot[:, slot, 0:GP * P].rearrange("p (e f) -> p e f", f=I0),
                             up_v[:, bass.ds(2 * GP * n, 2 * GP), :]).then_inc(ld_w0[slot], 16)
                sp.dma_start(wslot[:, slot, GP * P:2 * GP * P].rearrange("p (n d) -> p n d", d=D),
                             down_v[:, bass.ds(GP * n, GP), :]).then_inc(ld_w0[slot], 16)

            for slot in range(2):
                load0(slot, slot)
            for dst, name in ((wqa[:, :], "L1_attn_Wqa"), (wkva[:, :], "L1_attn_Wkva"),
                              (wqb[:, 0, :], "L1_attn_Wqb"), (wkvb[:, :], "L1_attn_Wkvb"),
                              (wo1[:, :], "L1_attn_Wout"), (wr1[:, 0:E1], "L1_ffn_w_router"),
                              (wr1[:, E1:2 * E1], "L1_ffn_w_gating"), (identb[:, :], "identb"),
                              (maskqk[:, :], "maskqk"), (maskkq[:, :], "maskkq")):
                sp.dma_start(dst, A[name]).then_inc(ld_c, 16)
            sp.dma_start(bo1[:, :], A["L1_attn_bout"].rearrange("(a n) -> a n", a=1).broadcast_to([P, D]))\
              .then_inc(ld_c, 16)
            sp.wait_ge(x1_ready, NC)
            sp.dma_start(wsh[:, 0, :], A["L0_ffn_shared_up_w"]).then_inc(ld_sel, 16)
            sp.dma_start(wsh[:, 1, :].rearrange("p (n d) -> p n d", d=D),
                         A["L0_ffn_shared_down_w"].rearrange("(n p) d -> p n d", p=P)).then_inc(ld_sel, 16)
            sp.dma_start(sel, A["sel"].rearrange("p (n f) -> p n f", f=P)).then_inc(ld_sel, 16)
            with sp.Fori(1, N_IT0) as it:
                for slot in range(2):
                    sp.wait_ge(moe_down, it * MU + (slot * GP * NC - GP * NC))
                    load0(slot, it * 2 + slot)

            w1_views = [A["L1_ffn_w_gate"], A["L1_ffn_w_up"],
                        A["L1_ffn_w_down"].rearrange("e (n p) d -> e p n d", p=P)]

            def load1(slot, e):
                for which in range(2):
                    sp.dma_start(wslot[:, slot, which * F1:(which + 1) * F1],
                                 w1_views[which][bass.ds(e, 1), :, :].rearrange("a p n -> (a p) n"))\
                      .then_inc(ld_w1[slot], 16)
                sp.dma_start(wslot[:, slot, 2 * F1:3 * F1].rearrange("p (n d) -> p n d", d=D),
                             w1_views[2][bass.ds(e, 1), :, :, :].rearrange("a p n d -> (a p) n d"))\
                  .then_inc(ld_w1[slot], 16)

            sp.wait_ge(x2_ready, NC)
            sp.dma_start(ropec, A["ropec"]).then_inc(ld_rope, 16)
            sp.dma_start(ropes, A["ropes"]).then_inc(ld_rope, 16)
            for slot in range(2):
                load1(slot, slot)
            for c in range(NC):
                sp.wait_ge(split_ready, 2 * c + 2)
                sp.dma_start(qs_dram[:, :, chunk(c)].rearrange("s p t -> p s t"), q3[:, c % 2])\
                  .then_inc(st_qk[c % 2], 16)
                sp.dma_start(ks_dram[:, :, chunk(c)].rearrange("s p t -> p s t"),
                             k3[0:G1 * HD, c % 2]).then_inc(st_qk[c % 2], 16)
            for b in range(2):
                sp.wait_ge(st_qk[b], 16 * NC)
            sp.wait_ge(kones, 1)

            def rows(a, b):
                return slice((a * NSPLIT + b) * HD, (a * NSPLIT + b + 1) * HD)

            for a in range(NSPLIT):
                for b in range(NSPLIT):
                    sp.dma_start(kst[rows(a, b), :, :],
                                 ks_dram[b].rearrange("(g d) t -> d g t", d=HD)).then_inc(ld_kst, 16)
            for g in range(G1):
                for a in range(NSPLIT):
                    for b in range(NSPLIT):
                        sp.dma_start(qst[rows(a, b), HPG * g:HPG * g + HPG, :],
                                     qs_dram[a, HPG * HD * g:HPG * HD * (g + 1), :]
                                     .rearrange("(h d) t -> d h t", d=HD)).then_inc(ld_qst[g], 16)
            for g in range(G1):
                sp.wait_ge(nm_row, g + 1)
                for s in range(2):
                    sp.dma_start(qst[KROWS + s:KROWS + s + 1, HPG * g:HPG * g + HPG, :]
                                 .rearrange("p h t -> p (h t)"),
                                 nrow[s * HPG * NT:(s + 1) * HPG * NT, :]).then_inc(ld_nm[g], 16)
            with sp.Fori(1, N_IT1) as it:
                for slot in range(2):
                    sp.wait_ge(ffn_down, it * MU + (slot * FT * NC - FT * NC))
                    load1(slot, it * 2 + slot)
            out_v = out.rearrange("a (n p) d -> p (a n) d", p=P)
            for c in range(NC):
                sp.wait_ge(out_ready, c + 1)
                sp.dma_start(out_v[:, TPC * c:TPC * c + TPC, :], obuf[:, TPC * c:TPC * c + TPC, :])\
                  .then_inc(st_out, 16)
            sp.wait_ge(st_out, 16 * NC)

        @block.gpsimd
        def _(pool):
            nc.gpsimd.memset(hT[:, 0:PAD], 0.0).then_inc(pad_zero, 1)
            pool.wait_ge(x2_ready, NC)
            nc.gpsimd.memset(kst[64:96, :, :], 1.0).then_inc(kones, 1)
            pool.wait_ge(kones, 1)
            nc.gpsimd.memset(vaug, 0.0).then_inc(vzero, 1)
            pool.wait_ge(vzero, 1)
            nc.gpsimd.memset(vaug[:, :, :, HD:HD + 1], 1.0).then_inc(vzero, 1)
            pool.wait_ge(vzero, 2)
            nc.gpsimd.memset(mx, -BIG).then_inc(mxinit, 1)

        @block.tensor
        def _(pe):
            mm = nc.tensor.matmul

            def norm(i):
                for c in range(NC):
                    pe.wait_ge(ln_xn[i], c + 1)
                    if c == 0 and i == 0:
                        pe.wait_ge(ld_const, 32)
                    if c >= 2:
                        pe.wait_ge(ln_h[i], c - 1)
                    for k, t in enumerate(tiles(c)):
                        last = nc.tensor.transpose(ps[:, c % 2, k * P:(k + 1) * P], xn[:, t, :], ident[:, :])
                    last.then_inc(ln_tr[i], 1)

            pe.wait_ge(ld_mod, 64)
            pe.wait_ge(scb_ready, 2)
            for l in range(2):
                mm(ps[:, 2, l * P:(l + 1) * P], scb[:, l, :], wmod[:, l, 2 * D:3 * D], start=True, stop=True)
                for n, j in enumerate((0, 1, 3, 4, 5)):
                    last = mm(ps[:, 3, 8 * l + n:8 * l + n + 1], wmod[:, l, j * D:(j + 1) * D],
                              tc("sc0" if l == 0 else "sc1"), start=True, stop=True)
            last.then_inc(mod_mm, 1)

            norm(0)

            def project(bank, grp, c, done):
                for k in range(TAPS):
                    last = mm(ps[:, bank, :], wfold[:, k, grp, :], hT[:, c * CW + k:c * CW + k + CW],
                              start=(k == 0), stop=(k == TAPS - 1))
                last.then_inc(done, 1)

            pe.wait_ge(fold_ready, 3)
            pe.wait_ge(pad_zero, 1)
            pe.wait_ge(mod_ready, 1)
            for c in range(NC):
                pe.wait_ge(ln_h[0], c + 1)
                if c >= 2:
                    pe.wait_ge(zs_lin, c - 1)
                project(2 + c % 2, 2, c, zs_mm)

            def mix(c):
                pe.wait_ge(num_ready, 2 * M0 * (c + 1))
                if c == 0:
                    pe.wait_ge(bd_ready, 1)
                if c >= 2:
                    pe.wait_ge(yg_ready, c - 1)
                for n in range(2 * M0):
                    last = mm(ps[:, 6 + c % 2, :], bd[:, n // M0, n % M0].rearrange("p k j -> p (k j)"),
                              nums[:, c % 2, n, :], start=(n == 0), stop=(n == 2 * M0 - 1))
                last.then_inc(y_mm, 1)
                pe.wait_ge(sq_ready, c + 1)
                for n in range(2 * M0):
                    last = mm(ps[:, c % 2, :], blk[:, :], sqs[:, n, :], start=(n == 0), stop=(n == 2 * M0 - 1))
                last.then_inc(ss_mm, 1)

            def out0(c):
                pe.wait_ge(yg_ready, c + 1)
                if c == 0:
                    pe.wait_ge(wo_ready, 1)
                pe.wait_ge(zs_lin, NC)
                if c >= 2:
                    pe.wait_ge(x1_ready, c - 1)
                for k, t in enumerate(tiles(c)):
                    last = mm(ps[:, 2 + c % 2, k * P:(k + 1) * P], yg[:, t * P:(t + 1) * P], wo0[:, :],
                              start=True, stop=True)
                last.then_inc(o0_mm, 1)

            for c in range(NC):
                if c >= 1:
                    pe.wait_ge(xv_ready, c)
                project(4, 0, c, zv_mm)
                if c >= 1:
                    pe.wait_ge(gate_ready, c)
                project(5, 1, c, zg_mm)
                if c >= 1:
                    mix(c - 1)
                if c >= 2:
                    out0(c - 2)
            mix(NC - 1)
            out0(NC - 2)
            out0(NC - 1)

            norm(1)

            pe.wait_ge(ld_b, 64)
            nc.tensor.transpose(ps[:, 2, 0:E0], rwn[:, :], ident[0:E0, 0:E0]).then_inc(rw_tr, 1)
            pe.wait_ge(rw_ready, 1)
            for c in range(NC):
                pe.wait_ge(ln_h[1], c + 1)
                for t in tiles(c):
                    last = mm(ps[:, 2 + t // 8, (t % 8) * E0:(t % 8 + 1) * E0],
                              hT[:, PAD + t * P:PAD + (t + 1) * P], rwT[:, :], start=True, stop=True)
            last.then_inc(lg_mm, 1)

            def rhs(c):
                return hT[:, PAD + c * CW:PAD + (c + 1) * CW]

            pe.wait_ge(ld_sel, 48)

            def shared_up(n):
                if n >= 2:
                    pe.wait_ge(sh_hid, n - 1)
                mm(ps[:, n % 2, :], wsh[:, 0, (n // NC) * P:(n // NC + 1) * P], rhs(n % NC),
                   start=True, stop=True).then_inc(sh_up, 1)

            def shared_down(n):
                pe.wait_ge(sh_hid, n + 1)
                mm(ps[:, 4 + n % NC, :], wsh[:, 1, (n // NC) * P:(n // NC + 1) * P], hid[:, n % 2, :],
                   start=(n < NC), stop=False).then_inc(sh_down, 1)

            NSU = NSH * NC
            for n in range(NSU + 1):
                if n < NSU:
                    shared_up(n)
                if n >= 1:
                    shared_down(n - 1)

            pe.wait_ge(ld_c, 16 * 11)
            for c in range(NC):
                pe.wait_ge(comb_ready, 1)
                if c >= 1:
                    pe.wait_ge(comb_T, 2 * c)
                pc = ps[:, 2:4, :].bitcast(BF16)
                for k, t in enumerate(tiles(c)):
                    nc.tensor.transpose(pc[:, 0, k * P:(k + 1) * P],
                                        comb3[:, t, 0:2, :].rearrange("p s e -> p (s e)"), identb[:, :])
                    last = nc.tensor.transpose(pc[0:E0, 1, k * P:(k + 1) * P], comb3[:, t, 2, :], identb[:, :])
                last.then_inc(comb_tr, 1)
            pe.wait_ge(comb_T, 2 * NC)

            def look0(base, k, slot_of):
                pair, c = k // NC, k % NC
                slot = (pair // GP) % 2
                if k % (GP * NC) == 0:
                    pe.wait_ge(ld_w0[slot], slot_of(slot))
                mm(ps[:, k % 2, :], up0(slot, pair % GP), rhs(c), start=True, stop=True).then_inc(moe_up, 1)
                w = sel[:, bass.ds(base + pair, 1), :].rearrange("p a f -> p (a f)")
                mm(ps[:, 2 + k % 2, :], w, combT[:, chunk(c)], start=True, stop=False)
                wl = sel[0:E0, bass.ds(base + pair, 1), :].rearrange("p a f -> p (a f)")
                mm(ps[:, 2 + k % 2, :], wl, combL[0:E0, chunk(c)], start=False, stop=True).then_inc(moe_cb, 1)

            def sum0(n0, k, last_one):
                pair, c = k // NC, k % NC
                pe.wait_ge(moe_hid, n0 + (k + 1))
                mm(ps[:, 4 + c, :], down0((pair // GP) % 2, pair % GP), hid[:, k % 2, :],
                   start=False, stop=last_one).then_inc(moe_down, 1)

            for k in range(2):
                look0(0, k, lambda s: 32)
            with pe.Fori(0, N_IT0 - 1) as it:
                for k in range(MU):
                    sum0(it * MU, k, False)
                    if k + 2 < MU:
                        look0(it * (2 * GP), k + 2, lambda s: it * 32 + 32)
                    else:
                        look0(it * (2 * GP) + 2 * GP, k + 2 - MU, lambda s: it * 32 + 64)
            for k in range(MU):
                sum0((N_IT0 - 1) * MU, k, k >= MU - NC)
                if k + 2 < MU:
                    look0((N_IT0 - 1) * 2 * GP, k + 2, lambda s: N_IT0 * 32)

            for c in range(NC):
                pe.wait_ge(y0_ready, c + 1)
                if c >= 2:
                    pe.wait_ge(x2_ready, c - 1)
                for k in range(TPC):
                    last = nc.tensor.transpose(ps[:, 2 + c % 2, k * P:(k + 1) * P],
                                               yT[:, c * CW + k * P:c * CW + (k + 1) * P], ident[:, :])
                last.then_inc(y0_tr, 1)

            norm(2)

            pe.wait_ge(wk_ready, 1)
            for c in range(NC):
                pe.wait_ge(ln_h[2], c + 1)
                if c >= 1:
                    pe.wait_ge(v_ready, c)
                mm(ps[0:QL, 2, :], wqa[:, :], rhs(c), start=True, stop=True)
                mm(ps[0:KVL, 3, :], wkva[:, :], rhs(c), start=True, stop=True).then_inc(lat_mm, 1)
                pe.wait_ge(lat_ready, 2 * c + 2)
                if c >= 1:
                    pe.wait_ge(rope_done, 4 * c)
                mm(ps[:, 4, :], wqb[:, 0, :], latq[0:QL, c % 2, :], start=True, stop=True)
                mm(ps[:, 5, :], wqb[:, 1, :], latq[0:QL, c % 2, :], start=True, stop=True)
                mm(ps[0:32, 6, :], wkk[:, 0, :], latk[0:KVL, c % 2, :], start=True, stop=True)
                mm(ps[0:32, 7, :], wkk[:, 1, :], latk[0:KVL, c % 2, :], start=True, stop=True).then_inc(qk_mm, 1)
                for k in range(TPC):
                    last = mm(ps[:, 2, k * 32:(k + 1) * 32], latk[0:KVL, c % 2, k * P:(k + 1) * P], wkk[:, 2, :],
                              start=True, stop=True)
                last.then_inc(v_mm, 1)

            def p1_unit(g, n):
                t, u = UNITS[n]
                diag = u == t // TPC
                w = (t % TPC + 1) * P if diag else CW
                for i in range(HPG):
                    m = (g * NU + n) * HPG + i
                    if m >= 2:
                        pe.wait_ge(p1_max, m - 1)
                    b = m % 2
                    q = qst[0:KROWS, HPG * g + i, t * P:(t + 1) * P]
                    full = w - P if diag else w
                    if full:
                        last = mm(ps[:, b, 0:full], q, kst[0:KROWS, g, u * CW:u * CW + full], start=True, stop=True)
                    if diag:
                        mm(ps[:, b, full:w], q, kst[0:KROWS, g, u * CW + full:u * CW + w], start=True, stop=False)
                        last = mm(ps[:, b, full:w], identb[:, :], maskqk[:, :], start=False, stop=True)
                    last.then_inc(p1_mm, 1)

            def p2_scores(g, s, pair):
                c, j = STEPS[s]
                off = max(0, j - TPC * c) * P
                n = 2 * (g * NS + s) + pair
                if n >= 2:
                    pe.wait_ge(p2_exp, n - 1)
                for i in (2 * pair, 2 * pair + 1):
                    k = kst[0:KROWS + 2, g, j * P:(j + 1) * P]
                    q = qst[0:KROWS + 2, HPG * g + i, chunk(c)]
                    full = off
                    if j >= TPC * c:
                        full = off + P
                        mm(ps[:, 2 + i, off:full], k, q[:, off:full], start=True, stop=False)
                        last = mm(ps[:, 2 + i, off:full], identb[:, :], maskkq[:, :], start=False, stop=True)
                    if full < CW:
                        last = mm(ps[:, 2 + i, full:CW], k, q[:, full:CW], start=True, stop=True)
                last.then_inc(p2_mm, 1)

            def p2_values(g, s):
                c, j = STEPS[s]
                off = max(0, j - TPC * c) * P
                pe.wait_ge(p2_exp, 2 * (g * NS + s) + 2)
                nchunk = g * NC + c
                if j == 0 and nchunk >= 1:
                    pe.wait_ge(o_copy, nchunk)
                for i in range(HPG):
                    last = mm(ps[32 * i:32 * i + 32, 6, off:CW], vaug[:, j, g, :],
                              probs[:, s % 2, i, off:CW], start=(j == 0), stop=(j == TPC * c + TPC - 1),
                              tile_position=(0, 32 * i))
                last.then_inc(pv_mm, 1)

            def turn_maxima(g):
                pe.wait_ge(nm_ready, g + 1)
                if g >= 1:
                    pe.wait_ge(o_norm, (g - 1) * NC + 3)
                nc.tensor.transpose(ps[:, 7, 0:P // 2].bitcast(BF16), nm2.rearrange("p s n -> p (s n)"),
                                    identb[:, :]).then_inc(nm_tr, 1)

            def turn_out(g, c):
                pe.wait_ge(o_copy, g * NC + c + 1)
                if g * NC + c >= 1:
                    pe.wait_ge(o_norm, g * NC + c)
                pe.wait_ge(nm_row, min(g + 2, G1) if c == NC - 1 else g + 1)
                for k in range(TPC):
                    last = nc.tensor.transpose(ps[:, 7, k * P:(k + 1) * P], oT[:, k * P:(k + 1) * P], ident[:, :])
                last.then_inc(o_tr, 1)

            pe.wait_ge(v_ready, NC)
            pe.wait_ge(rope_done, 4 * NC)
            pe.wait_ge(ld_kst, 16 * NSPLIT * NSPLIT)
            pe.wait_ge(ld_qst[0], 16 * NSPLIT * NSPLIT)
            for n in range(NU):
                p1_unit(0, n)
            turn_maxima(0)
            for g in range(G1):
                if g + 1 < G1:
                    pe.wait_ge(ld_qst[g + 1], 16 * NSPLIT * NSPLIT)
                pe.wait_ge(ld_nm[g], 32)
                at_unit = 0
                for s in range(NS):
                    p2_scores(g, s, 0)
                    p2_scores(g, s, 1)
                    if g + 1 < G1 and at_unit < NU:
                        for n in range(at_unit, min(NU, at_unit + 1 + (s % 4 == 3))):
                            p1_unit(g + 1, n)
                            at_unit = n + 1
                        if at_unit == NU:
                            pending = s + 1
                    if s >= 1:
                        p2_values(g, s - 1)
                        c, j = STEPS[s - 1]
                        if s >= 2 and STEPS[s - 2][0] != c:
                            turn_out(g, c - 1)
                    if g + 1 < G1 and at_unit == NU and s == pending:
                        turn_maxima(g + 1)
                p2_values(g, NS - 1)
                turn_out(g, NC - 1)

            for c in range(NC):
                pe.wait_ge(o_norm, G1 * NC)
                if c >= 2:
                    pe.wait_ge(ot_ready, c - 1)
                for k, t in enumerate(tiles(c)):
                    last = nc.tensor.transpose(ps[:, 2 * (c % 2), k * P:(k + 1) * P], otok[:, t, :], ident[:, :])
                last.then_inc(ot_tr, 1)
                pe.wait_ge(ot_ready, c + 1)
                if c >= 2:
                    pe.wait_ge(x3_ready, c - 1)
                for k in range(TPC):
                    last = mm(ps[:, 2 * (c % 2) + 1, k * P:(k + 1) * P], oTT[:, c % 2, k * P:(k + 1) * P], wo1[:, :],
                              start=True, stop=True)
                last.then_inc(o1_mm, 1)

            pe.wait_ge(x3_ready, NC)
            norm(3)

            for c in range(NC):
                pe.wait_ge(ln_h[3], c + 1)
                for t in tiles(c):
                    last = mm(ps[:, 2, t * 2 * E1:(t + 1) * 2 * E1], hT[:, PAD + t * P:PAD + (t + 1) * P], wr1[:, :],
                              start=True, stop=True)
            last.then_inc(lg1_mm, 1)
            pe.wait_ge(cw_ready, 1)
            for e in range(E1):
                for c in range(NC):
                    n = e * NC + c
                    if n >= 4:
                        pe.wait_ge(hcw_ready, n - 3)
                    for k, t in enumerate(tiles(c)):
                        last = nc.tensor.matmul(ps[:, 4 + n % 4, k * P:(k + 1) * P],
                                                cw[:, t, e:e + 1].broadcast_to([P, P]), ident[:, :],
                                                is_transpose=True, start=True, stop=True)
                    last.then_inc(cw_tr, 1)

            def look1(e0, k, loaded):
                e, ft, c = k // (FT * NC), k // NC % FT, k % NC
                if k % (FT * NC) == 0:
                    pe.wait_ge(ld_w1[e], loaded)
                mm(ps[:, k % 2, :], w1(e, 0, ft), rhs(c), start=True, stop=True).then_inc(ffn_g, 1)
                hw = hcw[:, bass.ds(e0 + e, 1), chunk(c)].rearrange("p a t -> p (a t)")
                mm(ps[:, 2 + k % 2, :], w1(e, 1, ft), hw, start=True, stop=True).then_inc(ffn_u, 1)

            def sum1(n0, k, first, last_one):
                e, ft, c = k // (FT * NC), k // NC % FT, k % NC
                pe.wait_ge(ffn_hid, n0 + (k + 1))
                mm(ps[:, 4 + c, :], w1(e, 2, ft), hid1[:, k % 2, :], start=first, stop=last_one)\
                    .then_inc(ffn_down, 1)

            pe.wait_ge(hcw_ready, E1 * NC)
            for k in range(2):
                look1(0, k, 48)
            for k in range(MU):
                sum1(0, k, k < NC, False)
                if k + 2 < MU:
                    look1(0, k + 2, 48)
                else:
                    look1(2, k + 2 - MU, 96)
            with pe.Fori(1, N_IT1 - 1) as it:
                for k in range(MU):
                    sum1(it * MU, k, False, False)
                    if k + 2 < MU:
                        look1(it * 2, k + 2, it * 48 + 48)
                    else:
                        look1(it * 2 + 2, k + 2 - MU, it * 48 + 96)
            for k in range(MU):
                sum1((N_IT1 - 1) * MU, k, False, k >= MU - NC)
                if k + 2 < MU:
                    look1((N_IT1 - 1) * 2, k + 2, 48 * N_IT1)
            for c in range(NC):
                pe.wait_ge(y1_ready, c + 1)
                if c >= 2:
                    pe.wait_ge(out_ready, c - 1)
                for k in range(TPC):
                    last = nc.tensor.transpose(ps[:, 2 + c % 2, k * P:(k + 1) * P],
                                               y1T[:, c * CW + k * P:c * CW + (k + 1) * P], ident[:, :])
                last.then_inc(y1_tr, 1)

        @block.scalar
        def _(act):
            a = nc.scalar.activation
            own = [0]

            def step(ins):
                own[0] += 1
                ins.then_inc(s_a, 1)

            def settle():
                act.wait_ge(s_a, own[0])

            def norm(i):
                act.wait_ge(ln_var[i], 1)
                a(sd[:, :], mv[:, :, 1], ACT.Sqrt).then_inc(ln_sd[i], 1)
                l, j = i // 2, 2 * (i % 2)
                if i == 0:
                    act.wait_ge(mod_ready, 1)
                for c in range(NC):
                    act.wait_ge(ln_tr[i], c + 1)
                    a(hT[:, PAD + c * CW:PAD + (c + 1) * CW], ps[:, c % 2, :], ACT.Identity,
                      bias=modc[:, l, j:j + 1], scale=modc[:, l, j + 1:j + 2]).then_inc(ln_h[i], 1)

            act.wait_ge(ld_mod, 64)
            a(tiny[:, 2:4], tiny[:, 0:2], ACT.Silu).then_inc(silu_c, 1)
            n_small = 16 * 12
            act.wait_ge(ld_small, n_small)
            step(a(tc("nabs"), tc("slope"), ACT.Abs))
            settle()
            a(tc("esl"), tc("nabs"), ACT.Exp, scale=-1.0).then_inc(slope_e, 1)
            act.wait_ge(slope_u, 1)
            a(tc("lsl"), tc("usl"), ACT.Ln).then_inc(slope_l, 1)
            act.wait_ge(dl_max, 1)
            a(dexp, dlog, ACT.Exp, bias=dmax, scale=1.0, accum_out=dsum).then_inc(dl_exp, 1)
            act.wait_ge(slope_ready, 1)
            act.wait_ge(ld_a, 48)
            a(tw, tw, ACT.Exp, scale=tc("nsd")).then_inc(tw_ready, 1)
            norm(0)

            for c in range(NC):
                act.wait_ge(zs_lin, c + 1)
                a(pw[:, chunk(c)], pw[:, chunk(c)], ACT.Exp).then_inc(zs_exp, 1)

            def values(c):
                act.wait_ge(zv_mm, c + 1)
                if c >= 2:
                    act.wait_ge(phi_ready, c - 1)
                a(xv[:, c % 2, :], ps[:, 4, :], ACT.Identity, bias=tc("bval")).then_inc(xv_ready, 1)
                act.wait_ge(zg_mm, c + 1)
                a(gate[:, chunk(c)], ps[:, 5, :], ACT.Silu, bias=tc("bgate")).then_inc(gate_ready, 1)

            def trig(c):
                act.wait_ge(phi_ready, c + 1)
                step(a(ang[:, c % 2], phi[:, c % 2], ACT.Abs))
                settle()
                step(a(ang[:, c % 2], ang[:, c % 2], ACT.Sin, bias=nsc, scale=-1.0))
                step(a(phi[:, c % 2], phi[:, c % 2], ACT.Sin))
                settle()
                nc.scalar.activation(nsc_copy, nsc, ACT.Copy).then_inc(trig_ready, 1)

            def squares(c):
                act.wait_ge(num_ready, 2 * M0 * (c + 1))
                if c >= 1:
                    act.wait_ge(ss_mm, c)
                a(sqs, nums[:, c % 2], ACT.Square).then_inc(sq_ready, 1)

            def root(c):
                act.wait_ge(q_ready, c + 1)
                a(ssq, ssq, ACT.Sqrt).then_inc(rt_ready, 1)

            nsc_copy = tiny[:, 44:45]
            values(0)
            trig(0)
            for c in range(NC):
                if c + 1 < NC:
                    values(c + 1)
                    trig(c + 1)
                squares(c)
                if c >= 1:
                    root(c - 1)
            root(NC - 1)

            norm(1)
            act.wait_ge(rw_tr, 1)
            a(rwT[:, :], ps[:, 2, 0:E0], ACT.Copy).then_inc(rw_ready, 1)
            act.wait_ge(lg_mm, 1)
            a(scores.rearrange("p (b n) e -> p b (n e)", b=2), ps[:, 2:4, :], ACT.Sigmoid).then_inc(sig_ready, 1)
            for n in range(NSH * NC):
                act.wait_ge(sh_up, n + 1)
                if n >= 2:
                    act.wait_ge(sh_down, n - 1)
                step(a(relu[:, n % 2, :], ps[:, n % 2, :], ACT.Relu))
                settle()
                a(hid[:, n % 2, :], relu[:, n % 2, :], ACT.Square).then_inc(sh_hid, 1)
            for c in range(NC):
                act.wait_ge(comb_tr, c + 1)
                a(combT[:, chunk(c)], ps[:, 2, 0:CW // 2].bitcast(BF16), ACT.Copy).then_inc(comb_T, 1)
                a(combL[0:E0, chunk(c)], ps[0:E0, 3, 0:CW // 2].bitcast(BF16), ACT.Copy).then_inc(comb_T, 1)

            def relu_unit(n0, k):
                act.wait_ge(moe_up, n0 + (k + 1))
                a(relu[:, k % 2, :], ps[:, k % 2, :], ACT.Relu).then_inc(moe_relu, 1)

            with act.Fori(0, N_IT0) as it:
                for k in range(MU):
                    relu_unit(it * MU, k)
            for c in range(NC):
                if c == 0:
                    act.wait_ge(moe_down, N_IT0 * MU)
                a(yT[:, chunk(c)], ps[:, 4 + c, :], ACT.Copy, scale=modc[:, 0, 4:5]).then_inc(y0_ready, 1)

            norm(2)
            for c in range(NC):
                act.wait_ge(lat_mm, c + 1)
                a(latq[0:QL, c % 2, :], ps[0:QL, 2, :], ACT.Copy).then_inc(lat_ready, 1)
                a(latk[0:KVL, c % 2, :], ps[0:KVL, 3, :], ACT.Copy).then_inc(lat_ready, 1)
                act.wait_ge(v_mm, c + 1)
                act.wait_ge(vzero, 2)
                a(vaug[:, TPC * c:TPC * c + TPC, :, 0:HD],
                  ps[:, 2, 0:TPC * 32].rearrange("p (n g d) -> p n g d", g=G1, d=HD), ACT.Copy)\
                    .then_inc(v_ready, 1)

            scale = float(HD) ** -0.5
            for g in range(G1):
                for s in range(NS):
                    c, j = STEPS[s]
                    off = max(0, j - TPC * c) * P
                    for pair in range(2):
                        n = g * NS + s
                        act.wait_ge(p2_mm, 2 * n + pair + 1)
                        if n >= 2:
                            act.wait_ge(pv_mm, n - 1)
                        a(probs[:, s % 2, 2 * pair:2 * pair + 2, off:CW],
                          ps[:, 2 + 2 * pair:4 + 2 * pair, off:CW], ACT.Exp, scale=scale).then_inc(p2_exp, 1)
            for c in range(NC):
                act.wait_ge(ot_tr, c + 1)
                if c >= 2:
                    act.wait_ge(o1_mm, c - 1)
                a(oTT[:, c % 2, :], ps[:, 2 * (c % 2), :], ACT.Copy).then_inc(ot_ready, 1)

            norm(3)
            act.wait_ge(lg1_max, 1)
            a(ex, lg, ACT.Exp).then_inc(lg1_exp, 1)

            def silu_unit(n0, k):
                act.wait_ge(ffn_g, n0 + (k + 1))
                a(silg[:, k % 2, :], ps[:, k % 2, :], ACT.Silu).then_inc(ffn_silu, 1)

            with act.Fori(0, N_IT1) as it:
                for k in range(MU):
                    silu_unit(it * MU, k)
            for c in range(NC):
                if c == 0:
                    act.wait_ge(ffn_down, N_IT1 * MU)
                a(y1T[:, chunk(c)], ps[:, 4 + c, :], ACT.Copy, scale=modc[:, 1, 4:5]).then_inc(y1_ready, 1)

        @block.vector
        def _(dve):
            v = nc.vector
            own = [0]

            def step(ins):
                own[0] += 1
                ins.then_inc(s_v, 1)

            def settle():
                dve.wait_ge(s_v, own[0])

            def chain(ins):
                step(ins)
                settle()

            def norm(i, ready):
                for t in range(NT):
                    if t % TPC == 0:
                        ready(t // TPC)
                    step(v.bn_stats(stats[:, t, :], xt[:, t, :]))
                settle()
                for t in range(NT):
                    step(v.bn_aggr(mv[:, t, :], stats[:, t, :]))
                settle()
                v.tensor_scalar(mv[:, :, 1], mv[:, :, 1], EPS, None, ALU.add).then_inc(ln_var[i], 1)
                dve.wait_ge(ln_sd[i], 1)
                chain(v.reciprocal(rstd[:, :], sd[:, :]))
                for c in range(NC):
                    for t in tiles(c):
                        last = v.tensor_scalar(xn[:, t, :], xt[:, t, :], mv[:, t, 0:1], rstd[:, t:t + 1],
                                               ALU.subtract, ALU.mult)
                    last.then_inc(ln_xn[i], 1)

            dve.wait_ge(silu_c, 1)
            for l in range(2):
                v.tensor_copy(scb[:, l, :], tiny[:, 2 + l:3 + l].broadcast_to([P, P])).then_inc(scb_ready, 1)
            dve.wait_ge(mod_mm, 1)
            for l in range(2):
                m = ps[:, 3, 8 * l:8 * l + 5]
                step(v.tensor_copy(modc[:, l, 0:5], m))
                step(v.tensor_scalar(gcol[:, 0:1], m[:, 4:5], 0.0, 2.0, ALU.is_ge, ALU.mult))
                step(v.tensor_scalar(gcol[:, 1:2], m[:, 4:5], -1.0, 0.25, ALU.mult, ALU.max))
                r = ps[:, 2, l * P:(l + 1) * P]
                step(v.tensor_scalar(gar[:, l, :], r, 0.0, 2.0, ALU.is_ge, ALU.mult))
                step(v.tensor_scalar(scb[:, l, :], r, -1.0, 0.25, ALU.mult, ALU.max))
                settle()
                step(v.tensor_tensor(gcol[:, 1:2], m[:, 4:5], gcol[:, 1:2], ALU.max))
                step(v.tensor_tensor(scb[:, l, :], r, scb[:, l, :], ALU.max))
                settle()
                step(v.tensor_scalar(modc[:, l, 1:2], modc[:, l, 1:2], 1.0, None, ALU.add))
                step(v.tensor_scalar(modc[:, l, 3:4], modc[:, l, 3:4], 1.0, None, ALU.add))
                step(v.scalar_tensor_tensor(modc[:, l, 4:5], gcol[:, 0:1], -1.0, gcol[:, 1:2], ALU.add, ALU.mult))
                chain(v.scalar_tensor_tensor(gar[:, l, :], gar[:, l, :], -1.0, scb[:, l, :], ALU.add, ALU.mult))
            v.tensor_copy(tiny[:, 45:46], tiny[:, 2:3]).then_inc(mod_ready, 1)

            def x_loaded(c):
                dve.wait_ge(ld_x[c], 16)

            n_small = 16 * 12
            dve.wait_ge(ld_small, n_small)
            dve.wait_ge(slope_e, 1)
            v.tensor_scalar(tc("usl"), tc("esl"), 1.0, None, ALU.add).then_inc(slope_u, 1)
            dve.wait_ge(slope_u, 1)
            chain(v.tensor_scalar(tc("dsl"), tc("usl"), -1.0, None, ALU.add))
            step(v.tensor_scalar(tc("zsl"), tc("dsl"), 0.0, tc("esl"), ALU.is_equal, ALU.mult))
            chain(v.tensor_scalar(tc("msl"), tc("dsl"), 1e-30, None, ALU.max))
            chain(v.reciprocal(tc("rsl"), tc("msl")))
            dve.wait_ge(slope_l, 1)
            chain(v.scalar_tensor_tensor(tc("sp"), tc("lsl"), tc("esl"), tc("rsl"), ALU.mult, ALU.mult))
            chain(v.tensor_tensor(tc("sp"), tc("sp"), tc("zsl"), ALU.add))
            chain(v.scalar_tensor_tensor(tc("sp"), tc("slope"), 0.0, tc("sp"), ALU.max, ALU.add))
            v.tensor_scalar(tc("nsd"), tc("sp"), -1.0, None, ALU.mult).then_inc(slope_ready, 1)
            v.tensor_reduce(dmax, dlog, AX_X, ALU.max, negate=True).then_inc(dl_max, 1)
            step(v.tensor_scalar(theta_n, theta_c, INV_2PI, None, ALU.mult))
            step(v.tensor_tensor(tc("ssb"), tc("bs"), tc("ss"), ALU.mult))
            step(v.memset(nsc, HALF_PI))
            dve.wait_ge(dl_exp, 1)
            chain(v.reciprocal(dsum, dsum))
            chain(v.tensor_scalar(dw, dexp, dsum, None, ALU.mult))
            chain(v.tensor_scalar(dw[:, 2:3], dw[:, 2:3], -1.0, None, ALU.mult))
            dve.wait_ge(ld_a, 48)
            for grp in range(2):
                cols = slice(grp * D, (grp + 1) * D)
                v.tensor_tensor(wfold[:, :, grp, :], wcv[:, :, cols],
                                win[:, cols].unsqueeze(1).broadcast_to([P, TAPS, D]), ALU.mult)\
                    .then_inc(fold_ready, 1)
            for k in range(TAPS):
                last = v.tensor_tensor(wfold[:, k, 2, :].rearrange("p (k h) -> p k h", h=H0),
                                       wcv[:, k, 2 * D:].unsqueeze(2).broadcast_to([P, K0, H0]),
                                       win[:, 2 * D:].unsqueeze(2).broadcast_to([P, K0, H0]), ALU.mult)
            last.then_inc(fold_ready, 1)
            norm(0, x_loaded)
            dve.wait_ge(ld_const, 32)
            chain(v.tensor_tensor(wrows, wrows, nscale[:, :, :].unsqueeze(3).broadcast_to([P, 2, M0, H0]), ALU.mult))
            for i in range(2):
                for m in range(M0):
                    last = v.tensor_tensor(bd[:, i, m], blk[:, :].rearrange("p (k j) -> p k j", j=H0),
                                           wrows[:, i, m].unsqueeze(1).broadcast_to([P, K0, H0]), ALU.mult)
            last.then_inc(bd_ready, 1)
            dve.wait_ge(ld_b, 64)
            v.tensor_tensor(wo0[:, :], wo0[:, :], gar[:, 0, :], ALU.mult).then_inc(wo_ready, 1)

            for c in range(NC):
                dve.wait_ge(zs_mm, c + 1)
                chain(v.tensor_scalar(pw[:, chunk(c)], ps[:, 2 + c % 2, :], tc("ss"), tc("ssb"), ALU.mult, ALU.add))
                v.tensor_scalar(pw[:, chunk(c)], pw[:, chunk(c)], 20.0, -20.0, ALU.min, ALU.max).then_inc(zs_lin, 1)
            dve.wait_ge(tw_ready, 1)
            for c in range(NC):
                dve.wait_ge(zs_exp, c + 1)
                v.tensor_tensor(pw[:, chunk(c)], pw[:, chunk(c)], tw[:, chunk(c)], ALU.mult).then_inc(pw_ready, 1)

            def front(c):
                b = c % 2
                dve.wait_ge(xv_ready, c + 1)
                x = xv[:, b, :]
                for m in range(M0):
                    step(v.tensor_scalar(phi[:, b, m, :], x, theta_c[:, m:m + 1], None, ALU.mult))
                    step(v.tensor_scalar(ang[:, b, m, :], x, theta_n[:, m:m + 1], ROUND, ALU.mult, ALU.add))
                step(v.tensor_scalar(tmp[:, 0, :], x, dw[:, 2:3], dw[:, 1:2], ALU.mult, ALU.add))
                settle()
                step(v.tensor_scalar(ang[:, b], ang[:, b], -ROUND, None, ALU.add))
                step(v.tensor_tensor(tmp[:, 0, :], tmp[:, 0, :], x, ALU.mult))
                settle()
                step(v.scalar_tensor_tensor(phi[:, b], ang[:, b], -TWO_PI_HI, phi[:, b], ALU.mult, ALU.add))
                if c == 0:
                    dve.wait_ge(pw_ready, NC)
                step(v.scalar_tensor_tensor(pw_poly[:, b, :], tmp[:, 0, :], dw[:, 0:1], pw[:, chunk(c)],
                                            ALU.add, ALU.mult))
                settle()
                chain(v.scalar_tensor_tensor(phi[:, b], ang[:, b], -TWO_PI_LO, phi[:, b], ALU.mult, ALU.add))
                v.tensor_scalar(phi[:, b], phi[:, b], PI, -PI, ALU.min, ALU.max).then_inc(phi_ready, 1)

            def back(c):
                b = c % 2
                dve.wait_ge(trig_ready, c + 1)
                w = pw_poly[:, b, :].unsqueeze(1).broadcast_to([P, M0, CW])
                step(v.tensor_tensor(ang[:, b], ang[:, b], w, ALU.mult))
                step(v.tensor_tensor(phi[:, b], phi[:, b], w, ALU.mult))
                prev = den[:, c * CW - 1:c * CW] if c else 0.0
                step(v.tensor_tensor_scan(den[:, chunk(c)], ones_b, pw[:, chunk(c)], prev, ALU.mult, ALU.add))
                settle()
                if c >= 2:
                    dve.wait_ge(y_mm, c - 1)
                for n in range(2 * M0):
                    src = (ang if n < M0 else phi)[:, b, n % M0, :]
                    prev = nums[:, 1 - b, n, CW - 1:CW] if c else 0.0
                    v.tensor_tensor_scan(nums[:, b, n, :], ones_b, src, prev, ALU.mult, ALU.add)\
                        .then_inc(num_ready, 1)

            def tail(c):
                chain(v.tensor_scalar(tmp[:, 1, :], den[:, chunk(c)], 1e-4, None, ALU.max))
                chain(v.scalar_tensor_tensor(tmp[:, 1, :], tmp[:, 1, :], EPS, tmp[:, 1, :], ALU.mult, ALU.mult))
                dve.wait_ge(ss_mm, c + 1)
                v.scalar_tensor_tensor(ssq, ps[:, c % 2, :], 1.0 / (2 * H0 * M0), tmp[:, 1, :], ALU.mult, ALU.add)\
                    .then_inc(q_ready, 1)
                dve.wait_ge(rt_ready, c + 1)
                chain(v.reciprocal(fac[:, 0, :], ssq))
                dve.wait_ge(gate_ready, c + 1)
                chain(v.tensor_tensor(fac[:, 1, :], fac[:, 0, :], gate[:, chunk(c)], ALU.mult))
                dve.wait_ge(y_mm, c + 1)
                v.tensor_tensor(yg[:, chunk(c)], ps[:, 6 + c % 2, :], fac[:, 1, :], ALU.mult).then_inc(yg_ready, 1)

            def residual(c, bank, mm_done, done):
                dve.wait_ge(mm_done, c + 1)
                v.tensor_tensor(xt[:, TPC * c:TPC * c + TPC, :].rearrange("p n d -> p (n d)"),
                                ps[:, bank, :],
                                xt[:, TPC * c:TPC * c + TPC, :].rearrange("p n d -> p (n d)"), ALU.add)\
                    .then_inc(done, 1)

            ones_b = ones_w[:, :].broadcast_to([P, CW])
            chain(v.memset(ones_w[:, :], 1.0))
            front(0)
            for c in range(NC):
                if c + 1 < NC:
                    front(c + 1)
                back(c)
                if c >= 1:
                    tail(c - 1)
                if c >= 2:
                    residual(c - 2, 2 + c % 2, o0_mm, x1_ready)
            tail(NC - 1)
            residual(NC - 2, 2 + NC % 2, o0_mm, x1_ready)
            residual(NC - 1, 2 + (NC - 1) % 2, o0_mm, x1_ready)

            norm(1, lambda c: dve.wait_ge(x1_ready, c + 1))
            dve.wait_ge(sig_ready, 1)
            chain(v.tensor_tensor(sfc, scores, cbias[:, :].unsqueeze(1).broadcast_to([P, NT, E0]), ALU.add))
            NGT = NT * NG0
            grp = sfc.rearrange("p n (g e) -> p (n g) e", e=GE0)
            b1g = b1.rearrange("p n (g e) -> p (n g) e", e=GE0)
            b2g = b2.rearrange("p n (g e) -> p (n g) e", e=GE0)
            m1, cnt, m2, dup, gs, rank, gm = (gsm[:, i, :] for i in range(7))

            def per_group(x):
                return x.unsqueeze(2).broadcast_to([P, NGT, GE0])

            chain(v.tensor_reduce(m1, grp, AX_X, ALU.max))
            chain(v.tensor_tensor(b1g, grp, per_group(m1), ALU.is_equal))
            step(v.tensor_reduce(cnt, b1g, AX_X, ALU.add))
            chain(v.scalar_tensor_tensor(b2g, b1g, -BIG, grp, ALU.mult, ALU.add))
            step(v.tensor_reduce(m2, b2g, AX_X, ALU.max))
            chain(v.tensor_scalar(dup, cnt, 1.5, 1.0, ALU.is_ge, ALU.subtract))
            chain(v.scalar_tensor_tensor(dup, dup, BIG, m1, ALU.mult, ALU.add))
            chain(v.tensor_tensor(m2, m2, dup, ALU.max))
            chain(v.tensor_tensor(gs, m1, m2, ALU.add))
            gs_v = gs.rearrange("p (n g) -> p n g", g=NG0)
            mine = gs_v.unsqueeze(3).broadcast_to([P, NT, NG0, NG0])
            other = gs_v.unsqueeze(2).broadcast_to([P, NT, NG0, NG0])
            b1q = b1.rearrange("p n (g e) -> p n g e", e=NG0)
            b2q = b2.rearrange("p n (g e) -> p n g e", e=NG0)
            step(v.tensor_tensor(b1q, other, mine, ALU.is_gt))
            chain(v.tensor_tensor(b2q, other, mine, ALU.is_equal))
            chain(v.tensor_tensor(b2, b2, tri[:, :, :].rearrange("p a b -> p (a b)").unsqueeze(1)
                                  .broadcast_to([P, NT, E0]), ALU.mult))
            chain(v.tensor_tensor(b1, b1, b2, ALU.add))
            chain(v.tensor_reduce(rank, b1g, AX_X, ALU.add))
            chain(v.tensor_scalar(gm, rank, TOPG - 0.5, None, ALU.is_lt))
            chain(v.tensor_tensor(msk.rearrange("p n (g e) -> p (n g) e", e=GE0), grp, per_group(gm), ALU.mult))
            for t in range(NT):
                step(v.max(top8[:, t, :], msk[:, t, :]))
            settle()
            for t in range(NT):
                step(v.match_replace(b1[:, t, :], top8[:, t, :], msk[:, t, :], -BIG))
            settle()
            chain(v.scalar_tensor_tensor(b2, b1, -BIG / 2, scores, ALU.is_lt, ALU.mult))
            chain(v.tensor_reduce(wsum[:, 0, :], b2, AX_X, ALU.add))
            chain(v.tensor_scalar(wsum[:, 1, :], wsum[:, 0, :], 1e-20, None, ALU.add))
            chain(v.reciprocal(wsum[:, 2, :], wsum[:, 1, :]))
            chain(v.scalar_tensor_tensor(b1, b2, 2.5, wsum[:, 2, :].unsqueeze(2).broadcast_to([P, NT, E0]),
                                         ALU.mult, ALU.mult))
            chain(v.tensor_copy(comb3[:, :, 0, :], b1))
            chain(v.tensor_tensor(b2, b1, comb3[:, :, 0, :], ALU.subtract))
            chain(v.tensor_copy(comb3[:, :, 1, :], b2))
            v.tensor_tensor(comb3[:, :, 2, :], b2, comb3[:, :, 1, :], ALU.subtract).then_inc(comb_ready, 1)

            def square_unit(n0, k):
                dve.wait_ge(moe_relu, n0 + (k + 1))
                v.tensor_tensor(gsq[:, k % 2, :], ps[:, k % 2, :], relu[:, k % 2, :], ALU.mult).then_inc(moe_g, 1)
                dve.wait_ge(moe_cb, n0 + (k + 1))
                dve.wait_ge(moe_g, n0 + (k + 1))
                v.tensor_tensor(hid[:, k % 2, :], ps[:, 2 + k % 2, :], gsq[:, k % 2, :], ALU.mult)\
                    .then_inc(moe_hid, 1)

            with dve.Fori(0, N_IT0) as it:
                for k in range(MU):
                    square_unit(it * MU, k)
            for c in range(NC):
                residual(c, 2 + c % 2, y0_tr, x2_ready)

            norm(2, lambda c: dve.wait_ge(x2_ready, c + 1))
            dve.wait_ge(ld_c, 16 * 11)
            swap = wqb[:, 1, :].rearrange("p (n two) -> p n two", two=2)
            plain = wqb[:, 0, :].rearrange("p (n two) -> p n two", two=2)
            kv = wkvb[:, :].rearrange("p (n two kv) -> p n two kv", two=2, kv=2)
            wk0 = wkk[:, 0, :].rearrange("p (n two) -> p n two", two=2)
            wk1 = wkk[:, 1, :].rearrange("p (n two) -> p n two", two=2)
            wv = wkk[:, 2, :].rearrange("p (n two) -> p n two", two=2)
            v.tensor_copy(swap[:, :, 0], plain[:, :, 1])
            v.tensor_copy(swap[:, :, 1], plain[:, :, 0])
            v.tensor_copy(wk0, kv[:, :, :, 0])
            v.tensor_copy(wk1[:, :, 0], kv[:, :, 1, 0])
            v.tensor_copy(wk1[:, :, 1], kv[:, :, 0, 0])
            v.tensor_copy(wv, kv[:, :, :, 1]).then_inc(wk_ready, 1)
            step(v.tensor_tensor(wo1[:, :], wo1[:, :], gar[:, 1, :], ALU.mult))
            chain(v.tensor_tensor(bo1[:, :], bo1[:, :], gar[:, 1, :], ALU.mult))
            dve.wait_ge(ld_rope, 32)
            for c in range(NC):
                dve.wait_ge(qk_mm, c + 1)
                b = c % 2
                cs, sn = ropec[:, chunk(c)], ropes[:, chunk(c)]
                KR = G1 * HD
                v.tensor_tensor(ra[:, b, :], ps[:, 4, :], cs, ALU.mult).then_inc(rope_done, 1)
                v.tensor_tensor(rb[:, b, :], ps[:, 5, :], sn, ALU.mult).then_inc(rope_done, 1)
                v.tensor_tensor(rk[0:KR, b, :], ps[0:KR, 6, :], cs[0:KR, :], ALU.mult).then_inc(rope_done, 1)
                v.tensor_tensor(rl[0:KR, b, :], ps[0:KR, 7, :], sn[0:KR, :], ALU.mult).then_inc(rope_done, 1)
                dve.wait_ge(rope_done, 4 * c + 4)
                step(v.tensor_tensor(ra[:, b, :], ra[:, b, :], rb[:, b, :], ALU.add))
                step(v.tensor_tensor(rk[0:KR, b, :], rk[0:KR, b, :], rl[0:KR, b, :], ALU.add))
                settle()
                if c >= 2:
                    dve.wait_ge(st_qk[b], 32 * (c // 2))
                step(v.tensor_copy(q3[:, b, 0, :], ra[:, b, :]))
                step(v.tensor_copy(k3[0:KR, b, 0, :], rk[0:KR, b, :]))
                settle()
                step(v.tensor_tensor(ra[:, b, :], ra[:, b, :], q3[:, b, 0, :], ALU.subtract))
                step(v.tensor_tensor(rk[0:KR, b, :], rk[0:KR, b, :], k3[0:KR, b, 0, :], ALU.subtract))
                settle()
                step(v.tensor_copy(q3[:, b, 1, :], ra[:, b, :]))
                step(v.tensor_copy(k3[0:KR, b, 1, :], rk[0:KR, b, :]))
                settle()
                v.tensor_tensor(q3[:, b, 2, :], ra[:, b, :], q3[:, b, 1, :], ALU.subtract).then_inc(split_ready, 1)
                v.tensor_tensor(k3[0:KR, b, 2, :], rk[0:KR, b, :], k3[0:KR, b, 1, :], ALU.subtract)\
                    .then_inc(split_ready, 1)
            chain(v.tensor_tensor(xt[:, :, :], xt[:, :, :], bo1[:, :].unsqueeze(1).broadcast_to([P, NT, D]), ALU.add))

            def p1_unit(g, n):
                t, u = UNITS[n]
                w = (t % TPC + 1) * P if u == t // TPC else CW
                for i in range(HPG):
                    m = (g * NU + n) * HPG + i
                    dve.wait_ge(p1_mm, m + 1)
                    v.tensor_reduce(mx[:, i, t, u:u + 1], ps[:, m % 2, 0:w], AX_X, ALU.max).then_inc(p1_max, 1)

            def maxima(g):
                dve.wait_ge(p1_max, (g + 1) * NU * HPG)
                chain(v.tensor_reduce(nmx, mx.rearrange("p h n u -> p (h n) u"), AX_X, ALU.max, negate=True))
                if g >= 1:
                    dve.wait_ge(nm_tr, g)
                chain(v.tensor_copy(nm2[:, 0, :], nmx))
                chain(v.tensor_tensor(nres, nmx, nm2[:, 0, :], ALU.subtract))
                v.tensor_copy(nm2[:, 1, :], nres).then_inc(nm_ready, 1)

            def maxima_rows(g):
                dve.wait_ge(nm_tr, g + 1)
                if g >= 1:
                    dve.wait_ge(ld_nm[g - 1], 32)
                v.tensor_copy(nrow, ps[:, 7, 0:P // 2].bitcast(BF16)).then_inc(nm_row, 1)

            def copy_out(g, c):
                n = 0
                for cc in range(c + 1):
                    n += TPC * cc + TPC
                dve.wait_ge(pv_mm, g * NS + n)
                if g * NC + c >= 1:
                    dve.wait_ge(o_tr, g * NC + c)
                v.tensor_copy(oT, ps[:, 6, :]).then_inc(o_copy, 1)

            def divide_out(g, c):
                dve.wait_ge(o_tr, g * NC + c + 1)
                o = ps[:, 7, :].rearrange("p (n h w) -> p n h w", h=HPG, w=32)
                chain(v.reciprocal(rden, o[:, :, :, HD]))
                for k in range(TPC):
                    last = v.tensor_tensor(otok[:, TPC * c + k, g * HPG * HD:(g + 1) * HPG * HD]
                                           .rearrange("p (h d) -> p h d", d=HD),
                                           o[:, k, :, 0:HD], rden[:, k, :].unsqueeze(2).broadcast_to([P, HPG, HD]),
                                           ALU.mult)
                last.then_inc(o_norm, 1)

            dve.wait_ge(mxinit, 1)
            for n in range(NU):
                p1_unit(0, n)
            maxima(0)
            maxima_rows(0)
            for g in range(G1):
                at_unit = 0
                for s in range(NS):
                    if g + 1 < G1 and at_unit < NU:
                        for n in range(at_unit, min(NU, at_unit + 1 + (s % 4 == 3))):
                            p1_unit(g + 1, n)
                            at_unit = n + 1
                        if at_unit == NU:
                            maxima(g + 1)
                            pending = s + 1
                    if s >= 1:
                        c, j = STEPS[s - 1]
                        if s >= 2 and STEPS[s - 2][0] != c:
                            copy_out(g, c - 1)
                            divide_out(g, c - 1)
                    if g + 1 < G1 and at_unit == NU and s == pending:
                        maxima_rows(g + 1)
                copy_out(g, NC - 1)
                divide_out(g, NC - 1)
            for c in range(NC):
                residual(c, 2 * (c % 2) + 1, o1_mm, x3_ready)

            norm(3, lambda c: dve.wait_ge(x3_ready, c + 1))
            dve.wait_ge(lg1_mm, 1)
            l4 = ps[:, 2, 0:NT * 2 * E1].rearrange("p (n e) -> p n e", e=E1)
            lgv = lg.rearrange("p n (a e) -> p (n a) e", a=2)
            chain(v.tensor_reduce(sm[:, 0, :], l4, AX_X, ALU.max))
            chain(v.tensor_tensor(lgv, l4, sm[:, 0, :].unsqueeze(2).broadcast_to([P, 2 * NT, E1]), ALU.subtract))
            v.tensor_scalar(lg[:, :, E1:2 * E1], lg[:, :, E1:2 * E1], 10.0, None, ALU.mult).then_inc(lg1_max, 1)
            dve.wait_ge(lg1_exp, 1)
            exv = ex.rearrange("p n (a e) -> p (n a) e", a=2)
            chain(v.tensor_reduce(sm[:, 1, :], exv, AX_X, ALU.add))
            chain(v.reciprocal(sm[:, 2, :], sm[:, 1, :]))
            chain(v.tensor_tensor(exv, exv, sm[:, 2, :].unsqueeze(2).broadcast_to([P, 2 * NT, E1]), ALU.mult))
            chain(v.tensor_tensor(cw, ex[:, :, 0:E1], ex[:, :, E1:2 * E1], ALU.mult))
            chain(v.tensor_reduce(sm[:, 3, 0:NT], cw, AX_X, ALU.add))
            chain(v.tensor_scalar(sm[:, 3, 0:NT], sm[:, 3, 0:NT], 1e-9, None, ALU.add))
            chain(v.reciprocal(sm[:, 4, 0:NT], sm[:, 3, 0:NT]))
            v.tensor_tensor(cw, cw, sm[:, 4, 0:NT].unsqueeze(2).broadcast_to([P, NT, E1]), ALU.mult)\
                .then_inc(cw_ready, 1)
            for e in range(E1):
                for c in range(NC):
                    n = e * NC + c
                    dve.wait_ge(cw_tr, n + 1)
                    v.tensor_tensor(hcw[:, e, chunk(c)], ps[:, 4 + n % 4, :],
                                    hT[:, PAD + c * CW:PAD + (c + 1) * CW], ALU.mult).then_inc(hcw_ready, 1)

            def gated_unit(n0, k):
                dve.wait_ge(ffn_silu, n0 + (k + 1))
                dve.wait_ge(ffn_u, n0 + (k + 1))
                v.tensor_tensor(hid1[:, k % 2, :], ps[:, 2 + k % 2, :], silg[:, k % 2, :], ALU.mult)\
                    .then_inc(ffn_hid, 1)

            with dve.Fori(0, N_IT1) as it:
                for k in range(MU):
                    gated_unit(it * MU, k)
            for c in range(NC):
                dve.wait_ge(y1_tr, c + 1)
                v.tensor_tensor(obuf[:, TPC * c:TPC * c + TPC, :].rearrange("p n d -> p (n d)"), ps[:, 2 + c % 2, :],
                                xt[:, TPC * c:TPC * c + TPC, :].rearrange("p n d -> p (n d)"), ALU.add)\
                    .then_inc(out_ready, 1)


_INS = ['L0_attn_x', 'L0_attn_W_in', 'L0_attn_w_conv', 'L0_attn_b_conv', 'L0_attn_theta', 'L0_attn_decay_slopes',
        'L0_attn_anchor_slopes', 'L0_attn_score_scale', 'L0_attn_deriv_logits', 'L0_attn_norm_scale', 'L0_attn_W_re',
        'L0_attn_W_im', 'L0_attn_W_out', 'L0_ffn_router_w', 'L0_ffn_correction_bias', 'L0_ffn_up_w',
        'L0_ffn_down_w', 'L0_ffn_shared_up_w', 'L0_ffn_shared_down_w', 'L0_c', 'L0_wmod', 'L1_attn_Wqa',
        'L1_attn_Wqb', 'L1_attn_Wkva', 'L1_attn_Wkvb', 'L1_attn_Wout', 'L1_attn_bout', 'L1_ffn_w_router',
        'L1_ffn_w_gating', 'L1_ffn_w_gate', 'L1_ffn_w_up', 'L1_ffn_w_down', 'L1_c', 'L1_wmod']


def _constants():
    import numpy as np

    f32 = np.float32

    def bf16_bits(x):
        return (x.astype(f32).view(np.uint32) >> 16).astype(np.uint16)

    ident = np.eye(P, dtype=f32)
    i = np.arange(P)
    later = (i[None, :] > i[:, None])
    pos = np.arange(T, dtype=f32)
    dist = np.broadcast_to(pos[None, :], (P, T)).copy()
    n_anchor = 4
    dist[0:(K0 - n_anchor) * H0] = (T - 1 - pos)[None, :]
    freq = (1.0 / np.float32(10000.0) ** (np.arange(0, HD, 2, dtype=f32) / f32(HD))).astype(f32)
    ang = (pos[:, None] * freq[None, :]).astype(f32).astype(np.float64)
    d = i % HD
    cos = np.cos(ang).astype(f32).T[d // 2]
    sin = np.sin(ang).astype(f32).T[d // 2] * np.where(d % 2 == 0, -1.0, 1.0).astype(f32)[:, None]
    sel = np.zeros((P, NPAIR, P), f32)
    for n in range(NPAIR):
        for j in range(2):
            for s in range(2):
                sel[s * E0 + 2 * n + j, n, j * I0:(j + 1) * I0] = 1.0
    tri = (np.arange(NG0)[None, :] < np.arange(NG0)[:, None]).astype(f32).ravel()
    return {
        "ident": ident, "identb": bf16_bits(ident),
        "maskqk": bf16_bits(np.where(later, -BIG, 0.0)), "maskkq": bf16_bits(np.where(later.T, -BIG, 0.0)),
        "blk": (i[:, None] // H0 == i[None, :] // H0).astype(f32), "dist": dist,
        "ropec": np.ascontiguousarray(cos, dtype=f32), "ropes": np.ascontiguousarray(sin, dtype=f32),
        "sel": bf16_bits(sel.reshape(P, NPAIR * P)), "tri": tri,
    }


def kernel(**inputs):
    import numpy as np
    import concourse.bacc as bacc
    from concourse.bass_utils import run_bass_kernel_spmd

    nc = bacc.Bacc("TRN2", target_bir_lowering=False, num_devices=1)
    arrays, aps = {}, {}
    every = {name: np.ascontiguousarray(inputs[name]) for name in _INS}
    every.update(_constants())
    for name, a in every.items():
        arrays[f"in_{name}"] = a
        aps[name] = nc.dram_tensor(f"in_{name}", a.shape, mybir.dt.from_np(a.dtype), kind="ExternalInput").ap()
        if a.dtype == np.uint16:
            aps[name] = aps[name].bitcast(BF16)
    out = nc.dram_tensor("out_0", (1, T, D), F32, kind="ExternalOutput").ap()
    adaln_two_layers(nc, aps, out)
    r = run_bass_kernel_spmd(nc, [arrays], core_ids=[0])
    return r.results[0]["out_0"]
```

```python
from contextlib import ExitStack

import concourse.bass as bass
from concourse import mybir

F32 = mybir.dt.float32
BF16 = mybir.dt.bfloat16
F32R = mybir.dt.float32r
ALU = mybir.AluOpType
ACT = mybir.ActivationFunctionType
AX_X = mybir.AxisListType.X

P = 128
T = 2048
D = 128
NT = T // P
CW = 512
NC = T // CW
TPC = CW // P
K0, H0, M0 = 32, 4, 4
TAPS = 4
E0, I0, ISH = 64, 64, 256
NG0, GE0, TOPG, TOPK = 8, 8, 4, 8
GP = 4
NPAIR = E0 // 2
NLOAD = NPAIR // GP
NSH = ISH // P
LOOK = 3
NBUF = LOOK + 1
H1, G1, HD = 16, 4, 8
QL, KVL = 64, 32
HPG = H1 // G1
NSPLIT = 3
KROWS = NSPLIT * NSPLIT * HD
NITEM = NC * G1
E1, F1 = 8, 512
FT = F1 // P

PI = 3.1415925
HALF_PI = 1.5707963267948966
INV_2PI = 0.15915494309189535
TWO_PI_HI = 6.28125
TWO_PI_LO = 0.0019353071795864769
ROUND = 12582912.0
BIG = 1.0e30
EPS = 1e-5


def attention_schedule():
    steps = [(n, j) for n in range(NITEM) for j in range(TPC * (n // G1 + 1))]
    first = {}
    for k, (n, _) in enumerate(steps):
        first.setdefault(n, k)
    scores = []
    for n in range(NITEM):
        c = n // G1
        for k, (t, u) in enumerate((t, u) for t in range(TPC * c, TPC * c + TPC) for u in range(c + 1)):
            scores += [("scores", n, t, u, i) for i in range(HPG)]
            if k == 0 and n > 0:
                scores.append(("maxima", n - 1))
    scores.append(("maxima", NITEM - 1))
    end = {n: max(k for k, x in enumerate(scores) if x[1] == n and x[0] == "scores") + 1 for n in range(NITEM)}
    slots = [scores[:end[1]]]
    done = end[1]
    late = {}
    for n in range(NITEM):
        s = first[n] + TPC * (n // G1 + 1)
        late.setdefault(s + 1, []).append(("out", n))
        if n % G1 == G1 - 1:
            late.setdefault(s + 2, []).append(("turned", n // G1))
            late.setdefault(s + 3, []).append(("product", n // G1))
    for k in range(len(steps)):
        rate = 0
        for n in range(2, NITEM):
            if first[n] - 3 >= k:
                want = min(end[n] + HPG + 1, len(scores)) - done
                rate = max(rate, -(-want // (first[n] - 2 - k)))
        here = scores[done:done + rate]
        done += len(here)
        slots.append(here + late.pop(k, []))
    assert done == len(scores)
    tail = [x for k in sorted(late) for x in late[k]]
    return steps, slots, tail


def adaln_two_layers(nc, A, out):
    ctx = ExitStack()
    with ctx:
        def sb(name, shape, dt=F32):
            return ctx.enter_context(nc.sbuf_tensor(name, shape, dt))

        def sem(name):
            return ctx.enter_context(nc.semaphore(name))

        xt = sb("xt", [P, NT, D])
        xn = sb("xn", [P, NT, D])
        PAD = TAPS - 1
        hT = sb("hT", [P, PAD + T])
        wslot = sb("wslot", [P, 2, 1536])
        ident = sb("ident", [P, P])
        identb = sb("identb", [P, P], BF16)
        maskqk = sb("maskqk", [P, P], BF16)
        maskkq = sb("maskkq", [P, P], BF16)
        blk = sb("blk", [P, P])
        stats = sb("stats", [P, NT, 6])
        mv = sb("mv", [P, NT, 2])
        sd = sb("sd", [P, NT])
        rstd = sb("rstd", [P, NT])
        modc = sb("modc", [P, 2, 8])
        gar = sb("gar", [P, 2, D])
        wo0 = sb("wo0", [P, D])
        wo1 = sb("wo1", [P, D])
        bo1 = sb("bo1", [P, D])
        wqa = sb("wqa", [P, QL])
        wkva = sb("wkva", [P, KVL])
        wqb = sb("wqb", [QL, 2, D])
        wkvb = sb("wkvb", [KVL, G1 * HD * 2])
        wkk = sb("wkk", [KVL, 3, G1 * HD])
        wr1 = sb("wr1", [P, 2 * E1])
        rwn = sb("rwn", [E0, D])
        rwT = sb("rwT", [P, E0])
        cbias = sb("cbias", [P, E0])
        tri = sb("tri", [P, NG0, NG0])
        tiny = sb("tiny", [P, 64])
        AW = 40800
        PW0 = 12288
        PW1 = 22528
        with nc.sbuf_tensor("arena_a", [P, PW1], F32) as arena_a:
            pass
        parts = sb("parts", [P, PW1], F32R)
        arena_b = sb("arena_b", [P, AW - PW1])
        ps = ctx.enter_context(nc.psum_tensor("ps", [P, 8, CW], F32))

        at = [0]

        def take(shape, dt=F32):
            n = 1
            for s in shape:
                n *= s
            words = n if dt != BF16 else (n + 1) // 2
            if at[0] < PW1 < at[0] + words:
                at[0] = PW1
            if at[0] >= PW1:
                v = arena_b[:, at[0] - PW1:at[0] - PW1 + words]
            else:
                v = (parts if dt == F32R else arena_a)[:, at[0]:at[0] + words]
            at[0] += words
            assert at[0] <= (PW1 if dt == F32R else AW), at[0]
            if dt == BF16:
                v = v.bitcast(dt)
            if len(shape) > 1:
                names = "abcd"[:len(shape)]
                v = v.rearrange("p (" + " ".join(names) + ") -> p " + " ".join(names),
                                **{names[i]: shape[i] for i in range(1, len(shape))})
            return v

        wmod = take([2, 6 * D])
        scb = take([2, P])
        win = take([2 * D + K0])
        wcv = take([TAPS, 2 * D + K0])
        wfold = take([TAPS, 3, P])
        wrows = take([2, M0, H0])
        bd = take([2, M0, K0, H0])
        tw = take([T])
        pw = take([T])
        gate = take([T])
        yg = xn[:, :, :].rearrange("p n d -> p (n d)")
        den = take([T])
        xv = take([2, CW])
        pw_poly = take([2, CW])
        tmp = take([3, CW])
        ssq = take([CW])
        phi = take([2, M0, CW])
        ang = take([2, M0, CW])
        nums = take([2, 2 * M0, CW])
        sqs = take([2 * M0, CW])
        fac = take([2, CW])
        at[0] = 0
        hid0 = take([NBUF, 2, CW], F32R)
        wsp0 = take([2, 2, 2 * GP * P], F32R)
        hs0 = take([2, T], F32R)
        assert at[0] == PW0
        scores = take([NT, E0])
        sfc = take([NT, E0])
        msk = take([NT, E0])
        b1 = take([NT, E0])
        b2 = take([NT, E0])
        comb3 = take([NT, 3, E0], BF16)
        combT = take([T], BF16)
        combL = take([T], BF16)
        sel = take([NPAIR, P], BF16)
        gsm = take([10, NT * NG0])
        top8 = take([NT, 8])
        wsum = take([3, NT])
        wsh = take([2, ISH])
        relu = take([2, CW])
        hid = take([2, CW])
        yT = take([T])
        sq0 = take([2, CW])
        prod0 = take([NBUF, CW])
        TAIL = AW - (G1 * T // 2 + NT * G1 * 32)
        assert at[0] <= TAIL, at[0]
        at[0] = TAIL
        kst = take([G1, T], BF16)
        vaug = take([NT, G1, 32])
        at[0] = 0
        qst = take([NC, H1, CW], BF16)
        mx = take([2, HPG, TPC, NC])
        nmx = take([HPG * TPC])
        nres = take([HPG * TPC])
        nm2 = take([2, HPG * TPC], BF16)
        nrow = take([2, P], BF16)
        rden = take([TPC, HPG])
        otok = xn
        ropec = take([T])
        ropes = take([T])
        assert at[0] <= PW1
        at[0] = PW1
        latq = take([2, CW])
        latk = take([2, CW])
        ra = take([2, CW])
        rb = take([2, CW])
        rk = take([2, CW])
        rl = take([2, CW])
        q3 = take([2, NSPLIT, CW], BF16)
        k3 = take([2, NSPLIT, CW], BF16)
        oT = take([2, CW])
        oTT = take([2, CW])
        probs = arena_b[:, 0:2 * HPG * CW].rearrange("p (a b c) -> p a b c", a=2, b=HPG)
        assert at[0] <= TAIL, at[0]
        at[0] = 0
        hs1 = take([2, T], F32R)
        hcw = take([2, 2, T], F32R)
        wsp1 = take([2, 2, 3 * F1], F32R)
        hid1 = take([NBUF, 2, CW], F32R)
        assert at[0] == PW1
        cwT = take([T])
        cwb = take([2, T])
        hcf = take([NC, CW])
        silg = take([2, CW])
        prod1 = take([NBUF, CW])
        lg = take([NT, 2 * E1])
        ex = take([NT, 2 * E1])
        cw = take([NT, E1])
        sm = take([6, NT * 2])
        y1T = take([T])
        obuf = take([NT, D])

        cw_dram = nc.dram_tensor("expert_weights", [E1, T], F32).ap()
        qs_dram = nc.dram_tensor("q_parts", [NSPLIT, P, T], BF16).ap()
        ks_dram = nc.dram_tensor("k_parts", [NSPLIT, G1 * HD, T], BF16).ap()

        ld_x = [sem(f"ld_x{c}") for c in range(NC)]
        ld_mod = sem("ld_mod")
        ld_a = sem("ld_a")
        ld_const = sem("ld_const")
        ld_small = sem("ld_small")
        ld_b = sem("ld_b")
        ld_c = sem("ld_c")
        ld_sel = sem("ld_sel")
        ld_rope = sem("ld_rope")
        ld_w0 = [sem(f"ld_w0_{i}") for i in range(2)]
        ld_w1 = [sem(f"ld_w1_{i}") for i in range(2)]
        st_qk = [sem(f"st_qk{b}") for b in range(2)]
        ld_stack = [sem(f"ld_stack{c}") for c in range(NC)]
        ld_nm = [sem(f"ld_nm{g}") for g in range(G1)]
        st_out = sem("st_out")
        s_v = sem("s_v")
        s_a = sem("s_a")
        pad_zero = sem("pad_zero")
        silu_c = sem("silu_c")
        scb_ready = sem("scb_ready")
        mod_mm = sem("mod_mm")
        mod_ready = sem("mod_ready")
        slope_in = sem("slope_in")
        slope_e = sem("slope_e")
        slope_u = sem("slope_u")
        slope_l = sem("slope_l")
        slope_ready = sem("slope_ready")
        fold_ready = sem("fold_ready")
        tw_ready = sem("tw_ready")
        dl_max = sem("dl_max")
        dl_exp = sem("dl_exp")
        bd_ready = sem("bd_ready")
        wo_ready = sem("wo_ready")
        ln_var = sem("ln_var")
        ln_sd = sem("ln_sd")
        ln_xn = sem("ln_xn")
        ln_tr = sem("ln_tr")
        ln_h = sem("ln_h")
        zs_mm = sem("zs_mm")
        zs_lin = sem("zs_lin")
        zs_exp = sem("zs_exp")
        pw_ready = sem("pw_ready")
        zv_mm = sem("zv_mm")
        zg_mm = sem("zg_mm")
        xv_ready = sem("xv_ready")
        gate_ready = sem("gate_ready")
        phi_ready = sem("phi_ready")
        trig_ready = sem("trig_ready")
        num_ready = sem("num_ready")
        sq_ready = sem("sq_ready")
        y_mm = sem("y_mm")
        ss_mm = sem("ss_mm")
        q_ready = sem("q_ready")
        rt_ready = sem("rt_ready")
        yg_ready = sem("yg_ready")
        o0_mm = sem("o0_mm")
        x1_ready = sem("x1_ready")
        rw_tr = sem("rw_tr")
        rw_ready = sem("rw_ready")
        lg_mm = sem("lg_mm")
        sig_ready = sem("sig_ready")
        sh_up = sem("sh_up")
        sh_hid = sem("sh_hid")
        sh_down = sem("sh_down")
        comb_ready = sem("comb_ready")
        comb_tr = sem("comb_tr")
        comb_T = sem("comb_T")
        moe_up = sem("moe_up")
        moe_cb = sem("moe_cb")
        moe_relu = sem("moe_relu")
        moe_sq = sem("moe_sq")
        moe_prod = sem("moe_prod")
        moe_hi = sem("moe_hi")
        moe_lo = sem("moe_lo")
        w0_hi = sem("w0_hi")
        w0_lo = sem("w0_lo")
        hs_lo = [sem(f"hs{l}_lo") for l in range(2)]
        moe_down = sem("moe_down")
        y0_ready = sem("y0_ready")
        y0_tr = sem("y0_tr")
        x2_ready = sem("x2_ready")
        wk_ready = sem("wk_ready")
        kones = sem("kones")
        qzero = sem("qzero")
        vzero = sem("vzero")
        lat_mm = sem("lat_mm")
        lat_ready = sem("lat_ready")
        qk_mm = sem("qk_mm")
        v_mm = sem("v_mm")
        v_ready = sem("v_ready")
        rope_done = sem("rope_done")
        split_ready = sem("split_ready")
        x2b_ready = sem("x2b_ready")
        slot_mm = sem("slot_mm")
        slot_read = sem("slot_read")
        nm_ready = sem("nm_ready")
        p2_mm = sem("p2_mm")
        p2_exp = sem("p2_exp")
        pv_mm = sem("pv_mm")
        o_copy = sem("o_copy")
        lg1_mm = sem("lg1_mm")
        lg1_max = sem("lg1_max")
        lg1_exp = sem("lg1_exp")
        cw_ready = sem("cw_ready")
        cw_tr = sem("cw_tr")
        cwT_ready = sem("cwT_ready")
        st_cw = sem("st_cw")
        ld_cwb = [sem(f"ld_cwb{b}") for b in range(2)]
        hc_prod = sem("hc_prod")
        hc_hi = sem("hc_hi")
        hc_lo = sem("hc_lo")
        w1_hi = sem("w1_hi")
        w1_lo = sem("w1_lo")
        ffn_g = sem("ffn_g")
        ffn_u = sem("ffn_u")
        ffn_silu = sem("ffn_silu")
        ffn_prod = sem("ffn_prod")
        ffn_hi = sem("ffn_hi")
        ffn_lo = sem("ffn_lo")
        ffn_down = sem("ffn_down")
        y1_ready = sem("y1_ready")
        y1_tr = sem("y1_tr")
        out_ready = sem("out_ready")

        STEPS, SLOTS, LAST_SLOTS = attention_schedule()
        READ = {what: m + 1 for m, what in enumerate([x for part in SLOTS for x in part] + LAST_SLOTS)}
        HALF = GP * NC
        MU = 2 * GP * NC
        assert MU == 2 * FT * NC
        N_IT0 = NLOAD // 2
        N_IT1 = E1 // 2

        def up0(slot, part, pair):
            return wsp0[:, slot, part, pair * P:(pair + 1) * P]

        def down0(slot, part, pair):
            return wsp0[:, slot, part, GP * P + pair * P:GP * P + (pair + 1) * P]

        def w1(slot, part, which, ft):
            return wsp1[:, slot, part, which * F1 + ft * P:which * F1 + (ft + 1) * P]

        def piece(n):
            return slice(n * CW, (n + 1) * CW)

        def tiles(c):
            return range(TPC * c, TPC * c + TPC)

        def chunk(c):
            return slice(c * CW, (c + 1) * CW)

        col = {n: i for i, n in enumerate(
            "c0 c1 sc0 sc1 bval bgate bs ssb ss slope nabs esl usl dsl msl rsl lsl zsl sp nsd".split())}

        def tc(name, n=1, parts=P):
            return tiny[0:parts, col[name]:col[name] + n]

        theta_c = tiny[:, 20:24]
        theta_n = tiny[:, 24:28]
        dlog = tiny[:, 28:31]
        dmax = tiny[:, 31:32]
        dexp = tiny[:, 32:35]
        dsum = tiny[:, 35:36]
        dw = tiny[:, 36:39]
        nsc = tiny[:, 39:40]
        gcol = tiny[:, 40:44]
        nscale = sb("nscale", [P, 2, M0])
        ones_w = sb("ones_w", [P, 1])

        block = ctx.enter_context(nc.Block())

        @block.sync
        def _(sp):
            sp.dma_start(tc("c0"), A["L0_c"].rearrange("a (p b) -> (a p) b", b=1)).then_inc(ld_mod, 16)
            sp.dma_start(tc("c1"), A["L1_c"].rearrange("a (p b) -> (a p) b", b=1)).then_inc(ld_mod, 16)
            sp.dma_start(wmod[:, 0, :], A["L0_wmod"]).then_inc(ld_mod, 16)
            sp.dma_start(wmod[:, 1, :], A["L1_wmod"]).then_inc(ld_mod, 16)
            x_v = A["L0_attn_x"].rearrange("a (n p) d -> p (a n) d", p=P)
            for c in range(NC):
                sp.dma_start(xt[:, TPC * c:TPC * c + TPC, :], x_v[:, TPC * c:TPC * c + TPC, :])\
                  .then_inc(ld_x[c], 16)
            sp.dma_start(ident[:, :], A["ident"]).then_inc(ld_const, 16)
            sp.dma_start(blk[:, :], A["blk"]).then_inc(ld_const, 16)
            sp.dma_start(win, A["L0_attn_W_in"]).then_inc(ld_a, 16)
            sp.dma_start(wcv, A["L0_attn_w_conv"].rearrange("k a c -> a (k c)").broadcast_to(
                [P, TAPS * (2 * D + K0)]).rearrange("p (k c) -> p k c", k=TAPS))\
              .then_inc(ld_a, 16)
            sp.dma_start(tw, A["dist"]).then_inc(ld_a, 16)
            bc = A["L0_attn_b_conv"]
            sp.dma_start(tc("bval"), bc[0:D].rearrange("(p b) -> p b", b=1)).then_inc(ld_small, 16)
            sp.dma_start(tc("bgate"), bc[D:2 * D].rearrange("(p b) -> p b", b=1)).then_inc(ld_small, 16)

            def by_head(dst, lo, n, src):
                sp.dma_start(dst[H0 * lo:H0 * (lo + n), :],
                             src.rearrange("(k h b) -> k h b", h=1, b=1).broadcast_to([n, H0, 1]))\
                  .then_inc(ld_small, 16)

            by_head(tc("bs"), 0, K0, bc[2 * D:2 * D + K0])
            by_head(tc("ss"), 0, K0, A["L0_attn_score_scale"])
            na = A["L0_attn_anchor_slopes"].shape[0]
            by_head(tc("slope"), 0, K0 - na, A["L0_attn_decay_slopes"])
            by_head(tc("slope"), K0 - na, na, A["L0_attn_anchor_slopes"])
            sp.dma_start(theta_c, A["L0_attn_theta"].rearrange("a b k h m -> (a b k h) m")).then_inc(ld_small, 16)
            sp.dma_start(dlog, A["L0_attn_deriv_logits"].rearrange("(a n) -> a n", a=1).broadcast_to([P, 3]))\
              .then_inc(ld_small, 16)
            for i, name in enumerate(("L0_attn_W_re", "L0_attn_W_im")):
                w = A[name].rearrange("(h m) j -> h (m j)", m=M0)
                sp.dma_start(wrows[:, i].rearrange("p m j -> p (m j)"),
                             w.unsqueeze(0).broadcast_to([K0, H0, M0 * H0])).then_inc(ld_small, 16)
            for i in range(2):
                n_v = A["L0_attn_norm_scale"].rearrange("(i h m) -> i h m", i=2, m=M0)[i]
                sp.dma_start(nscale[:, i, :],
                             n_v.unsqueeze(0).broadcast_to([K0, H0, M0])).then_inc(ld_small, 16)
            sp.dma_start(wo0[:, :], A["L0_attn_W_out"]).then_inc(ld_b, 16)
            sp.dma_start(rwn[:, :], A["L0_ffn_router_w"]).then_inc(ld_b, 16)
            sp.dma_start(cbias[:, :], A["L0_ffn_correction_bias"].rearrange("(a n) -> a n", a=1).broadcast_to([P, E0]))\
              .then_inc(ld_b, 16)
            sp.dma_start(tri[:, :, :].rearrange("p a b -> p (a b)"), A["tri"].rearrange("(a n) -> a n", a=1)
                         .broadcast_to([P, NG0 * NG0])).then_inc(ld_b, 16)
            up_v = A["L0_ffn_up_w"].rearrange("e d f -> d e f")
            down_v = A["L0_ffn_down_w"].rearrange("(n two) f d -> (two f) n d", two=2)

            def load0(slot, n):
                sp.dma_start(wslot[:, slot, 0:GP * P].rearrange("p (e f) -> p e f", f=I0),
                             up_v[:, bass.ds(2 * GP * n, 2 * GP), :]).then_inc(ld_w0[slot], 16)
                sp.dma_start(wslot[:, slot, GP * P:2 * GP * P].rearrange("p (n d) -> p n d", d=D),
                             down_v[:, bass.ds(GP * n, GP), :]).then_inc(ld_w0[slot], 16)

            for slot in range(2):
                load0(slot, slot)
            for dst, name in ((wqa[:, :], "L1_attn_Wqa"), (wkva[:, :], "L1_attn_Wkva"),
                              (wqb[:, 0, :], "L1_attn_Wqb"), (wkvb[:, :], "L1_attn_Wkvb"),
                              (wo1[:, :], "L1_attn_Wout"), (wr1[:, 0:E1], "L1_ffn_w_router"),
                              (wr1[:, E1:2 * E1], "L1_ffn_w_gating"), (identb[:, :], "identb"),
                              (maskqk[:, :], "maskqk"), (maskkq[:, :], "maskkq")):
                sp.dma_start(dst, A[name]).then_inc(ld_c, 16)
            sp.dma_start(bo1[:, :], A["L1_attn_bout"].rearrange("(a n) -> a n", a=1).broadcast_to([P, D]))\
              .then_inc(ld_c, 16)
            sp.wait_ge(x1_ready, NC)
            sp.dma_start(wsh[:, 0, :], A["L0_ffn_shared_up_w"]).then_inc(ld_sel, 16)
            sp.dma_start(wsh[:, 1, :].rearrange("p (n d) -> p n d", d=D),
                         A["L0_ffn_shared_down_w"].rearrange("(n p) d -> p n d", p=P)).then_inc(ld_sel, 16)
            sp.dma_start(sel, A["sel"].rearrange("p (n f) -> p n f", f=P)).then_inc(ld_sel, 16)
            with sp.Fori(1, N_IT0) as it:
                for slot in range(2):
                    sp.wait_ge(w0_lo, it * 4 + (2 * slot - 2))
                    load0(slot, it * 2 + slot)

            w1_views = [A["L1_ffn_w_gate"], A["L1_ffn_w_up"],
                        A["L1_ffn_w_down"].rearrange("e (n p) d -> e p n d", p=P)]

            def load1(slot, e):
                for which in range(2):
                    sp.dma_start(wslot[:, slot, which * F1:(which + 1) * F1],
                                 w1_views[which][bass.ds(e, 1), :, :].rearrange("a p n -> (a p) n"))\
                      .then_inc(ld_w1[slot], 16)
                sp.dma_start(wslot[:, slot, 2 * F1:3 * F1].rearrange("p (n d) -> p n d", d=D),
                             w1_views[2][bass.ds(e, 1), :, :, :].rearrange("a p n d -> (a p) n d"))\
                  .then_inc(ld_w1[slot], 16)

            sp.wait_ge(x2_ready, NC)
            sp.dma_start(ropec, A["ropec"]).then_inc(ld_rope, 16)
            sp.dma_start(ropes, A["ropes"]).then_inc(ld_rope, 16)
            for slot in range(2):
                load1(slot, slot)
            sp.wait_ge(kones, 1)
            sp.wait_ge(qzero, 1)

            def stack(c):
                sp.wait_ge(st_qk[c % 2], 32 * (c // 2 + 1))
                for a in range(NSPLIT):
                    for b in range(NSPLIT):
                        lo = (a * NSPLIT + b) * HD
                        sp.dma_start(kst[lo:lo + HD, :, chunk(c)],
                                     ks_dram[b, :, chunk(c)].rearrange("(g d) t -> d g t", d=HD))\
                          .then_inc(ld_stack[c], 16)
                        sp.dma_start(qst[lo:lo + HD, c, :, :],
                                     qs_dram[a, :, chunk(c)].rearrange("(h d) t -> d h t", d=HD))\
                          .then_inc(ld_stack[c], 16)

            for c in range(NC):
                sp.wait_ge(split_ready, 2 * c + 2)
                sp.dma_start(qs_dram[:, :, chunk(c)].rearrange("s p t -> p s t"), q3[:, c % 2])\
                  .then_inc(st_qk[c % 2], 16)
                sp.dma_start(ks_dram[:, :, chunk(c)].rearrange("s p t -> p s t"),
                             k3[0:G1 * HD, c % 2]).then_inc(st_qk[c % 2], 16)
                stack(c)
            for n in range(NITEM):
                c, g = n // G1, n % G1
                sp.wait_ge(slot_read, READ["maxima", n])
                for s in range(2):
                    sp.dma_start(qst[KROWS + s:KROWS + s + 1, c, HPG * g:HPG * g + HPG, :].rearrange("p h t -> p (h t)"),
                                 nrow[s * HPG * TPC:(s + 1) * HPG * TPC, n % 2, :]).then_inc(ld_nm[g], 16)
            sp.wait_ge(cwT_ready, 1)
            sp.dma_start(cw_dram, cwT[0:E1, :]).then_inc(st_cw, 16)
            sp.wait_ge(st_cw, 16)

            def load_cwb(slot, e):
                sp.dma_start(cwb[:, slot, :], cw_dram[bass.ds(e, 1), :].broadcast_to([P, T]))\
                  .then_inc(ld_cwb[slot], 16)

            for slot in range(2):
                load_cwb(slot, slot)
            with sp.Fori(1, N_IT1) as it:
                for slot in range(2):
                    sp.wait_ge(w1_lo, it * 6 + (3 * slot - 3))
                    load1(slot, it * 2 + slot)
                    sp.wait_ge(hc_prod, it * (2 * NC) + (NC * slot - NC))
                    load_cwb(slot, it * 2 + slot)
            out_v = out.rearrange("a (n p) d -> p (a n) d", p=P)
            for c in range(NC):
                sp.wait_ge(out_ready, c + 1)
                sp.dma_start(out_v[:, TPC * c:TPC * c + TPC, :], obuf[:, TPC * c:TPC * c + TPC, :])\
                  .then_inc(st_out, 16)
            sp.wait_ge(st_out, 16 * NC)

        @block.gpsimd
        def _(pool):
            nc.gpsimd.memset(hT[:, 0:PAD], 0.0).then_inc(pad_zero, 1)
            pool.wait_ge(x1_ready, NC)
            nc.gpsimd.memset(kst[64:P, :, :], 1.0).then_inc(kones, 1)
            pool.wait_ge(kones, 1)
            nc.gpsimd.memset(vaug, 0.0).then_inc(vzero, 1)
            pool.wait_ge(vzero, 1)
            nc.gpsimd.memset(vaug[:, :, :, HD:HD + 1], 1.0).then_inc(vzero, 1)
            pool.wait_ge(vzero, 2)
            pool.wait_ge(x2_ready, NC)
            nc.gpsimd.memset(qst[64:P].rearrange("p c h t -> p (c h t)").bitcast(F32), 0.0).then_inc(qzero, 1)

        @block.tensor
        def _(pe):
            mm = nc.tensor.matmul

            def norm(i):
                for c in range(NC):
                    pe.wait_ge(ln_xn, i * NC + c + 1)
                    if c == 0 and i == 0:
                        pe.wait_ge(ld_const, 32)
                    if c >= 2:
                        pe.wait_ge(ln_h, i * NC + c - 1)
                    for k, t in enumerate(tiles(c)):
                        last = nc.tensor.transpose(ps[:, c % 2, k * P:(k + 1) * P], xn[:, t, :], ident[:, :])
                    last.then_inc(ln_tr, 1)

            pe.wait_ge(ld_mod, 64)
            pe.wait_ge(scb_ready, 2)
            for l in range(2):
                mm(ps[:, 2, l * P:(l + 1) * P], scb[:, l, :], wmod[:, l, 2 * D:3 * D], start=True, stop=True)
                for n, j in enumerate((0, 1, 3, 4, 5)):
                    last = mm(ps[:, 3, 8 * l + n:8 * l + n + 1], wmod[:, l, j * D:(j + 1) * D],
                              tc("sc0" if l == 0 else "sc1"), start=True, stop=True)
            last.then_inc(mod_mm, 1)

            norm(0)

            def project(bank, grp, c, done):
                for k in range(TAPS):
                    last = mm(ps[:, bank, :], wfold[:, k, grp, :], hT[:, c * CW + k:c * CW + k + CW],
                              start=(k == 0), stop=(k == TAPS - 1))
                last.then_inc(done, 1)

            pe.wait_ge(fold_ready, 3)
            pe.wait_ge(pad_zero, 1)
            pe.wait_ge(mod_ready, 1)
            for c in range(NC):
                pe.wait_ge(ln_h, c + 1)
                if c >= 2:
                    pe.wait_ge(zs_lin, c - 1)
                project(2 + c % 2, 2, c, zs_mm)

            def mix(c):
                pe.wait_ge(num_ready, 2 * M0 * (c + 1))
                if c == 0:
                    pe.wait_ge(bd_ready, 1)
                if c >= 2:
                    pe.wait_ge(yg_ready, c - 1)
                for n in range(2 * M0):
                    last = mm(ps[:, 6 + c % 2, :], bd[:, n // M0, n % M0].rearrange("p k j -> p (k j)"),
                              nums[:, c % 2, n, :], start=(n == 0), stop=(n == 2 * M0 - 1))
                last.then_inc(y_mm, 1)
                pe.wait_ge(sq_ready, c + 1)
                for n in range(2 * M0):
                    last = mm(ps[:, c % 2, :], blk[:, :], sqs[:, n, :], start=(n == 0), stop=(n == 2 * M0 - 1))
                last.then_inc(ss_mm, 1)

            def out0(c):
                pe.wait_ge(yg_ready, c + 1)
                if c == 0:
                    pe.wait_ge(wo_ready, 1)
                pe.wait_ge(zs_lin, NC)
                if c >= 2:
                    pe.wait_ge(x1_ready, c - 1)
                for k, t in enumerate(tiles(c)):
                    last = mm(ps[:, 2 + c % 2, k * P:(k + 1) * P], yg[:, t * P:(t + 1) * P], wo0[:, :],
                              start=True, stop=True)
                last.then_inc(o0_mm, 1)

            for c in range(NC):
                if c >= 1:
                    pe.wait_ge(xv_ready, c)
                project(4, 0, c, zv_mm)
                if c >= 1:
                    pe.wait_ge(gate_ready, c)
                project(5, 1, c, zg_mm)
                if c >= 1:
                    mix(c - 1)
                if c >= 2:
                    out0(c - 2)
            mix(NC - 1)
            out0(NC - 2)
            out0(NC - 1)

            norm(1)

            pe.wait_ge(ld_b, 64)
            nc.tensor.transpose(ps[:, 2, 0:E0], rwn[:, :], ident[0:E0, 0:E0]).then_inc(rw_tr, 1)
            pe.wait_ge(rw_ready, 1)
            for c in range(NC):
                pe.wait_ge(ln_h, 1 * NC + c + 1)
                for t in tiles(c):
                    last = mm(ps[:, 2 + t // 8, (t % 8) * E0:(t % 8 + 1) * E0],
                              hT[:, PAD + t * P:PAD + (t + 1) * P], rwT[:, :], start=True, stop=True)
            last.then_inc(lg_mm, 1)

            def rhs(c):
                return hT[:, PAD + c * CW:PAD + (c + 1) * CW]

            pe.wait_ge(ld_sel, 48)

            def shared_up(n):
                if n >= 2:
                    pe.wait_ge(sh_hid, n - 1)
                mm(ps[:, n % 2, :], wsh[:, 0, (n // NC) * P:(n // NC + 1) * P], rhs(n % NC),
                   start=True, stop=True).then_inc(sh_up, 1)

            def shared_down(n):
                pe.wait_ge(sh_hid, n + 1)
                mm(ps[:, 4 + n % NC, :], wsh[:, 1, (n // NC) * P:(n // NC + 1) * P], hid[:, n % 2, :],
                   start=(n < NC), stop=False).then_inc(sh_down, 1)

            NSU = NSH * NC
            for n in range(NSU + 1):
                if n < NSU:
                    shared_up(n)
                if n >= 1:
                    shared_down(n - 1)

            pe.wait_ge(ld_c, 16 * 11)
            for c in range(NC):
                pe.wait_ge(comb_ready, 1)
                if c >= 1:
                    pe.wait_ge(comb_T, 2 * c)
                pc = ps[:, 2:4, :].bitcast(BF16)
                for k, t in enumerate(tiles(c)):
                    nc.tensor.transpose(pc[:, 0, k * P:(k + 1) * P],
                                        comb3[:, t, 0:2, :].rearrange("p s e -> p (s e)"), identb[:, :])
                    last = nc.tensor.transpose(pc[0:E0, 1, k * P:(k + 1) * P], comb3[:, t, 2, :], identb[:, :])
                last.then_inc(comb_tr, 1)
            pe.wait_ge(comb_T, 2 * NC)

            def three(bank, w, x, start, stop):
                mm(bank, w(0), x(0), start=start, stop=False)
                mm(bank, w(0), x(1), start=False, stop=False)
                return mm(bank, w(1), x(0), start=False, stop=stop)

            def look0(base, k, n0, loads):
                pair, c = k // NC, k % NC
                slot = (pair // GP) % 2
                if k % HALF == 0:
                    pe.wait_ge(w0_lo, loads)
                if n0 is not None:
                    pe.wait_ge(moe_prod, n0 + (k - 1))
                three(ps[:, k % 2, :], lambda i: up0(slot, i, pair % GP), lambda i: hs0[:, i, chunk(c)],
                      True, True).then_inc(moe_up, 1)
                w = sel[:, bass.ds(base + pair, 1), :].rearrange("p a f -> p (a f)")
                mm(ps[:, 2 + k % 2, :], w, combT[:, chunk(c)], start=True, stop=False)
                wl = sel[0:E0, bass.ds(base + pair, 1), :].rearrange("p a f -> p (a f)")
                mm(ps[:, 2 + k % 2, :], wl, combL[0:E0, chunk(c)], start=False, stop=True).then_inc(moe_cb, 1)

            def sum0(n0, k, last_one):
                pair, c = k // NC, k % NC
                pe.wait_ge(moe_lo, n0 + (k + 1))
                three(ps[:, 4 + c, :], lambda i: down0((pair // GP) % 2, i, pair % GP),
                      lambda i: hid0[:, k % NBUF, i, :], False, last_one).then_inc(moe_down, 1)

            pe.wait_ge(hs_lo[0], NC)
            for k in range(LOOK):
                look0(0, k, 0 if k >= 2 else None, 2)
            with pe.Fori(0, N_IT0 - 1) as it:
                for k in range(MU):
                    if k + LOOK < MU:
                        look0(it * (2 * GP), k + LOOK, it * MU, it * 4 + 4)
                    else:
                        look0(it * (2 * GP) + 2 * GP, k + LOOK - MU, it * MU + MU, it * 4 + 6)
                    sum0(it * MU, k, False)
            for k in range(MU):
                if k + LOOK < MU:
                    look0((N_IT0 - 1) * 2 * GP, k + LOOK, (N_IT0 - 1) * MU, N_IT0 * 4)
                sum0((N_IT0 - 1) * MU, k, k >= MU - NC)

            for c in range(NC):
                pe.wait_ge(y0_ready, c + 1)
                if c >= 2:
                    pe.wait_ge(x2_ready, c - 1)
                for k in range(TPC):
                    last = nc.tensor.transpose(ps[:, 2 + c % 2, k * P:(k + 1) * P],
                                               yT[:, c * CW + k * P:c * CW + (k + 1) * P], ident[:, :])
                last.then_inc(y0_tr, 1)

            norm(2)

            pe.wait_ge(wk_ready, 1)
            for c in range(NC):
                pe.wait_ge(ln_h, 2 * NC + c + 1)
                if c >= 1:
                    pe.wait_ge(v_ready, c)
                mm(ps[0:QL, 2, :], wqa[:, :], rhs(c), start=True, stop=True)
                mm(ps[0:KVL, 3, :], wkva[:, :], rhs(c), start=True, stop=True).then_inc(lat_mm, 1)
                pe.wait_ge(lat_ready, 2 * c + 2)
                if c >= 1:
                    pe.wait_ge(rope_done, 4 * c)
                mm(ps[:, 4, :], wqb[:, 0, :], latq[0:QL, c % 2, :], start=True, stop=True)
                mm(ps[:, 5, :], wqb[:, 1, :], latq[0:QL, c % 2, :], start=True, stop=True)
                mm(ps[0:32, 6, :], wkk[:, 0, :], latk[0:KVL, c % 2, :], start=True, stop=True)
                mm(ps[0:32, 7, :], wkk[:, 1, :], latk[0:KVL, c % 2, :], start=True, stop=True).then_inc(qk_mm, 1)
                for k in range(TPC):
                    last = mm(ps[:, 2, k * 32:(k + 1) * 32], latk[0:KVL, c % 2, k * P:(k + 1) * P], wkk[:, 2, :],
                              start=True, stop=True)
                last.then_inc(v_mm, 1)

            slot_at = [0]

            def slot(what):
                m = slot_at[0]
                slot_at[0] += 1
                if m >= 2:
                    pe.wait_ge(slot_read, m - 1)
                b = ps[:, m % 2, :]
                if what[0] == "scores":
                    _, n, t, u, i = what
                    g = n % G1
                    if n % G1 == 0:
                        pe.wait_ge(ld_stack[n // G1], 32 * NSPLIT * NSPLIT)
                    diag = u == t // TPC
                    full = t % TPC * P if diag else CW
                    q = qst[:, t // TPC, HPG * g + i, t % TPC * P:(t % TPC + 1) * P]
                    if full:
                        last = mm(b[:, 0:full], q, kst[:, g, u * CW:u * CW + full], start=True, stop=True)
                    if diag:
                        mm(b[:, full:full + P], q, kst[:, g, t * P:(t + 1) * P], start=True, stop=False)
                        last = mm(b[:, full:full + P], identb[:, :], maskqk[:, :], start=False, stop=True)
                elif what[0] == "maxima":
                    pe.wait_ge(nm_ready, what[1] + 1)
                    last = nc.tensor.transpose(b[0:2 * HPG * TPC, 0:P // 2].bitcast(BF16),
                                               nm2.rearrange("p s n -> p (s n)"), identb[:, :])
                elif what[0] == "out":
                    n = what[1]
                    pe.wait_ge(o_copy, n + 1)
                    for k in range(TPC):
                        last = nc.tensor.transpose(b[:, k * P:(k + 1) * P], oT[:, n % 2, k * P:(k + 1) * P],
                                                   ident[:, :])
                elif what[0] == "turned":
                    c = what[1]
                    pe.wait_ge(slot_read, READ["out", c * G1 + G1 - 1])
                    for k, t in enumerate(tiles(c)):
                        last = nc.tensor.transpose(b[:, k * P:(k + 1) * P], otok[:, t, :], ident[:, :])
                else:
                    c = what[1]
                    pe.wait_ge(slot_read, READ["turned", c])
                    for k in range(TPC):
                        last = mm(b[:, k * P:(k + 1) * P], oTT[:, c % 2, k * P:(k + 1) * P], wo1[:, :],
                                  start=True, stop=True)
                last.then_inc(slot_mm, 1)

            def sum_scores(s, pair):
                n, j = STEPS[s]
                c, g = n // G1, n % G1
                off = max(0, j - TPC * c) * P
                if s >= 1:
                    pe.wait_ge(p2_exp, 2 * s + pair - 1)
                for i in (2 * pair, 2 * pair + 1):
                    k = kst[:, g, j * P:(j + 1) * P]
                    q = qst[:, c, HPG * g + i, :]
                    full = off
                    if j >= TPC * c:
                        full = off + P
                        mm(ps[:, 2 + i, off:full], k, q[:, off:full], start=True, stop=False)
                        last = mm(ps[:, 2 + i, off:full], identb[:, :], maskkq[:, :], start=False, stop=True)
                    if full < CW:
                        last = mm(ps[:, 2 + i, full:CW], k, q[:, full:CW], start=True, stop=True)
                last.then_inc(p2_mm, 1)

            def values(s):
                n, j = STEPS[s]
                c, g = n // G1, n % G1
                off = max(0, j - TPC * c) * P
                pe.wait_ge(p2_exp, 2 * s + 2)
                if j == 0 and n >= 2:
                    pe.wait_ge(o_copy, n - 1)
                for i in range(HPG):
                    last = mm(ps[32 * i:32 * i + 32, 6 + n % 2, off:CW], vaug[:, j, g, :],
                              probs[:, s % 2, i, off:CW], start=(j == 0), stop=(j == TPC * c + TPC - 1),
                              tile_position=(0, 32 * i))
                last.then_inc(pv_mm, 1)

            pe.wait_ge(v_ready, NC)
            pe.wait_ge(rope_done, 4 * NC)
            for what in SLOTS[0]:
                slot(what)
            for s, (n, j) in enumerate(STEPS):
                beside = SLOTS[s + 1]
                if j == 0:
                    pe.wait_ge(ld_nm[n % G1], 32 * (n // G1 + 1))
                cuts = [0, (len(beside) + 3) // 4, (len(beside) + 1) // 2, len(beside)]
                sum_scores(s, 0)
                for what in beside[cuts[0]:cuts[1]]:
                    slot(what)
                sum_scores(s, 1)
                for what in beside[cuts[1]:cuts[2]]:
                    slot(what)
                if s >= 1:
                    values(s - 1)
                for what in beside[cuts[2]:cuts[3]]:
                    slot(what)
            values(len(STEPS) - 1)
            for what in LAST_SLOTS:
                slot(what)

            norm(3)

            for c in range(NC):
                pe.wait_ge(ln_h, 3 * NC + c + 1)
                for t in tiles(c):
                    last = mm(ps[:, 2, t * 2 * E1:(t + 1) * 2 * E1], hT[:, PAD + t * P:PAD + (t + 1) * P], wr1[:, :],
                              start=True, stop=True)
            last.then_inc(lg1_mm, 1)
            pe.wait_ge(cw_ready, 1)
            for t in range(NT):
                last = nc.tensor.transpose(ps[0:E1, 4 + t // TPC, t % TPC * P:(t % TPC + 1) * P], cw[:, t, :],
                                           ident[:, :])
            last.then_inc(cw_tr, 1)
            pe.wait_ge(cwT_ready, 1)

            def look1(k, n0, w_parts, h_parts):
                e, ft, c = k // (FT * NC), k // NC % FT, k % NC
                if k % HALF == 0:
                    pe.wait_ge(w1_lo, w_parts)
                    pe.wait_ge(hc_lo, h_parts)
                if n0 is not None:
                    pe.wait_ge(ffn_prod, n0 + (k - 1))
                three(ps[:, k % 2, :], lambda i: w1(e, i, 0, ft), lambda i: hs1[:, i, chunk(c)],
                      True, True).then_inc(ffn_g, 1)
                three(ps[:, 2 + k % 2, :], lambda i: w1(e, i, 1, ft), lambda i: hcw[:, e, i, chunk(c)],
                      True, True).then_inc(ffn_u, 1)

            def sum1(n0, k, first, last_one):
                e, ft, c = k // (FT * NC), k // NC % FT, k % NC
                pe.wait_ge(ffn_lo, n0 + (k + 1))
                three(ps[:, 4 + c, :], lambda i: w1(e, i, 2, ft), lambda i: hid1[:, k % NBUF, i, :],
                      first, last_one).then_inc(ffn_down, 1)

            pe.wait_ge(hs_lo[1], NC)
            for k in range(LOOK):
                look1(k, 0 if k >= 2 else None, 3, NC)
            for k in range(MU):
                if k + LOOK < MU:
                    look1(k + LOOK, 0, 6, 2 * NC)
                else:
                    look1(k + LOOK - MU, MU, 9, 3 * NC)
                sum1(0, k, k < NC, False)
            with pe.Fori(1, N_IT1 - 1) as it:
                for k in range(MU):
                    if k + LOOK < MU:
                        look1(k + LOOK, it * MU, it * 6 + 6, it * (2 * NC) + 2 * NC)
                    else:
                        look1(k + LOOK - MU, it * MU + MU, it * 6 + 9, it * (2 * NC) + 3 * NC)
                    sum1(it * MU, k, False, False)
            for k in range(MU):
                if k + LOOK < MU:
                    look1(k + LOOK, (N_IT1 - 1) * MU, 6 * N_IT1, 2 * NC * N_IT1)
                sum1((N_IT1 - 1) * MU, k, False, k >= MU - NC)
            for c in range(NC):
                pe.wait_ge(y1_ready, c + 1)
                if c >= 2:
                    pe.wait_ge(out_ready, c - 1)
                for k in range(TPC):
                    last = nc.tensor.transpose(ps[:, 2 + c % 2, k * P:(k + 1) * P],
                                               y1T[:, c * CW + k * P:c * CW + (k + 1) * P], ident[:, :])
                last.then_inc(y1_tr, 1)

        @block.scalar
        def _(act):
            a = nc.scalar.activation
            own = [0]

            def step(ins):
                own[0] += 1
                ins.then_inc(s_a, 1)

            def settle():
                act.wait_ge(s_a, own[0])

            def norm(i):
                act.wait_ge(ln_var, i + 1)
                a(sd[:, :], mv[:, :, 1], ACT.Sqrt).then_inc(ln_sd, 1)
                l, j = i // 2, 2 * (i % 2)
                if i == 0:
                    act.wait_ge(mod_ready, 1)
                for c in range(NC):
                    act.wait_ge(ln_tr, i * NC + c + 1)
                    if i % 2:
                        a((hs0, hs1)[l][:, 0, chunk(c)], ps[:, c % 2, :], ACT.Identity,
                          bias=modc[:, l, j:j + 1], scale=modc[:, l, j + 1:j + 2])
                    a(hT[:, PAD + c * CW:PAD + (c + 1) * CW], ps[:, c % 2, :], ACT.Identity,
                      bias=modc[:, l, j:j + 1], scale=modc[:, l, j + 1:j + 2]).then_inc(ln_h, 1)

            act.wait_ge(ld_mod, 64)
            a(tiny[:, 2:4], tiny[:, 0:2], ACT.Silu).then_inc(silu_c, 1)
            n_small = 16 * 12
            act.wait_ge(ld_small, n_small)
            step(a(tc("nabs"), tc("slope"), ACT.Abs))
            settle()
            a(tc("esl"), tc("nabs"), ACT.Exp, scale=-1.0).then_inc(slope_e, 1)
            act.wait_ge(slope_u, 1)
            a(tc("lsl"), tc("usl"), ACT.Ln).then_inc(slope_l, 1)
            act.wait_ge(dl_max, 1)
            a(dexp, dlog, ACT.Exp, bias=dmax, scale=1.0, accum_out=dsum).then_inc(dl_exp, 1)
            act.wait_ge(slope_ready, 1)
            act.wait_ge(ld_a, 48)
            a(tw, tw, ACT.Exp, scale=tc("nsd")).then_inc(tw_ready, 1)
            norm(0)

            for c in range(NC):
                act.wait_ge(zs_lin, c + 1)
                a(pw[:, chunk(c)], pw[:, chunk(c)], ACT.Exp).then_inc(zs_exp, 1)

            def values(c):
                act.wait_ge(zv_mm, c + 1)
                if c >= 2:
                    act.wait_ge(phi_ready, c - 1)
                a(xv[:, c % 2, :], ps[:, 4, :], ACT.Identity, bias=tc("bval")).then_inc(xv_ready, 1)
                act.wait_ge(zg_mm, c + 1)
                a(gate[:, chunk(c)], ps[:, 5, :], ACT.Silu, bias=tc("bgate")).then_inc(gate_ready, 1)

            def trig(c):
                act.wait_ge(phi_ready, c + 1)
                step(a(ang[:, c % 2], phi[:, c % 2], ACT.Abs))
                settle()
                step(a(ang[:, c % 2], ang[:, c % 2], ACT.Sin, bias=nsc, scale=-1.0))
                step(a(phi[:, c % 2], phi[:, c % 2], ACT.Sin))
                settle()
                nc.scalar.activation(nsc_copy, nsc, ACT.Copy).then_inc(trig_ready, 1)

            def squares(c):
                act.wait_ge(num_ready, 2 * M0 * (c + 1))
                if c >= 1:
                    act.wait_ge(ss_mm, c)
                a(sqs, nums[:, c % 2], ACT.Square).then_inc(sq_ready, 1)

            def root(c):
                act.wait_ge(q_ready, c + 1)
                a(ssq, ssq, ACT.Sqrt).then_inc(rt_ready, 1)

            nsc_copy = tiny[:, 44:45]
            values(0)
            trig(0)
            for c in range(NC):
                if c + 1 < NC:
                    values(c + 1)
                    trig(c + 1)
                squares(c)
                if c >= 1:
                    root(c - 1)
            root(NC - 1)

            norm(1)
            act.wait_ge(rw_tr, 1)
            a(rwT[:, :], ps[:, 2, 0:E0], ACT.Copy).then_inc(rw_ready, 1)

            def high0(slot, n, loaded):
                if loaded is not None:
                    act.wait_ge(ld_w0[slot], loaded)
                a(wsp0[:, slot, 0, piece(n)], wslot[:, slot, piece(n)], ACT.Copy).then_inc(w0_hi, 1)

            high0(0, 0, 32)
            high0(0, 1, None)
            act.wait_ge(lg_mm, 1)
            a(scores.rearrange("p (b n) e -> p b (n e)", b=2), ps[:, 2:4, :], ACT.Sigmoid).then_inc(sig_ready, 1)
            for n in range(NSH * NC):
                act.wait_ge(sh_up, n + 1)
                if n >= 2:
                    act.wait_ge(sh_down, n - 1)
                step(a(relu[:, n % 2, :], ps[:, n % 2, :], ACT.Relu))
                settle()
                a(hid[:, n % 2, :], relu[:, n % 2, :], ACT.Square).then_inc(sh_hid, 1)
            for c in range(NC):
                act.wait_ge(comb_tr, c + 1)
                a(combT[:, chunk(c)], ps[:, 2, 0:CW // 2].bitcast(BF16), ACT.Copy).then_inc(comb_T, 1)
                a(combL[0:E0, chunk(c)], ps[0:E0, 3, 0:CW // 2].bitcast(BF16), ACT.Copy).then_inc(comb_T, 1)

            def relu0(n0, k):
                act.wait_ge(moe_up, n0 + (k + 1))
                a(relu[:, k % 2, :], ps[:, k % 2, :], ACT.Relu).then_inc(moe_relu, 1)

            def sq_unit(n0, k):
                act.wait_ge(moe_relu, n0 + (k + 1))
                a(sq0[:, k % 2, :], relu[:, k % 2, :], ACT.Square).then_inc(moe_sq, 1)

            def high_unit(n0, k):
                act.wait_ge(moe_prod, n0 + (k + 1))
                a(hid0[:, k % NBUF, 0, :], prod0[:, k % NBUF, :], ACT.Copy).then_inc(moe_hi, 1)

            def units0(n0, nb, loads, last_iteration):
                for k in range(MU):
                    n = (n0, k + 1) if k + 1 < MU else (nb, 0)
                    if n[0] is not None:
                        relu0(*n)
                    high_unit(n0, k)
                    if n[0] is not None:
                        sq_unit(*n)
                    half, u = k // HALF, k % HALF
                    if u in (4, 6) and not (last_iteration and half):
                        high0((half + 1) % 2, u // 2 - 2, loads * 16 + (32 if half == 0 else 64))

            relu0(0, 0)
            sq_unit(0, 0)
            with act.Fori(0, N_IT0 - 1) as it:
                units0(it * MU, it * MU + MU, it * 2, False)
            units0((N_IT0 - 1) * MU, None, (N_IT0 - 1) * 2, True)
            for c in range(NC):
                if c == 0:
                    act.wait_ge(moe_down, N_IT0 * MU)
                a(yT[:, chunk(c)], ps[:, 4 + c, :], ACT.Copy, scale=modc[:, 0, 4:5]).then_inc(y0_ready, 1)

            norm(2)
            for c in range(NC):
                act.wait_ge(lat_mm, c + 1)
                a(latq[0:QL, c % 2, :], ps[0:QL, 2, :], ACT.Copy).then_inc(lat_ready, 1)
                a(latk[0:KVL, c % 2, :], ps[0:KVL, 3, :], ACT.Copy).then_inc(lat_ready, 1)
                act.wait_ge(v_mm, c + 1)
                act.wait_ge(vzero, 2)
                a(vaug[:, TPC * c:TPC * c + TPC, :, 0:HD],
                  ps[:, 2, 0:TPC * 32].rearrange("p (n g d) -> p n g d", g=G1, d=HD), ACT.Copy)\
                    .then_inc(v_ready, 1)

            scale = float(HD) ** -0.5
            for s, (n, j) in enumerate(STEPS):
                off = max(0, j - TPC * (n // G1)) * P
                for pair in range(2):
                    act.wait_ge(p2_mm, 2 * s + pair + 1)
                    if s >= 2:
                        act.wait_ge(pv_mm, s - 1)
                    a(probs[:, s % 2, 2 * pair:2 * pair + 2, off:CW],
                      ps[:, 2 + 2 * pair:4 + 2 * pair, off:CW], ACT.Exp, scale=scale).then_inc(p2_exp, 1)

            norm(3)
            act.wait_ge(lg1_max, 1)
            a(ex, lg, ACT.Exp).then_inc(lg1_exp, 1)
            act.wait_ge(cw_tr, 1)
            a(cwT[0:E1, :].rearrange("p (c t) -> p c t", c=NC), ps[0:E1, 4:8, :], ACT.Copy).then_inc(cwT_ready, 1)

            def high1(slot, n, loaded):
                if loaded is not None:
                    act.wait_ge(ld_w1[slot], loaded)
                a(wsp1[:, slot, 0, piece(n)], wslot[:, slot, piece(n)], ACT.Copy).then_inc(w1_hi, 1)

            def high_stream(slot, c, n):
                act.wait_ge(hc_prod, n + 1)
                a(hcw[:, slot, 0, chunk(c)], hcf[:, c, :], ACT.Copy).then_inc(hc_hi, 1)

            def silu1(n0, k):
                act.wait_ge(ffn_g, n0 + (k + 1))
                a(silg[:, k % 2, :], ps[:, k % 2, :], ACT.Silu).then_inc(ffn_silu, 1)

            def high_hid(n0, k):
                act.wait_ge(ffn_prod, n0 + (k + 1))
                a(hid1[:, k % NBUF, 0, :], prod1[:, k % NBUF, :], ACT.Copy).then_inc(ffn_hi, 1)

            def units1(n0, nb, it2, last_iteration):
                for k in range(MU):
                    n = (n0, k + 1) if k + 1 < MU else (nb, 0)
                    if n[0] is not None:
                        silu1(*n)
                    high_hid(n0, k)
                    half, u = k // HALF, k % HALF
                    if last_iteration and half:
                        continue
                    if u in (4, 6, 8):
                        high1((half + 1) % 2, u // 2 - 2, it2 * 24 + (48 if half == 0 else 96))
                    if u in (5, 7, 9, 11):
                        c = (u - 5) // 2
                        high_stream((half + 1) % 2, c, it2 * NC + ((half + 1) * NC + c))

            for n in range(3):
                high1(0, n, 48)
            for c in range(NC):
                high_stream(0, c, c)
            silu1(0, 0)
            with act.Fori(0, N_IT1 - 1) as it:
                units1(it * MU, it * MU + MU, it * 2, False)
            units1((N_IT1 - 1) * MU, None, (N_IT1 - 1) * 2, True)
            for c in range(NC):
                if c == 0:
                    act.wait_ge(ffn_down, N_IT1 * MU)
                a(y1T[:, chunk(c)], ps[:, 4 + c, :], ACT.Copy, scale=modc[:, 1, 4:5]).then_inc(y1_ready, 1)

        @block.vector
        def _(dve):
            v = nc.vector
            own = [0]

            def step(ins):
                own[0] += 1
                ins.then_inc(s_v, 1)

            def settle():
                dve.wait_ge(s_v, own[0])

            def chain(ins):
                step(ins)
                settle()

            def norm(i, ready, counted=False):
                for t in range(0 if not counted else NT, NT):
                    if t % TPC == 0:
                        ready(t // TPC)
                    step(v.bn_stats(stats[:, t, :], xt[:, t, :]))
                settle()
                for t in range(NT):
                    step(v.bn_aggr(mv[:, t, :], stats[:, t, :]))
                settle()
                v.tensor_scalar(mv[:, :, 1], mv[:, :, 1], EPS, None, ALU.add).then_inc(ln_var, 1)
                dve.wait_ge(ln_sd, i + 1)
                chain(v.reciprocal(rstd[:, :], sd[:, :]))
                for c in range(NC):
                    for t in tiles(c):
                        last = v.tensor_scalar(xn[:, t, :], xt[:, t, :], mv[:, t, 0:1], rstd[:, t:t + 1],
                                               ALU.subtract, ALU.mult)
                    last.then_inc(ln_xn, 1)

            dve.wait_ge(silu_c, 1)
            for l in range(2):
                v.tensor_copy(scb[:, l, :], tiny[:, 2 + l:3 + l].broadcast_to([P, P])).then_inc(scb_ready, 1)
            dve.wait_ge(mod_mm, 1)
            for l in range(2):
                m = ps[:, 3, 8 * l:8 * l + 5]
                step(v.tensor_copy(modc[:, l, 0:5], m))
                step(v.tensor_scalar(gcol[:, 0:1], m[:, 4:5], 0.0, 2.0, ALU.is_ge, ALU.mult))
                step(v.tensor_scalar(gcol[:, 1:2], m[:, 4:5], -1.0, 0.25, ALU.mult, ALU.max))
                r = ps[:, 2, l * P:(l + 1) * P]
                step(v.tensor_scalar(gar[:, l, :], r, 0.0, 2.0, ALU.is_ge, ALU.mult))
                step(v.tensor_scalar(scb[:, l, :], r, -1.0, 0.25, ALU.mult, ALU.max))
                settle()
                step(v.tensor_tensor(gcol[:, 1:2], m[:, 4:5], gcol[:, 1:2], ALU.max))
                step(v.tensor_tensor(scb[:, l, :], r, scb[:, l, :], ALU.max))
                settle()
                step(v.tensor_scalar(modc[:, l, 1:2], modc[:, l, 1:2], 1.0, None, ALU.add))
                step(v.tensor_scalar(modc[:, l, 3:4], modc[:, l, 3:4], 1.0, None, ALU.add))
                step(v.scalar_tensor_tensor(modc[:, l, 4:5], gcol[:, 0:1], -1.0, gcol[:, 1:2], ALU.add, ALU.mult))
                chain(v.scalar_tensor_tensor(gar[:, l, :], gar[:, l, :], -1.0, scb[:, l, :], ALU.add, ALU.mult))
            v.tensor_copy(tiny[:, 45:46], tiny[:, 2:3]).then_inc(mod_ready, 1)

            def x_loaded(c):
                dve.wait_ge(ld_x[c], 16)

            n_small = 16 * 12
            dve.wait_ge(ld_small, n_small)
            dve.wait_ge(slope_e, 1)
            v.tensor_scalar(tc("usl"), tc("esl"), 1.0, None, ALU.add).then_inc(slope_u, 1)
            dve.wait_ge(slope_u, 1)
            chain(v.tensor_scalar(tc("dsl"), tc("usl"), -1.0, None, ALU.add))
            step(v.tensor_scalar(tc("zsl"), tc("dsl"), 0.0, tc("esl"), ALU.is_equal, ALU.mult))
            chain(v.tensor_scalar(tc("msl"), tc("dsl"), 1e-30, None, ALU.max))
            chain(v.reciprocal(tc("rsl"), tc("msl")))
            dve.wait_ge(slope_l, 1)
            chain(v.scalar_tensor_tensor(tc("sp"), tc("lsl"), tc("esl"), tc("rsl"), ALU.mult, ALU.mult))
            chain(v.tensor_tensor(tc("sp"), tc("sp"), tc("zsl"), ALU.add))
            chain(v.scalar_tensor_tensor(tc("sp"), tc("slope"), 0.0, tc("sp"), ALU.max, ALU.add))
            v.tensor_scalar(tc("nsd"), tc("sp"), -1.0, None, ALU.mult).then_inc(slope_ready, 1)
            v.tensor_reduce(dmax, dlog, AX_X, ALU.max, negate=True).then_inc(dl_max, 1)
            step(v.tensor_scalar(theta_n, theta_c, INV_2PI, None, ALU.mult))
            step(v.tensor_tensor(tc("ssb"), tc("bs"), tc("ss"), ALU.mult))
            step(v.memset(nsc, HALF_PI))
            dve.wait_ge(dl_exp, 1)
            chain(v.reciprocal(dsum, dsum))
            chain(v.tensor_scalar(dw, dexp, dsum, None, ALU.mult))
            chain(v.tensor_scalar(dw[:, 2:3], dw[:, 2:3], -1.0, None, ALU.mult))
            dve.wait_ge(ld_a, 48)
            for grp in range(2):
                cols = slice(grp * D, (grp + 1) * D)
                v.tensor_tensor(wfold[:, :, grp, :], wcv[:, :, cols],
                                win[:, cols].unsqueeze(1).broadcast_to([P, TAPS, D]), ALU.mult)\
                    .then_inc(fold_ready, 1)
            for k in range(TAPS):
                last = v.tensor_tensor(wfold[:, k, 2, :].rearrange("p (k h) -> p k h", h=H0),
                                       wcv[:, k, 2 * D:].unsqueeze(2).broadcast_to([P, K0, H0]),
                                       win[:, 2 * D:].unsqueeze(2).broadcast_to([P, K0, H0]), ALU.mult)
            last.then_inc(fold_ready, 1)
            norm(0, x_loaded)
            dve.wait_ge(ld_const, 32)
            chain(v.tensor_tensor(wrows, wrows, nscale[:, :, :].unsqueeze(3).broadcast_to([P, 2, M0, H0]), ALU.mult))
            for i in range(2):
                for m in range(M0):
                    last = v.tensor_tensor(bd[:, i, m], blk[:, :].rearrange("p (k j) -> p k j", j=H0),
                                           wrows[:, i, m].unsqueeze(1).broadcast_to([P, K0, H0]), ALU.mult)
            last.then_inc(bd_ready, 1)
            dve.wait_ge(ld_b, 64)
            v.tensor_tensor(wo0[:, :], wo0[:, :], gar[:, 0, :], ALU.mult).then_inc(wo_ready, 1)

            for c in range(NC):
                dve.wait_ge(zs_mm, c + 1)
                chain(v.tensor_scalar(pw[:, chunk(c)], ps[:, 2 + c % 2, :], tc("ss"), tc("ssb"), ALU.mult, ALU.add))
                v.tensor_scalar(pw[:, chunk(c)], pw[:, chunk(c)], 20.0, -20.0, ALU.min, ALU.max).then_inc(zs_lin, 1)
            dve.wait_ge(tw_ready, 1)
            for c in range(NC):
                dve.wait_ge(zs_exp, c + 1)
                v.tensor_tensor(pw[:, chunk(c)], pw[:, chunk(c)], tw[:, chunk(c)], ALU.mult).then_inc(pw_ready, 1)

            def front(c):
                b = c % 2
                dve.wait_ge(xv_ready, c + 1)
                x = xv[:, b, :]
                for m in range(M0):
                    step(v.tensor_scalar(phi[:, b, m, :], x, theta_c[:, m:m + 1], None, ALU.mult))
                    step(v.tensor_scalar(ang[:, b, m, :], x, theta_n[:, m:m + 1], ROUND, ALU.mult, ALU.add))
                step(v.tensor_scalar(tmp[:, 0, :], x, dw[:, 2:3], dw[:, 1:2], ALU.mult, ALU.add))
                settle()
                step(v.tensor_scalar(ang[:, b], ang[:, b], -ROUND, None, ALU.add))
                step(v.tensor_tensor(tmp[:, 0, :], tmp[:, 0, :], x, ALU.mult))
                settle()
                step(v.scalar_tensor_tensor(phi[:, b], ang[:, b], -TWO_PI_HI, phi[:, b], ALU.mult, ALU.add))
                if c == 0:
                    dve.wait_ge(pw_ready, NC)
                step(v.scalar_tensor_tensor(pw_poly[:, b, :], tmp[:, 0, :], dw[:, 0:1], pw[:, chunk(c)],
                                            ALU.add, ALU.mult))
                settle()
                chain(v.scalar_tensor_tensor(phi[:, b], ang[:, b], -TWO_PI_LO, phi[:, b], ALU.mult, ALU.add))
                v.tensor_scalar(phi[:, b], phi[:, b], PI, -PI, ALU.min, ALU.max).then_inc(phi_ready, 1)

            def back(c):
                b = c % 2
                dve.wait_ge(trig_ready, c + 1)
                w = pw_poly[:, b, :].unsqueeze(1).broadcast_to([P, M0, CW])
                step(v.tensor_tensor(ang[:, b], ang[:, b], w, ALU.mult))
                step(v.tensor_tensor(phi[:, b], phi[:, b], w, ALU.mult))
                prev = den[:, c * CW - 1:c * CW] if c else 0.0
                step(v.tensor_tensor_scan(den[:, chunk(c)], ones_b, pw[:, chunk(c)], prev, ALU.mult, ALU.add))
                settle()
                if c >= 2:
                    dve.wait_ge(y_mm, c - 1)
                for n in range(2 * M0):
                    src = (ang if n < M0 else phi)[:, b, n % M0, :]
                    prev = nums[:, 1 - b, n, CW - 1:CW] if c else 0.0
                    v.tensor_tensor_scan(nums[:, b, n, :], ones_b, src, prev, ALU.mult, ALU.add)\
                        .then_inc(num_ready, 1)

            def tail(c):
                chain(v.tensor_scalar(tmp[:, 1, :], den[:, chunk(c)], 1e-4, None, ALU.max))
                chain(v.scalar_tensor_tensor(tmp[:, 1, :], tmp[:, 1, :], EPS, tmp[:, 1, :], ALU.mult, ALU.mult))
                dve.wait_ge(ss_mm, c + 1)
                v.scalar_tensor_tensor(ssq, ps[:, c % 2, :], 1.0 / (2 * H0 * M0), tmp[:, 1, :], ALU.mult, ALU.add)\
                    .then_inc(q_ready, 1)
                dve.wait_ge(rt_ready, c + 1)
                chain(v.reciprocal(fac[:, 0, :], ssq))
                dve.wait_ge(gate_ready, c + 1)
                chain(v.tensor_tensor(fac[:, 1, :], fac[:, 0, :], gate[:, chunk(c)], ALU.mult))
                dve.wait_ge(y_mm, c + 1)
                v.tensor_tensor(yg[:, chunk(c)], ps[:, 6 + c % 2, :], fac[:, 1, :], ALU.mult).then_inc(yg_ready, 1)

            def residual(c, bank, mm_done, done):
                dve.wait_ge(mm_done, c + 1)
                v.tensor_tensor(xt[:, TPC * c:TPC * c + TPC, :].rearrange("p n d -> p (n d)"),
                                ps[:, bank, :],
                                xt[:, TPC * c:TPC * c + TPC, :].rearrange("p n d -> p (n d)"), ALU.add)\
                    .then_inc(done, 1)

            ones_b = ones_w[:, :].broadcast_to([P, CW])
            chain(v.memset(ones_w[:, :], 1.0))
            front(0)
            for c in range(NC):
                if c + 1 < NC:
                    front(c + 1)
                back(c)
                if c >= 1:
                    tail(c - 1)
                if c >= 2:
                    residual(c - 2, 2 + c % 2, o0_mm, x1_ready)
            tail(NC - 1)
            residual(NC - 2, 2 + NC % 2, o0_mm, x1_ready)
            residual(NC - 1, 2 + (NC - 1) % 2, o0_mm, x1_ready)

            norm(1, lambda c: dve.wait_ge(x1_ready, c + 1))
            def low_h(l):
                for c in range(NC):
                    dve.wait_ge(ln_h, (2 * l + 1) * NC + c + 1)
                    hs = (hs0, hs1)[l]
                    v.tensor_tensor(hs[:, 1, chunk(c)], hT[:, PAD + c * CW:PAD + (c + 1) * CW],
                                    hs[:, 0, chunk(c)].bitcast(F32), ALU.subtract).then_inc(hs_lo[l], 1)

            def low0(slot, n, count):
                dve.wait_ge(w0_hi, count)
                v.tensor_tensor(wsp0[:, slot, 1, piece(n)], wslot[:, slot, piece(n)],
                                wsp0[:, slot, 0, piece(n)].bitcast(F32), ALU.subtract).then_inc(w0_lo, 1)

            low_h(0)
            low0(0, 0, 1)
            low0(0, 1, 2)
            dve.wait_ge(sig_ready, 1)
            chain(v.tensor_tensor(sfc, scores, cbias[:, :].unsqueeze(1).broadcast_to([P, NT, E0]), ALU.add))
            NGT = NT * NG0
            grp = sfc.rearrange("p n (g e) -> p (n g) e", e=GE0)
            b1g = b1.rearrange("p n (g e) -> p (n g) e", e=GE0)
            b2g = b2.rearrange("p n (g e) -> p (n g) e", e=GE0)
            m1, cnt, m2, dup, gs, rank, gm = (gsm[:, i, :] for i in range(7))

            def per_group(x):
                return x.unsqueeze(2).broadcast_to([P, NGT, GE0])

            chain(v.tensor_reduce(m1, grp, AX_X, ALU.max))
            chain(v.tensor_tensor(b1g, grp, per_group(m1), ALU.is_equal))
            step(v.tensor_reduce(cnt, b1g, AX_X, ALU.add))
            chain(v.scalar_tensor_tensor(b2g, b1g, -BIG, grp, ALU.mult, ALU.add))
            step(v.tensor_reduce(m2, b2g, AX_X, ALU.max))
            chain(v.tensor_scalar(dup, cnt, 1.5, 1.0, ALU.is_ge, ALU.subtract))
            chain(v.scalar_tensor_tensor(dup, dup, BIG, m1, ALU.mult, ALU.add))
            chain(v.tensor_tensor(m2, m2, dup, ALU.max))
            chain(v.tensor_tensor(gs, m1, m2, ALU.add))
            gs_v = gs.rearrange("p (n g) -> p n g", g=NG0)
            mine = gs_v.unsqueeze(3).broadcast_to([P, NT, NG0, NG0])
            other = gs_v.unsqueeze(2).broadcast_to([P, NT, NG0, NG0])
            b1q = b1.rearrange("p n (g e) -> p n g e", e=NG0)
            b2q = b2.rearrange("p n (g e) -> p n g e", e=NG0)
            step(v.tensor_tensor(b1q, other, mine, ALU.is_gt))
            chain(v.tensor_tensor(b2q, other, mine, ALU.is_equal))
            chain(v.tensor_tensor(b2, b2, tri[:, :, :].rearrange("p a b -> p (a b)").unsqueeze(1)
                                  .broadcast_to([P, NT, E0]), ALU.mult))
            chain(v.tensor_tensor(b1, b1, b2, ALU.add))
            chain(v.tensor_reduce(rank, b1g, AX_X, ALU.add))
            chain(v.tensor_scalar(gm, rank, TOPG - 0.5, None, ALU.is_lt))
            chain(v.tensor_tensor(msk.rearrange("p n (g e) -> p (n g) e", e=GE0), grp, per_group(gm), ALU.mult))
            for t in range(NT):
                step(v.max(top8[:, t, :], msk[:, t, :]))
            settle()
            for t in range(NT):
                step(v.match_replace(b1[:, t, :], top8[:, t, :], msk[:, t, :], -BIG))
            settle()
            chain(v.scalar_tensor_tensor(b2, b1, -BIG / 2, scores, ALU.is_lt, ALU.mult))
            chain(v.tensor_reduce(wsum[:, 0, :], b2, AX_X, ALU.add))
            chain(v.tensor_scalar(wsum[:, 1, :], wsum[:, 0, :], 1e-20, None, ALU.add))
            chain(v.reciprocal(wsum[:, 2, :], wsum[:, 1, :]))
            chain(v.scalar_tensor_tensor(b1, b2, 2.5, wsum[:, 2, :].unsqueeze(2).broadcast_to([P, NT, E0]),
                                         ALU.mult, ALU.mult))
            chain(v.tensor_copy(comb3[:, :, 0, :], b1))
            chain(v.tensor_tensor(b2, b1, comb3[:, :, 0, :], ALU.subtract))
            chain(v.tensor_copy(comb3[:, :, 1, :], b2))
            v.tensor_tensor(comb3[:, :, 2, :], b2, comb3[:, :, 1, :], ALU.subtract).then_inc(comb_ready, 1)

            def prod_unit(n0, k):
                dve.wait_ge(moe_sq, n0 + (k + 1))
                dve.wait_ge(moe_cb, n0 + (k + 1))
                v.tensor_tensor(prod0[:, k % NBUF, :], ps[:, 2 + k % 2, :], sq0[:, k % 2, :], ALU.mult)\
                    .then_inc(moe_prod, 1)

            def low_unit(n0, k):
                dve.wait_ge(moe_hi, n0 + (k + 1))
                v.tensor_tensor(hid0[:, k % NBUF, 1, :], prod0[:, k % NBUF, :],
                                hid0[:, k % NBUF, 0, :].bitcast(F32), ALU.subtract).then_inc(moe_lo, 1)

            def units0(n0, nb, loads, last_iteration):
                for k in range(MU):
                    n = (n0, k + 1) if k + 1 < MU else (nb, 0)
                    if n[0] is not None:
                        prod_unit(*n)
                    low_unit(n0, k)
                    half, u = k // HALF, k % HALF
                    if u in (5, 7) and not (last_iteration and half):
                        m = (u - 5) // 2
                        low0((half + 1) % 2, m, loads * 2 + (2 * half + 3 + m))

            prod_unit(0, 0)
            with dve.Fori(0, N_IT0 - 1) as it:
                units0(it * MU, it * MU + MU, it * 2, False)
            units0((N_IT0 - 1) * MU, None, (N_IT0 - 1) * 2, True)
            for c in range(NC):
                residual(c, 2 + c % 2, y0_tr, x2_ready)

            norm(2, lambda c: dve.wait_ge(x2_ready, c + 1))
            dve.wait_ge(ld_c, 16 * 11)
            swap = wqb[:, 1, :].rearrange("p (n two) -> p n two", two=2)
            plain = wqb[:, 0, :].rearrange("p (n two) -> p n two", two=2)
            kv = wkvb[:, :].rearrange("p (n two kv) -> p n two kv", two=2, kv=2)
            wk0 = wkk[:, 0, :].rearrange("p (n two) -> p n two", two=2)
            wk1 = wkk[:, 1, :].rearrange("p (n two) -> p n two", two=2)
            wv = wkk[:, 2, :].rearrange("p (n two) -> p n two", two=2)
            v.tensor_copy(swap[:, :, 0], plain[:, :, 1])
            v.tensor_copy(swap[:, :, 1], plain[:, :, 0])
            v.tensor_copy(wk0, kv[:, :, :, 0])
            v.tensor_copy(wk1[:, :, 0], kv[:, :, 1, 0])
            v.tensor_copy(wk1[:, :, 1], kv[:, :, 0, 0])
            v.tensor_copy(wv, kv[:, :, :, 1]).then_inc(wk_ready, 1)
            step(v.tensor_tensor(wo1[:, :], wo1[:, :], gar[:, 1, :], ALU.mult))
            chain(v.tensor_tensor(bo1[:, :], bo1[:, :], gar[:, 1, :], ALU.mult))
            dve.wait_ge(ld_rope, 32)
            for c in range(NC):
                dve.wait_ge(qk_mm, c + 1)
                b = c % 2
                cs, sn = ropec[:, chunk(c)], ropes[:, chunk(c)]
                KR = G1 * HD
                v.tensor_tensor(ra[:, b, :], ps[:, 4, :], cs, ALU.mult).then_inc(rope_done, 1)
                v.tensor_tensor(rb[:, b, :], ps[:, 5, :], sn, ALU.mult).then_inc(rope_done, 1)
                v.tensor_tensor(rk[0:KR, b, :], ps[0:KR, 6, :], cs[0:KR, :], ALU.mult).then_inc(rope_done, 1)
                v.tensor_tensor(rl[0:KR, b, :], ps[0:KR, 7, :], sn[0:KR, :], ALU.mult).then_inc(rope_done, 1)
                dve.wait_ge(rope_done, 4 * c + 4)
                step(v.tensor_tensor(ra[:, b, :], ra[:, b, :], rb[:, b, :], ALU.add))
                step(v.tensor_tensor(rk[0:KR, b, :], rk[0:KR, b, :], rl[0:KR, b, :], ALU.add))
                settle()
                if c >= 2:
                    dve.wait_ge(st_qk[b], 32 * (c // 2))
                step(v.tensor_copy(q3[:, b, 0, :], ra[:, b, :]))
                step(v.tensor_copy(k3[0:KR, b, 0, :], rk[0:KR, b, :]))
                settle()
                step(v.tensor_tensor(ra[:, b, :], ra[:, b, :], q3[:, b, 0, :], ALU.subtract))
                step(v.tensor_tensor(rk[0:KR, b, :], rk[0:KR, b, :], k3[0:KR, b, 0, :], ALU.subtract))
                settle()
                step(v.tensor_copy(q3[:, b, 1, :], ra[:, b, :]))
                step(v.tensor_copy(k3[0:KR, b, 1, :], rk[0:KR, b, :]))
                settle()
                v.tensor_tensor(q3[:, b, 2, :], ra[:, b, :], q3[:, b, 1, :], ALU.subtract).then_inc(split_ready, 1)
                v.tensor_tensor(k3[0:KR, b, 2, :], rk[0:KR, b, :], k3[0:KR, b, 1, :], ALU.subtract)\
                    .then_inc(split_ready, 1)
            chain(v.tensor_tensor(xt[:, :, :], xt[:, :, :], bo1[:, :].unsqueeze(1).broadcast_to([P, NT, D]), ALU.add))

            def copy_out(n, steps):
                dve.wait_ge(pv_mm, steps)
                if n >= 2:
                    dve.wait_ge(slot_read, READ["out", n - 2])
                v.tensor_copy(oT[:, n % 2, :], ps[:, 6 + n % 2, :]).then_inc(o_copy, 1)

            slot_at = [0]

            def slot(what):
                m = slot_at[0]
                slot_at[0] += 1
                dve.wait_ge(slot_mm, m + 1)
                b = ps[:, m % 2, :]
                if what[0] == "scores":
                    _, n, t, u, i = what
                    w = (t % TPC + 1) * P if u == t // TPC else CW
                    v.tensor_reduce(mx[:, n % 2, i, t % TPC, u:u + 1], b[:, 0:w], AX_X, ALU.max)\
                        .then_inc(slot_read, 1)
                    if t % TPC == TPC - 1 and u == t // TPC and i == HPG - 1:
                        maxima(n, m + 1)
                elif what[0] == "maxima":
                    n = what[1]
                    if n >= 2:
                        dve.wait_ge(ld_nm[(n - 2) % G1], 32 * ((n - 2) // G1 + 1))
                    v.tensor_copy(nrow[0:2 * HPG * TPC, n % 2, :], b[0:2 * HPG * TPC, 0:P // 2].bitcast(BF16))\
                        .then_inc(slot_read, 1)
                elif what[0] == "out":
                    n = what[1]
                    c, g = n // G1, n % G1
                    o = b.rearrange("p (n h w) -> p n h w", h=HPG, w=32)
                    chain(v.reciprocal(rden, o[:, :, :, HD]))
                    for k in range(TPC):
                        last = v.tensor_tensor(otok[:, TPC * c + k, g * HPG * HD:(g + 1) * HPG * HD]
                                               .rearrange("p (h d) -> p h d", d=HD),
                                               o[:, k, :, 0:HD],
                                               rden[:, k, :].unsqueeze(2).broadcast_to([P, HPG, HD]), ALU.mult)
                        if k < TPC - 1:
                            step(last)
                    last.then_inc(slot_read, 1)
                elif what[0] == "turned":
                    v.tensor_copy(oTT[:, what[1] % 2, :], b).then_inc(slot_read, 1)
                else:
                    c = what[1]
                    x = xt[:, TPC * c:TPC * c + TPC, :].rearrange("p n d -> p (n d)")
                    v.tensor_tensor(x, b, x, ALU.add).then_inc(slot_read, 1)
                    dve.wait_ge(slot_read, m + 1)
                    for t in tiles(c):
                        step(v.bn_stats(stats[:, t, :], xt[:, t, :]))

            def maxima(n, count):
                c = n // G1
                dve.wait_ge(slot_read, count)
                chain(v.tensor_reduce(nmx, mx[:, n % 2, :, :, 0:c + 1].rearrange("p h t u -> p (h t) u"), AX_X,
                                      ALU.max, negate=True))
                chain(v.tensor_copy(nm2[:, 0, :], nmx))
                chain(v.tensor_tensor(nres, nmx, nm2[:, 0, :], ALU.subtract))
                v.tensor_copy(nm2[:, 1, :], nres).then_inc(nm_ready, 1)

            for what in SLOTS[0]:
                slot(what)
            for s, (n, j) in enumerate(STEPS):
                for what in SLOTS[s + 1]:
                    slot(what)
                if s >= 1 and STEPS[s - 1][0] != n:
                    copy_out(n - 1, s)
            copy_out(NITEM - 1, len(STEPS))
            for what in LAST_SLOTS:
                slot(what)

            norm(3, None, counted=True)
            low_h(1)
            dve.wait_ge(lg1_mm, 1)
            l4 = ps[:, 2, 0:NT * 2 * E1].rearrange("p (n e) -> p n e", e=E1)
            lgv = lg.rearrange("p n (a e) -> p (n a) e", a=2)
            chain(v.tensor_reduce(sm[:, 0, :], l4, AX_X, ALU.max))
            chain(v.tensor_tensor(lgv, l4, sm[:, 0, :].unsqueeze(2).broadcast_to([P, 2 * NT, E1]), ALU.subtract))
            v.tensor_scalar(lg[:, :, E1:2 * E1], lg[:, :, E1:2 * E1], 10.0, None, ALU.mult).then_inc(lg1_max, 1)
            dve.wait_ge(lg1_exp, 1)
            exv = ex.rearrange("p n (a e) -> p (n a) e", a=2)
            chain(v.tensor_reduce(sm[:, 1, :], exv, AX_X, ALU.add))
            chain(v.reciprocal(sm[:, 2, :], sm[:, 1, :]))
            chain(v.tensor_tensor(exv, exv, sm[:, 2, :].unsqueeze(2).broadcast_to([P, 2 * NT, E1]), ALU.mult))
            chain(v.tensor_tensor(cw, ex[:, :, 0:E1], ex[:, :, E1:2 * E1], ALU.mult))
            chain(v.tensor_reduce(sm[:, 3, 0:NT], cw, AX_X, ALU.add))
            chain(v.tensor_scalar(sm[:, 3, 0:NT], sm[:, 3, 0:NT], 1e-9, None, ALU.add))
            chain(v.reciprocal(sm[:, 4, 0:NT], sm[:, 3, 0:NT]))
            v.tensor_tensor(cw, cw, sm[:, 4, 0:NT].unsqueeze(2).broadcast_to([P, NT, E1]), ALU.mult)\
                .then_inc(cw_ready, 1)

            def low1(slot, n, count):
                dve.wait_ge(w1_hi, count)
                v.tensor_tensor(wsp1[:, slot, 1, piece(n)], wslot[:, slot, piece(n)],
                                wsp1[:, slot, 0, piece(n)].bitcast(F32), ALU.subtract).then_inc(w1_lo, 1)

            def prod_stream(slot, c, loaded):
                dve.wait_ge(ld_cwb[slot], loaded)
                v.tensor_tensor(hcf[:, c, :], hT[:, PAD + c * CW:PAD + (c + 1) * CW], cwb[:, slot, chunk(c)],
                                ALU.mult).then_inc(hc_prod, 1)

            def low_stream(slot, c, n):
                dve.wait_ge(hc_hi, n + 1)
                v.tensor_tensor(hcw[:, slot, 1, chunk(c)], hcf[:, c, :],
                                hcw[:, slot, 0, chunk(c)].bitcast(F32), ALU.subtract).then_inc(hc_lo, 1)

            def prod_hid(n0, k):
                dve.wait_ge(ffn_silu, n0 + (k + 1))
                dve.wait_ge(ffn_u, n0 + (k + 1))
                v.tensor_tensor(prod1[:, k % NBUF, :], ps[:, 2 + k % 2, :], silg[:, k % 2, :], ALU.mult)\
                    .then_inc(ffn_prod, 1)

            def low_hid(n0, k):
                dve.wait_ge(ffn_hi, n0 + (k + 1))
                v.tensor_tensor(hid1[:, k % NBUF, 1, :], prod1[:, k % NBUF, :],
                                hid1[:, k % NBUF, 0, :].bitcast(F32), ALU.subtract).then_inc(ffn_lo, 1)

            def units1(n0, nb, it1, last_iteration):
                for k in range(MU):
                    n = (n0, k + 1) if k + 1 < MU else (nb, 0)
                    if n[0] is not None:
                        prod_hid(*n)
                    low_hid(n0, k)
                    half, u = k // HALF, k % HALF
                    if last_iteration and half:
                        continue
                    to = (half + 1) % 2
                    if u in (6, 8, 10, 12):
                        c = (u - 6) // 2
                        low_stream(to, c, it1 * (2 * NC) + ((half + 1) * NC + c))
                    if u in (4, 6, 8, 10):
                        prod_stream(to, (u - 4) // 2, it1 * 16 + (16 if half == 0 else 32))
                    if u in (5, 7, 9):
                        m = (u - 5) // 2
                        low1(to, m, it1 * 6 + (3 * half + 4 + m))

            for n in range(3):
                low1(0, n, n + 1)
            prod_stream(0, 0, 16)
            for c in range(NC):
                if c + 1 < NC:
                    prod_stream(0, c + 1, 16)
                low_stream(0, c, c)
            prod_hid(0, 0)
            with dve.Fori(0, N_IT1 - 1) as it:
                units1(it * MU, it * MU + MU, it, False)
            units1((N_IT1 - 1) * MU, None, N_IT1 - 1, True)
            for c in range(NC):
                dve.wait_ge(y1_tr, c + 1)
                v.tensor_tensor(obuf[:, TPC * c:TPC * c + TPC, :].rearrange("p n d -> p (n d)"), ps[:, 2 + c % 2, :],
                                xt[:, TPC * c:TPC * c + TPC, :].rearrange("p n d -> p (n d)"), ALU.add)\
                    .then_inc(out_ready, 1)


_INS = ['L0_attn_x', 'L0_attn_W_in', 'L0_attn_w_conv', 'L0_attn_b_conv', 'L0_attn_theta', 'L0_attn_decay_slopes',
        'L0_attn_anchor_slopes', 'L0_attn_score_scale', 'L0_attn_deriv_logits', 'L0_attn_norm_scale', 'L0_attn_W_re',
        'L0_attn_W_im', 'L0_attn_W_out', 'L0_ffn_router_w', 'L0_ffn_correction_bias', 'L0_ffn_up_w',
        'L0_ffn_down_w', 'L0_ffn_shared_up_w', 'L0_ffn_shared_down_w', 'L0_c', 'L0_wmod', 'L1_attn_Wqa',
        'L1_attn_Wqb', 'L1_attn_Wkva', 'L1_attn_Wkvb', 'L1_attn_Wout', 'L1_attn_bout', 'L1_ffn_w_router',
        'L1_ffn_w_gating', 'L1_ffn_w_gate', 'L1_ffn_w_up', 'L1_ffn_w_down', 'L1_c', 'L1_wmod']


def _constants():
    import numpy as np

    f32 = np.float32

    def bf16_bits(x):
        return (x.astype(f32).view(np.uint32) >> 16).astype(np.uint16)

    ident = np.eye(P, dtype=f32)
    i = np.arange(P)
    later = (i[None, :] > i[:, None])
    pos = np.arange(T, dtype=f32)
    dist = np.broadcast_to(pos[None, :], (P, T)).copy()
    n_anchor = 4
    dist[0:(K0 - n_anchor) * H0] = (T - 1 - pos)[None, :]
    freq = (1.0 / np.float32(10000.0) ** (np.arange(0, HD, 2, dtype=f32) / f32(HD))).astype(f32)
    ang = (pos[:, None] * freq[None, :]).astype(f32).astype(np.float64)
    d = i % HD
    cos = np.cos(ang).astype(f32).T[d // 2]
    sin = np.sin(ang).astype(f32).T[d // 2] * np.where(d % 2 == 0, -1.0, 1.0).astype(f32)[:, None]
    sel = np.zeros((P, NPAIR, P), f32)
    for n in range(NPAIR):
        for j in range(2):
            for s in range(2):
                sel[s * E0 + 2 * n + j, n, j * I0:(j + 1) * I0] = 1.0
    tri = (np.arange(NG0)[None, :] < np.arange(NG0)[:, None]).astype(f32).ravel()
    return {
        "ident": ident, "identb": bf16_bits(ident),
        "maskqk": bf16_bits(np.where(later, -BIG, 0.0)), "maskkq": bf16_bits(np.where(later.T, -BIG, 0.0)),
        "blk": (i[:, None] // H0 == i[None, :] // H0).astype(f32), "dist": dist,
        "ropec": np.ascontiguousarray(cos, dtype=f32), "ropes": np.ascontiguousarray(sin, dtype=f32),
        "sel": bf16_bits(sel.reshape(P, NPAIR * P)), "tri": tri,
    }


def kernel(**inputs):
    import numpy as np
    import concourse.bacc as bacc
    from concourse.bass_utils import run_bass_kernel_spmd

    nc = bacc.Bacc("TRN2", target_bir_lowering=False, num_devices=1)
    arrays, aps = {}, {}
    every = {name: np.ascontiguousarray(inputs[name]) for name in _INS}
    every.update(_constants())
    for name, a in every.items():
        arrays[f"in_{name}"] = a
        aps[name] = nc.dram_tensor(f"in_{name}", a.shape, mybir.dt.from_np(a.dtype), kind="ExternalInput").ap()
        if a.dtype == np.uint16:
            aps[name] = aps[name].bitcast(BF16)
    out = nc.dram_tensor("out_0", (1, T, D), F32, kind="ExternalOutput").ap()
    adaln_two_layers(nc, aps, out)
    r = run_bass_kernel_spmd(nc, [arrays], core_ids=[0])
    return r.results[0]["out_0"]
```

```python
from contextlib import ExitStack

import concourse.bass as bass
from concourse import mybir

F32 = mybir.dt.float32
BF16 = mybir.dt.bfloat16
F32R = mybir.dt.float32r
ALU = mybir.AluOpType
ACT = mybir.ActivationFunctionType
AX_X = mybir.AxisListType.X

P = 128
T = 2048
D = 128
NT = T // P
CW = 512
NC = T // CW
TPC = CW // P
K0, H0, M0 = 32, 4, 4
TAPS = 4
E0, I0, ISH = 64, 64, 256
NG0, GE0, TOPG, TOPK = 8, 8, 4, 8
GP = 4
NPAIR = E0 // 2
NLOAD = NPAIR // GP
NSH = ISH // P
EH = E0 // 2
NCB = 3 * EH
LOOK = 3
NBUF = LOOK + 1
H1, G1, HD = 16, 4, 8
QL, KVL = 64, 32
HPG = H1 // G1
NSPLIT = 3
KROWS = NSPLIT * NSPLIT * HD
NITEM = NC * G1
E1, F1 = 8, 512
FT = F1 // P

TURN = 6.283185
HALF_PI = 1.5707963267948966
INV_2PI = 0.15915494309189535
ROUND = 12582912.0
BIG = 1.0e30
EPS = 1e-5


def attention_schedule():
    steps = [(n, j) for n in range(NITEM) for j in range(TPC * (n // G1 + 1))]
    first = {}
    for k, (n, _) in enumerate(steps):
        first.setdefault(n, k)
    scores = []
    for n in range(NITEM):
        c = n // G1
        for k, (t, u) in enumerate((t, u) for t in range(TPC * c, TPC * c + TPC) for u in range(c + 1)):
            fit = max(1, CW // ((t % TPC + 1) * P)) if u == t // TPC else 1
            scores += [("scores", n, t, u, i, fit) for i in range(0, HPG, fit)]
            if k == 0 and n > 0:
                scores.append(("maxima", n - 1))
    scores.append(("maxima", NITEM - 1))
    end = {n: max(k for k, x in enumerate(scores) if x[1] == n and x[0] == "scores") + 1 for n in range(NITEM)}
    slots = [scores[:end[1]]]
    done = end[1]
    late = {}
    for n in range(NITEM):
        s = first[n] + TPC * (n // G1 + 1)
        late.setdefault(s + 1, []).append(("out", n))
        if n % G1 == G1 - 1:
            late.setdefault(s + 2, []).append(("turned", n // G1))
            late.setdefault(s + 3, []).append(("product", n // G1))
    for k in range(len(steps)):
        rate = 0
        for n in range(2, NITEM):
            if first[n] - 3 >= k:
                want = min(end[n] + HPG + 1, len(scores)) - done
                rate = max(rate, -(-want // (first[n] - 2 - k)))
        here = scores[done:done + rate]
        done += len(here)
        slots.append(here + late.pop(k, []))
    assert done == len(scores)
    tail = [x for k in sorted(late) for x in late[k]]
    return steps, slots, tail


def adaln_two_layers(nc, A, out):
    ctx = ExitStack()
    with ctx:
        def sb(name, shape, dt=F32):
            return ctx.enter_context(nc.sbuf_tensor(name, shape, dt))

        def sem(name):
            return ctx.enter_context(nc.semaphore(name))

        xt = sb("xt", [P, NT, D])
        xn = sb("xn", [P, NT, D])
        PAD = TAPS - 1
        hT = sb("hT", [P, PAD + T])
        wslot = sb("wslot", [P, 2, 1536])
        ident = sb("ident", [P, P])
        identb = sb("identb", [P, P], BF16)
        maskqk = sb("maskqk", [P, P], BF16)
        maskkq = sb("maskkq", [P, P], BF16)
        blk = sb("blk", [P, P])
        stats = sb("stats", [P, NT, 6])
        mv = sb("mv", [P, NT, 2])
        sd = sb("sd", [P, NT])
        rstd = sb("rstd", [P, NT])
        modc = sb("modc", [P, 2, 8])
        gar = sb("gar", [P, 2, D])
        wo0 = sb("wo0", [P, D])
        wo1 = sb("wo1", [P, D])
        bo1 = sb("bo1", [P, D])
        wqa = sb("wqa", [P, QL])
        wkva = sb("wkva", [P, KVL])
        wqb = sb("wqb", [QL, 2, D])
        wkvb = sb("wkvb", [KVL, G1 * HD * 2])
        wkk = sb("wkk", [KVL, 3, G1 * HD])
        wr1 = sb("wr1", [P, 2 * E1])
        rwn = sb("rwn", [E0, D])
        rwT = sb("rwT", [P, E0])
        cbias = sb("cbias", [P, E0])
        tiny = sb("tiny", [P, 64])
        AW = 40800
        PW0 = 12288
        PW1 = 22528
        with nc.sbuf_tensor("arena_a", [P, PW1], F32) as arena_a:
            pass
        parts = sb("parts", [P, PW1], F32R)
        arena_b = sb("arena_b", [P, AW - PW1])
        ps = ctx.enter_context(nc.psum_tensor("ps", [P, 8, CW], F32))

        at = [0]

        def take(shape, dt=F32):
            n = 1
            for s in shape:
                n *= s
            words = n if dt != BF16 else (n + 1) // 2
            if at[0] < PW1 < at[0] + words:
                at[0] = PW1
            if at[0] >= PW1:
                v = arena_b[:, at[0] - PW1:at[0] - PW1 + words]
            else:
                v = (parts if dt == F32R else arena_a)[:, at[0]:at[0] + words]
            at[0] += words
            assert at[0] <= (PW1 if dt == F32R else AW), at[0]
            if dt == BF16:
                v = v.bitcast(dt)
            if len(shape) > 1:
                names = "abcd"[:len(shape)]
                v = v.rearrange("p (" + " ".join(names) + ") -> p " + " ".join(names),
                                **{names[i]: shape[i] for i in range(1, len(shape))})
            return v

        wmod = take([2, 6 * D])
        scb = take([2, P])
        win = take([2 * D + K0])
        wcv = take([TAPS, 2 * D + K0])
        wfold = take([TAPS, 3, P])
        wrows = take([2, M0, H0])
        bd = take([2, M0, K0, H0])
        tw = take([T])
        pw = take([T])
        gate = take([T])
        yg = xn[:, :, :].rearrange("p n d -> p (n d)")
        den = take([T])
        xv = take([2, CW])
        pw_poly = take([2, CW])
        tmp = take([3, CW])
        ssq = take([CW])
        phi = take([2, M0, CW])
        ang = take([2, M0, CW])
        nums = take([2, 2 * M0, CW])
        sqs = take([2 * M0, CW])
        fac = take([2, CW])
        at[0] = 0
        hid0 = take([NBUF, 2, CW], F32R)
        wsp0 = take([2, 2, 2 * GP * P], F32R)
        hs0 = take([2, T], F32R)
        assert at[0] == PW0
        scores = take([NT, E0])
        sfc = take([NT, E0])
        msk = take([NT, E0])
        b1 = take([NT, E0])
        b2 = take([NT, E0])
        comb3 = take([2, NT, 3, EH], BF16)
        combT = take([2, T], BF16)
        sel = take([NPAIR // 2, P], BF16)
        gsm = take([7, NT * NG0])
        top8 = take([NT, 8])
        wsum = take([3, NT])
        wsh = take([2, ISH])
        relu = take([NBUF, CW])
        hid = take([2, CW])
        yT = take([T])
        sq0 = take([NBUF, CW])
        prod0 = take([NBUF, CW])
        TAIL = AW - (G1 * T // 2 + NT * G1 * 32)
        assert at[0] <= TAIL, at[0]
        at[0] = TAIL
        kst = take([G1, T], BF16)
        vaug = take([NT, G1, 32])
        at[0] = 0
        qst = take([NC, H1, CW], BF16)
        mx = take([2, HPG, TPC, NC])
        nmx = take([HPG * TPC])
        nres = take([HPG * TPC])
        nm2 = take([2, HPG * TPC], BF16)
        nrow = take([2, P], BF16)
        rden = take([TPC, HPG])
        otok = xn
        ropec = take([T])
        ropes = take([T])
        assert at[0] <= PW1
        at[0] = PW1
        latq = take([2, CW])
        latk = take([2, CW])
        ra = take([2, CW])
        rb = take([2, CW])
        rk = take([2, CW])
        rl = take([2, CW])
        q3 = take([2, NSPLIT, CW], BF16)
        k3 = take([2, NSPLIT, CW], BF16)
        oT = take([2, CW])
        oTT = take([2, CW])
        probs = arena_b[:, 0:2 * HPG * CW].rearrange("p (a b c) -> p a b c", a=2, b=HPG)
        assert at[0] <= TAIL, at[0]
        at[0] = 0
        hs1 = take([2, T], F32R)
        hcw = take([2, 2, T], F32R)
        wsp1 = take([2, 2, 3 * F1], F32R)
        hid1 = take([NBUF, 2, CW], F32R)
        assert at[0] == PW1
        cwT = take([T])
        cwb = take([2, T])
        hcf = take([NC, CW])
        silg = take([2, CW])
        prod1 = take([NBUF, CW])
        lg = take([NT, 2 * E1])
        ex = take([NT, 2 * E1])
        cw = take([NT, E1])
        sm = take([6, NT * 2])
        y1T = take([T])
        obuf = take([NT, D])

        cw_dram = nc.dram_tensor("expert_weights", [E1, T], F32).ap()
        qs_dram = nc.dram_tensor("q_parts", [NSPLIT, P, T], BF16).ap()
        ks_dram = nc.dram_tensor("k_parts", [NSPLIT, G1 * HD, T], BF16).ap()

        ld_x = [sem(f"ld_x{c}") for c in range(NC)]
        ld_mod = sem("ld_mod")
        ld_a = sem("ld_a")
        ld_const = sem("ld_const")
        ld_small = sem("ld_small")
        ld_b = sem("ld_b")
        ld_c = sem("ld_c")
        ld_sel = sem("ld_sel")
        ld_rope = sem("ld_rope")
        ld_w0 = [sem(f"ld_w0_{i}") for i in range(2)]
        ld_w1 = [sem(f"ld_w1_{i}") for i in range(2)]
        st_qk = [sem(f"st_qk{b}") for b in range(2)]
        ld_stack = [sem(f"ld_stack{c}") for c in range(NC)]
        ld_nm = [sem(f"ld_nm{g}") for g in range(G1)]
        st_out = sem("st_out")
        s_v = sem("s_v")
        s_a = sem("s_a")
        pad_zero = sem("pad_zero")
        silu_c = sem("silu_c")
        scb_ready = sem("scb_ready")
        mod_mm = sem("mod_mm")
        mod_ready = sem("mod_ready")
        slope_in = sem("slope_in")
        slope_e = sem("slope_e")
        slope_u = sem("slope_u")
        slope_l = sem("slope_l")
        slope_ready = sem("slope_ready")
        fold_ready = sem("fold_ready")
        tw_ready = sem("tw_ready")
        dl_max = sem("dl_max")
        dl_exp = sem("dl_exp")
        bd_ready = sem("bd_ready")
        wo_ready = sem("wo_ready")
        ln_var = sem("ln_var")
        ln_sd = sem("ln_sd")
        ln_xn = sem("ln_xn")
        ln_tr = sem("ln_tr")
        ln_h = sem("ln_h")
        zs_mm = sem("zs_mm")
        zs_lin = sem("zs_lin")
        zs_exp = sem("zs_exp")
        pw_ready = sem("pw_ready")
        zv_mm = sem("zv_mm")
        zg_mm = sem("zg_mm")
        xv_ready = sem("xv_ready")
        xv_used = sem("xv_used")
        gate_ready = sem("gate_ready")
        phi_ready = sem("phi_ready")
        trig_ready = sem("trig_ready")
        num_ready = sem("num_ready")
        sq_ready = sem("sq_ready")
        y_mm = sem("y_mm")
        ss_mm = sem("ss_mm")
        q_ready = sem("q_ready")
        rt_ready = sem("rt_ready")
        yg_ready = sem("yg_ready")
        o0_mm = sem("o0_mm")
        x1_ready = sem("x1_ready")
        rw_tr = sem("rw_tr")
        rw_ready = sem("rw_ready")
        lg_mm = sem("lg_mm")
        sig_ready = sem("sig_ready")
        sh_up = sem("sh_up")
        sh_hid = sem("sh_hid")
        sh_down = sem("sh_down")
        comb_ready = sem("comb_ready")
        comb_tr = sem("comb_tr")
        comb_T = sem("comb_T")
        comb_TL = sem("comb_TL")
        moe_up = sem("moe_up")
        moe_cb = sem("moe_cb")
        moe_relu = sem("moe_relu")
        moe_sq = sem("moe_sq")
        moe_prod = sem("moe_prod")
        moe_hi = sem("moe_hi")
        moe_hi_own = sem("moe_hi_own")
        moe_lo = sem("moe_lo")
        w0_hi = sem("w0_hi")
        w0_lo = sem("w0_lo")
        hs_lo = [sem(f"hs{l}_lo") for l in range(2)]
        moe_down = sem("moe_down")
        y0_ready = sem("y0_ready")
        y0_tr = sem("y0_tr")
        x2_ready = sem("x2_ready")
        wk_ready = sem("wk_ready")
        kones = sem("kones")
        qzero = sem("qzero")
        vzero = sem("vzero")
        lat_mm = sem("lat_mm")
        lat_ready = sem("lat_ready")
        qk_mm = sem("qk_mm")
        v_mm = sem("v_mm")
        v_ready = sem("v_ready")
        rope_done = sem("rope_done")
        split_ready = sem("split_ready")
        x2b_ready = sem("x2b_ready")
        slot_mm = sem("slot_mm")
        slot_read = sem("slot_read")
        nm_ready = sem("nm_ready")
        p2_mm = sem("p2_mm")
        p2_exp = sem("p2_exp")
        pv_mm = sem("pv_mm")
        o_copy = sem("o_copy")
        lg1_mm = sem("lg1_mm")
        lg1_max = sem("lg1_max")
        lg1_exp = sem("lg1_exp")
        cw_ready = sem("cw_ready")
        cw_tr = sem("cw_tr")
        cwT_ready = sem("cwT_ready")
        st_cw = sem("st_cw")
        ld_cwb = [sem(f"ld_cwb{b}") for b in range(2)]
        hc_prod = sem("hc_prod")
        hc_hi = sem("hc_hi")
        hc_lo = sem("hc_lo")
        w1_hi = sem("w1_hi")
        w1_lo = sem("w1_lo")
        ffn_g = sem("ffn_g")
        ffn_u = sem("ffn_u")
        ffn_silu = sem("ffn_silu")
        ffn_prod = sem("ffn_prod")
        ffn_hi = sem("ffn_hi")
        ffn_lo = sem("ffn_lo")
        ffn_down = sem("ffn_down")
        y1_ready = sem("y1_ready")
        y1_tr = sem("y1_tr")
        out_ready = sem("out_ready")

        STEPS, SLOTS, LAST_SLOTS = attention_schedule()
        FIRST = [SLOTS[0][:len(SLOTS[0]) // 2], SLOTS[0][len(SLOTS[0]) // 2:]]
        NFIRST = len(SLOTS[0])

        def slot_bank(m):
            return m % 2 if m < NFIRST else (0, 1, 7)[m % 3]

        def slot_free(m):
            return m - 1 if m < NFIRST else max(NFIRST, m - 2)

        READ = {what: m + 1 for m, what in enumerate([x for part in SLOTS for x in part] + LAST_SLOTS)}
        HALF = GP * NC
        MU = 2 * GP * NC
        assert MU == 2 * FT * NC
        N_IT0 = NLOAD // 2
        N_IT1 = E1 // 2

        def up0(slot, part, pair):
            return wsp0[:, slot, part, pair * P:(pair + 1) * P]

        def down0(slot, part, pair):
            return wsp0[:, slot, part, GP * P + pair * P:GP * P + (pair + 1) * P]

        def w1(slot, part, which, ft):
            return wsp1[:, slot, part, which * F1 + ft * P:which * F1 + (ft + 1) * P]

        def comb_bank(c):
            return 2 - 2 * (c % 2)

        def piece(n):
            return slice(n * CW, (n + 1) * CW)

        def tiles(c):
            return range(TPC * c, TPC * c + TPC)

        def chunk(c):
            return slice(c * CW, (c + 1) * CW)

        col = {n: i for i, n in enumerate(
            "c0 c1 sc0 sc1 bval bgate bs ssb ss slope nabs esl usl dsl msl rsl lsl zsl sp nsd".split())}

        def tc(name, n=1, parts=P):
            return tiny[0:parts, col[name]:col[name] + n]

        theta_c = tiny[:, 20:24]
        theta_n = tiny[:, 24:28]
        dlog = tiny[:, 28:31]
        dmax = tiny[:, 31:32]
        dexp = tiny[:, 32:35]
        dsum = tiny[:, 35:36]
        dw = tiny[:, 36:39]
        nsc = tiny[:, 39:40]
        gcol = tiny[:, 40:44]
        nscale = sb("nscale", [P, 2, M0])
        ones_w = sb("ones_w", [P, 1])

        block = ctx.enter_context(nc.Block())

        def stack(queue, c):
            queue.wait_ge(st_qk[c % 2], 32 * (c // 2 + 1))
            for a in range(NSPLIT):
                for b in range(NSPLIT):
                    lo = (a * NSPLIT + b) * HD
                    queue.dma_start(kst[lo:lo + HD, :, chunk(c)],
                                    ks_dram[b, :, chunk(c)].rearrange("(g d) t -> d g t", d=HD))\
                        .then_inc(ld_stack[c], 16)
                    queue.dma_start(qst[lo:lo + HD, c, :, :],
                                    qs_dram[a, :, chunk(c)].rearrange("(h d) t -> d h t", d=HD))\
                        .then_inc(ld_stack[c], 16)

        @block.sync
        def _(sp):
            sp.dma_start(tc("c0"), A["L0_c"].rearrange("a (p b) -> (a p) b", b=1)).then_inc(ld_mod, 16)
            sp.dma_start(tc("c1"), A["L1_c"].rearrange("a (p b) -> (a p) b", b=1)).then_inc(ld_mod, 16)
            sp.dma_start(wmod[:, 0, :], A["L0_wmod"]).then_inc(ld_mod, 16)
            sp.dma_start(wmod[:, 1, :], A["L1_wmod"]).then_inc(ld_mod, 16)
            x_v = A["L0_attn_x"].rearrange("a (n p) d -> p (a n) d", p=P)
            for c in range(NC):
                sp.dma_start(xt[:, TPC * c:TPC * c + TPC, :], x_v[:, TPC * c:TPC * c + TPC, :])\
                  .then_inc(ld_x[c], 16)
            sp.dma_start(ident[:, :], A["ident"]).then_inc(ld_const, 16)
            sp.dma_start(blk[:, :], A["blk"]).then_inc(ld_const, 16)
            sp.dma_start(win, A["L0_attn_W_in"]).then_inc(ld_a, 16)
            sp.dma_start(wcv, A["L0_attn_w_conv"].rearrange("k a c -> a (k c)").broadcast_to(
                [P, TAPS * (2 * D + K0)]).rearrange("p (k c) -> p k c", k=TAPS))\
              .then_inc(ld_a, 16)
            sp.dma_start(tw, A["dist"]).then_inc(ld_a, 16)
            bc = A["L0_attn_b_conv"]
            sp.dma_start(tc("bval"), bc[0:D].rearrange("(p b) -> p b", b=1)).then_inc(ld_small, 16)
            sp.dma_start(tc("bgate"), bc[D:2 * D].rearrange("(p b) -> p b", b=1)).then_inc(ld_small, 16)

            def by_head(dst, lo, n, src):
                sp.dma_start(dst[H0 * lo:H0 * (lo + n), :],
                             src.rearrange("(k h b) -> k h b", h=1, b=1).broadcast_to([n, H0, 1]))\
                  .then_inc(ld_small, 16)

            by_head(tc("bs"), 0, K0, bc[2 * D:2 * D + K0])
            by_head(tc("ss"), 0, K0, A["L0_attn_score_scale"])
            na = A["L0_attn_anchor_slopes"].shape[0]
            by_head(tc("slope"), 0, K0 - na, A["L0_attn_decay_slopes"])
            by_head(tc("slope"), K0 - na, na, A["L0_attn_anchor_slopes"])
            sp.dma_start(theta_c, A["L0_attn_theta"].rearrange("a b k h m -> (a b k h) m")).then_inc(ld_small, 16)
            sp.dma_start(dlog, A["L0_attn_deriv_logits"].rearrange("(a n) -> a n", a=1).broadcast_to([P, 3]))\
              .then_inc(ld_small, 16)
            for i, name in enumerate(("L0_attn_W_re", "L0_attn_W_im")):
                w = A[name].rearrange("(h m) j -> h (m j)", m=M0)
                sp.dma_start(wrows[:, i].rearrange("p m j -> p (m j)"),
                             w.unsqueeze(0).broadcast_to([K0, H0, M0 * H0])).then_inc(ld_small, 16)
            for i in range(2):
                n_v = A["L0_attn_norm_scale"].rearrange("(i h m) -> i h m", i=2, m=M0)[i]
                sp.dma_start(nscale[:, i, :],
                             n_v.unsqueeze(0).broadcast_to([K0, H0, M0])).then_inc(ld_small, 16)
            sp.dma_start(wo0[:, :], A["L0_attn_W_out"]).then_inc(ld_b, 16)
            sp.dma_start(rwn[:, :], A["L0_ffn_router_w"]).then_inc(ld_b, 16)
            sp.dma_start(cbias[:, :], A["L0_ffn_correction_bias"].rearrange("(a n) -> a n", a=1).broadcast_to([P, E0]))\
              .then_inc(ld_b, 16)
            up_v = A["L0_ffn_up_w"].rearrange("e d f -> d e f")
            down_v = A["L0_ffn_down_w"].rearrange("(n two) f d -> (two f) n d", two=2)

            def load0(slot, n):
                sp.dma_start(wslot[:, slot, 0:GP * P].rearrange("p (e f) -> p e f", f=I0),
                             up_v[:, bass.ds(2 * GP * n, 2 * GP), :]).then_inc(ld_w0[slot], 16)
                sp.dma_start(wslot[:, slot, GP * P:2 * GP * P].rearrange("p (n d) -> p n d", d=D),
                             down_v[:, bass.ds(GP * n, GP), :]).then_inc(ld_w0[slot], 16)

            for slot in range(2):
                load0(slot, slot)
            for dst, name in ((wqa[:, :], "L1_attn_Wqa"), (wkva[:, :], "L1_attn_Wkva"),
                              (wqb[:, 0, :], "L1_attn_Wqb"), (wkvb[:, :], "L1_attn_Wkvb"),
                              (wo1[:, :], "L1_attn_Wout"), (wr1[:, 0:E1], "L1_ffn_w_router"),
                              (wr1[:, E1:2 * E1], "L1_ffn_w_gating"), (identb[:, :], "identb"),
                              (maskqk[:, :], "maskqk"), (maskkq[:, :], "maskkq")):
                sp.dma_start(dst, A[name]).then_inc(ld_c, 16)
            sp.dma_start(bo1[:, :], A["L1_attn_bout"].rearrange("(a n) -> a n", a=1).broadcast_to([P, D]))\
              .then_inc(ld_c, 16)
            sp.wait_ge(x1_ready, NC)
            sp.dma_start(wsh[:, 0, :], A["L0_ffn_shared_up_w"]).then_inc(ld_sel, 16)
            sp.dma_start(wsh[:, 1, :].rearrange("p (n d) -> p n d", d=D),
                         A["L0_ffn_shared_down_w"].rearrange("(n p) d -> p n d", p=P)).then_inc(ld_sel, 16)
            sp.dma_start(sel, A["sel"].rearrange("p (n f) -> p n f", f=P)).then_inc(ld_sel, 16)
            with sp.Fori(1, N_IT0) as it:
                for slot in range(2):
                    sp.wait_ge(w0_lo, it * 4 + (2 * slot - 2))
                    load0(slot, it * 2 + slot)

            w1_views = [A["L1_ffn_w_gate"], A["L1_ffn_w_up"],
                        A["L1_ffn_w_down"].rearrange("e (n p) d -> e p n d", p=P)]

            def load1(slot, e):
                for which in range(2):
                    sp.dma_start(wslot[:, slot, which * F1:(which + 1) * F1],
                                 w1_views[which][bass.ds(e, 1), :, :].rearrange("a p n -> (a p) n"))\
                      .then_inc(ld_w1[slot], 16)
                sp.dma_start(wslot[:, slot, 2 * F1:3 * F1].rearrange("p (n d) -> p n d", d=D),
                             w1_views[2][bass.ds(e, 1), :, :, :].rearrange("a p n d -> (a p) n d"))\
                  .then_inc(ld_w1[slot], 16)

            sp.wait_ge(moe_down, N_IT0 * MU)
            sp.dma_start(ropec, A["ropec"]).then_inc(ld_rope, 16)
            sp.dma_start(ropes, A["ropes"]).then_inc(ld_rope, 16)
            for slot in range(2):
                load1(slot, slot)
            sp.wait_ge(kones, 1)
            sp.wait_ge(qzero, 1)

            def store_parts(c):
                sp.wait_ge(split_ready, 2 * c + 2)
                sp.dma_start(qs_dram[:, :, chunk(c)].rearrange("s p t -> p s t"), q3[:, c % 2])\
                  .then_inc(st_qk[c % 2], 16)
                sp.dma_start(ks_dram[:, :, chunk(c)].rearrange("s p t -> p s t"),
                             k3[0:G1 * HD, c % 2]).then_inc(st_qk[c % 2], 16)

            def maxima_rows(n):
                c, g = n // G1, n % G1
                sp.wait_ge(slot_read, READ["maxima", n])
                for s in range(2):
                    sp.dma_start(qst[KROWS + s:KROWS + s + 1, c, HPG * g:HPG * g + HPG, :].rearrange("p h t -> p (h t)"),
                                 nrow[s * HPG * TPC:(s + 1) * HPG * TPC, n % 2, :]).then_inc(ld_nm[g], 16)

            for c in range(2):
                store_parts(c)
                stack(sp, c)
            store_parts(2)
            maxima_rows(0)
            store_parts(NC - 1)
            for n in range(1, NITEM):
                maxima_rows(n)
            sp.wait_ge(cwT_ready, 1)
            sp.dma_start(cw_dram, cwT[0:E1, :]).then_inc(st_cw, 16)
            sp.wait_ge(st_cw, 16)

            def load_cwb(slot, e):
                sp.dma_start(cwb[:, slot, :], cw_dram[bass.ds(e, 1), :].broadcast_to([P, T]))\
                  .then_inc(ld_cwb[slot], 16)

            load_cwb(1, 1)
            with sp.Fori(1, N_IT1) as it:
                for slot in range(2):
                    sp.wait_ge(w1_lo, it * 6 + (3 * slot - 3))
                    load1(slot, it * 2 + slot)
                    sp.wait_ge(hc_prod, it * (2 * NC) + (NC * slot - NC))
                    load_cwb(slot, it * 2 + slot)
            out_v = out.rearrange("a (n p) d -> p (a n) d", p=P)
            for c in range(NC):
                sp.wait_ge(out_ready, c + 1)
                sp.dma_start(out_v[:, TPC * c:TPC * c + TPC, :], obuf[:, TPC * c:TPC * c + TPC, :])\
                  .then_inc(st_out, 16)
            sp.wait_ge(st_out, 16 * NC)

        @block.gpsimd
        def _(pool):
            nc.gpsimd.memset(hT[:, 0:PAD], 0.0).then_inc(pad_zero, 1)
            pool.wait_ge(x1_ready, NC)
            nc.gpsimd.memset(kst[64:P, :, :], 1.0).then_inc(kones, 1)
            pool.wait_ge(kones, 1)
            nc.gpsimd.memset(vaug, 0.0).then_inc(vzero, 1)
            pool.wait_ge(vzero, 1)
            nc.gpsimd.memset(vaug[:, :, :, HD:HD + 1], 1.0).then_inc(vzero, 1)
            pool.wait_ge(vzero, 2)
            pool.wait_ge(x2_ready, NC)
            nc.gpsimd.memset(qst[64:P].rearrange("p c h t -> p (c h t)").bitcast(F32), 0.0).then_inc(qzero, 1)
            pool.wait_ge(qzero, 1)
            for c in range(2, NC):
                stack(pool, c)

        @block.tensor
        def _(pe):
            mm = nc.tensor.matmul

            def norm(i, after=lambda c: None):
                for c in range(NC):
                    pe.wait_ge(ln_xn, i * NC + c + 1)
                    if c == 0 and i == 0:
                        pe.wait_ge(ld_const, 32)
                    if c >= 2:
                        pe.wait_ge(ln_h, i * NC + c - 1)
                    for k, t in enumerate(tiles(c)):
                        last = nc.tensor.transpose(ps[:, c % 2, k * P:(k + 1) * P], xn[:, t, :], ident[:, :])
                    last.then_inc(ln_tr, 1)
                    after(c)

            pe.wait_ge(ld_mod, 64)
            pe.wait_ge(scb_ready, 2)
            for l in range(2):
                mm(ps[:, 2, l * P:(l + 1) * P], scb[:, l, :], wmod[:, l, 2 * D:3 * D], start=True, stop=True)
                for n, j in enumerate((0, 1, 3, 4, 5)):
                    last = mm(ps[:, 3, 8 * l + n:8 * l + n + 1], wmod[:, l, j * D:(j + 1) * D],
                              tc("sc0" if l == 0 else "sc1"), start=True, stop=True)
            last.then_inc(mod_mm, 1)

            norm(0)

            def project(bank, grp, c, done):
                for k in range(TAPS):
                    last = mm(ps[:, bank, :], wfold[:, k, grp, :], hT[:, c * CW + k:c * CW + k + CW],
                              start=(k == 0), stop=(k == TAPS - 1))
                last.then_inc(done, 1)

            pe.wait_ge(fold_ready, 3)
            pe.wait_ge(pad_zero, 1)
            pe.wait_ge(mod_ready, 1)

            def values0(c):
                if c >= 1:
                    pe.wait_ge(xv_ready, c)
                project(4, 0, c, zv_mm)

            def gates0(c):
                if c >= 1:
                    pe.wait_ge(gate_ready, c)
                project(5, 1, c, zg_mm)

            pe.wait_ge(ln_h, 1)
            values0(0)
            for c in range(NC):
                pe.wait_ge(ln_h, c + 1)
                if c >= 2:
                    pe.wait_ge(zs_lin, c - 1)
                project(2 + c % 2, 2, c, zs_mm)
            gates0(0)

            def mix(c):
                if c == 0:
                    pe.wait_ge(bd_ready, 1)
                if c >= 2:
                    pe.wait_ge(yg_ready, c - 1)
                for n in range(2 * M0):
                    pe.wait_ge(num_ready, 2 * M0 * c + n + 1)
                    last = mm(ps[:, 6 + c % 2, :], bd[:, n // M0, n % M0].rearrange("p k j -> p (k j)"),
                              nums[:, c % 2, n, :], start=(n == 0), stop=(n == 2 * M0 - 1))
                last.then_inc(y_mm, 1)
                for n in range(2 * M0):
                    if n % M0 == 0:
                        pe.wait_ge(sq_ready, 2 * c + n // M0 + 1)
                    last = mm(ps[:, c % 2, :], blk[:, :], sqs[:, n, :], start=(n == 0), stop=(n == 2 * M0 - 1))
                last.then_inc(ss_mm, 1)

            def out0(c):
                pe.wait_ge(yg_ready, c + 1)
                if c == 0:
                    pe.wait_ge(wo_ready, 1)
                pe.wait_ge(zs_lin, NC)
                if c >= 2:
                    pe.wait_ge(x1_ready, c - 1)
                for k, t in enumerate(tiles(c)):
                    last = mm(ps[:, 2 + c % 2, k * P:(k + 1) * P], yg[:, t * P:(t + 1) * P], wo0[:, :],
                              start=True, stop=True)
                last.then_inc(o0_mm, 1)

            pe.wait_ge(ld_b, 48)
            nc.tensor.transpose(ps[:, 7, 0:E0], rwn[:, :], ident[0:E0, 0:E0]).then_inc(rw_tr, 1)
            for c in range(NC):
                if c == 1:
                    pe.wait_ge(rw_ready, 1)
                if c + 1 < NC:
                    values0(c + 1)
                    gates0(c + 1)
                if c >= 2:
                    out0(c - 2)
                mix(c)
            out0(NC - 2)
            out0(NC - 1)

            def route0(c):
                pe.wait_ge(ln_h, 1 * NC + c + 1)
                for t in tiles(c):
                    last = mm(ps[:, 4 + t // 8, (t % 8) * E0:(t % 8 + 1) * E0],
                              hT[:, PAD + t * P:PAD + (t + 1) * P], rwT[:, :], start=True, stop=True)
                last.then_inc(lg_mm, 1)

            norm(1, lambda c: route0(c - 1) if c else None)
            route0(NC - 1)

            def rhs(c):
                return hT[:, PAD + c * CW:PAD + (c + 1) * CW]

            pe.wait_ge(ld_sel, 48)

            def shared_up(n):
                if n >= 2:
                    pe.wait_ge(sh_hid, n - 1)
                mm(ps[:, n % 2, :], wsh[:, 0, (n // NC) * P:(n // NC + 1) * P], rhs(n % NC),
                   start=True, stop=True).then_inc(sh_up, 1)

            def shared_down(n):
                pe.wait_ge(sh_hid, n + 1)
                if n == 0:
                    pe.wait_ge(sig_ready, 1)
                mm(ps[:, 4 + n % NC, :], wsh[:, 1, (n // NC) * P:(n // NC + 1) * P], hid[:, n % 2, :],
                   start=(n < NC), stop=False).then_inc(sh_down, 1)

            NSU = NSH * NC
            for n in range(NSU + 1):
                if n < NSU:
                    shared_up(n)
                if n >= 1:
                    shared_down(n - 1)

            pe.wait_ge(ld_c, 16 * 11)
            for c in range(NC):
                pe.wait_ge(comb_ready, 2)
                if c >= 2:
                    pe.wait_ge(comb_T, c - 1)
                    pe.wait_ge(comb_TL, c - 1)
                b = comb_bank(c)
                pc = ps[:, b:b + 2, :].bitcast(BF16)
                for k, t in enumerate(tiles(c)):
                    nc.tensor.transpose(pc[0:NCB, 0, k * P:(k + 1) * P],
                                        comb3[:, 0, t].rearrange("p s e -> p (s e)"), identb[:, :])
                    last = nc.tensor.transpose(pc[0:NCB, 1, k * P:(k + 1) * P],
                                               comb3[:, 1, t].rearrange("p s e -> p (s e)"), identb[:, :])
                last.then_inc(comb_tr, 1)
            pe.wait_ge(comb_T, NC)
            pe.wait_ge(comb_TL, NC)

            def three(bank, w, x, start, stop):
                mm(bank, w(0), x(0), start=start, stop=False)
                mm(bank, w(0), x(1), start=False, stop=False)
                return mm(bank, w(1), x(0), start=False, stop=stop)

            def look0(base, k, n0, loads):
                pair, c = k // NC, k % NC
                slot = (pair // GP) % 2
                if k % HALF == 0:
                    pe.wait_ge(w0_lo, loads)
                if n0 is not None:
                    pe.wait_ge(moe_relu, n0 + (k - 1))
                three(ps[:, k % 2, :], lambda i: up0(slot, i, pair % GP), lambda i: hs0[:, i, chunk(c)],
                      True, True).then_inc(moe_up, 1)
                if n0 is not None:
                    pe.wait_ge(moe_prod, n0 + (k - 1))
                w = sel[0:NCB, bass.ds(base + pair % GP, 1), :].rearrange("p a f -> p (a f)")
                mm(ps[:, 2 + k % 2, :], w, combT[0:NCB, slot, chunk(c)], start=True, stop=True).then_inc(moe_cb, 1)

            def sum0(n0, k, last_one):
                pair, c = k // NC, k % NC
                pe.wait_ge(moe_lo, n0 + (k + 1))
                three(ps[:, 4 + c, :], lambda i: down0((pair // GP) % 2, i, pair % GP),
                      lambda i: hid0[:, k % NBUF, i, :], False, last_one).then_inc(moe_down, 1)

            pe.wait_ge(hs_lo[0], NC)
            for k in range(LOOK):
                look0(0, k, 0 if k >= 2 else None, 2)
            with pe.Fori(0, N_IT0 - 1) as it:
                for k in range(MU):
                    if k + LOOK < MU:
                        look0(it * GP, k + LOOK, it * MU, it * 4 + 4)
                    else:
                        look0(it * GP + GP, k + LOOK - MU, it * MU + MU, it * 4 + 6)
                    sum0(it * MU, k, False)
            for k in range(MU):
                if k + LOOK < MU:
                    look0((N_IT0 - 1) * GP, k + LOOK, (N_IT0 - 1) * MU, N_IT0 * 4)
                sum0((N_IT0 - 1) * MU, k, k >= MU - NC)

            for c in range(NC):
                pe.wait_ge(y0_ready, c + 1)
                if c >= 2:
                    pe.wait_ge(x2_ready, c - 1)
                for k in range(TPC):
                    last = nc.tensor.transpose(ps[:, 2 + c % 2, k * P:(k + 1) * P],
                                               yT[:, c * CW + k * P:c * CW + (k + 1) * P], ident[:, :])
                last.then_inc(y0_tr, 1)

            def latents(c):
                if c == 0:
                    pe.wait_ge(wk_ready, 1)
                    pe.wait_ge(x2_ready, NC)
                pe.wait_ge(ln_h, 2 * NC + c + 1)
                if c >= 1:
                    pe.wait_ge(v_ready, c)
                mm(ps[0:QL, 2, :], wqa[:, :], rhs(c), start=True, stop=True)
                mm(ps[0:KVL, 3, :], wkva[:, :], rhs(c), start=True, stop=True).then_inc(lat_mm, 1)

            def heads(c):
                pe.wait_ge(lat_ready, 2 * c + 2)
                if c >= 1:
                    pe.wait_ge(rope_done, 4 * c - 2)
                mm(ps[:, 4, :], wqb[:, 0, :], latq[0:QL, c % 2, :], start=True, stop=True)
                mm(ps[:, 5, :], wqb[:, 1, :], latq[0:QL, c % 2, :], start=True, stop=True)
                if c >= 1:
                    pe.wait_ge(rope_done, 4 * c)
                mm(ps[0:32, 6, :], wkk[:, 0, :], latk[0:KVL, c % 2, :], start=True, stop=True)
                mm(ps[0:32, 7, :], wkk[:, 1, :], latk[0:KVL, c % 2, :], start=True, stop=True).then_inc(qk_mm, 1)
                for k in range(TPC):
                    last = mm(ps[:, 2, k * 32:(k + 1) * 32], latk[0:KVL, c % 2, k * P:(k + 1) * P], wkk[:, 2, :],
                              start=True, stop=True)
                last.then_inc(v_mm, 1)

            def after_turn(c):
                if c >= 2:
                    heads(c - 2)
                if c >= 1:
                    latents(c - 1)

            slot_at = [0]

            def slot(what):
                m = slot_at[0]
                slot_at[0] += 1
                if m >= 2:
                    pe.wait_ge(slot_read, slot_free(m))
                b = ps[:, slot_bank(m), :]
                if what[0] == "scores":
                    _, n, t, u, i, fit = what
                    g = n % G1
                    if n % G1 == 0:
                        pe.wait_ge(ld_stack[n // G1], 32 * NSPLIT * NSPLIT)
                    diag = u == t // TPC
                    full = t % TPC * P if diag else CW
                    for h in range(fit):
                        q = qst[:, t // TPC, HPG * g + i + h, t % TPC * P:(t % TPC + 1) * P]
                        at_ = h * (full + P)
                        if full:
                            last = mm(b[:, at_:at_ + full], q, kst[:, g, u * CW:u * CW + full], start=True, stop=True)
                        if diag:
                            at_ += full
                            mm(b[:, at_:at_ + P], q, kst[:, g, t * P:(t + 1) * P], start=True, stop=False)
                            last = mm(b[:, at_:at_ + P], identb[:, :], maskqk[:, :], start=False, stop=True)
                elif what[0] == "maxima":
                    pe.wait_ge(nm_ready, what[1] + 1)
                    last = nc.tensor.transpose(b[0:2 * HPG * TPC, 0:P // 2].bitcast(BF16),
                                               nm2.rearrange("p s n -> p (s n)"), identb[:, :])
                elif what[0] == "out":
                    n = what[1]
                    pe.wait_ge(o_copy, n + 1)
                    for k in range(TPC):
                        last = nc.tensor.transpose(b[:, k * P:(k + 1) * P], oT[:, n % 2, k * P:(k + 1) * P],
                                                   ident[:, :])
                elif what[0] == "turned":
                    c = what[1]
                    pe.wait_ge(slot_read, READ["out", c * G1 + G1 - 1])
                    for k, t in enumerate(tiles(c)):
                        last = nc.tensor.transpose(b[:, k * P:(k + 1) * P], otok[:, t, :], ident[:, :])
                else:
                    c = what[1]
                    pe.wait_ge(slot_read, READ["turned", c])
                    for k in range(TPC):
                        last = mm(b[:, k * P:(k + 1) * P], oTT[:, c % 2, k * P:(k + 1) * P], wo1[:, :],
                                  start=True, stop=True)
                last.then_inc(slot_mm, 1)

            def sum_scores(s, pair):
                n, j = STEPS[s]
                c, g = n // G1, n % G1
                off = max(0, j - TPC * c) * P
                if s >= 1:
                    pe.wait_ge(p2_exp, 2 * s + pair - 1)
                for i in (2 * pair, 2 * pair + 1):
                    k = kst[:, g, j * P:(j + 1) * P]
                    q = qst[:, c, HPG * g + i, :]
                    full = off
                    if j >= TPC * c:
                        full = off + P
                        mm(ps[:, 2 + i, off:full], k, q[:, off:full], start=True, stop=False)
                        last = mm(ps[:, 2 + i, off:full], identb[:, :], maskkq[:, :], start=False, stop=True)
                    if full < CW:
                        last = mm(ps[:, 2 + i, full:CW], k, q[:, full:CW], start=True, stop=True)
                last.then_inc(p2_mm, 1)

            def values(s):
                n, j = STEPS[s]
                c, g = n // G1, n % G1
                off = max(0, j - TPC * c) * P
                pe.wait_ge(p2_exp, 2 * s + 2)
                if j == 0 and n >= 1:
                    pe.wait_ge(o_copy, n)
                for i in range(HPG):
                    last = mm(ps[32 * i:32 * i + 32, 6, off:CW], vaug[:, j, g, :],
                              probs[:, s % 2, i, off:CW], start=(j == 0), stop=(j == TPC * c + TPC - 1),
                              tile_position=(0, 32 * i))
                last.then_inc(pv_mm, 1)

            norm(2, after_turn)
            heads(NC - 2)
            pe.wait_ge(ln_h, 3 * NC)
            for what in FIRST[0]:
                slot(what)
            latents(NC - 1)
            heads(NC - 1)
            for what in FIRST[1]:
                slot(what)
            pe.wait_ge(v_ready, NC)
            pe.wait_ge(rope_done, 4 * NC)
            for s, (n, j) in enumerate(STEPS):
                beside = SLOTS[s + 1]
                if j == 0:
                    pe.wait_ge(ld_nm[n % G1], 32 * (n // G1 + 1))
                cuts = [0, (len(beside) + 3) // 4, (len(beside) + 1) // 2, len(beside)]
                sum_scores(s, 0)
                for what in beside[cuts[0]:cuts[1]]:
                    slot(what)
                sum_scores(s, 1)
                for what in beside[cuts[1]:cuts[2]]:
                    slot(what)
                if s >= 1:
                    values(s - 1)
                for what in beside[cuts[2]:cuts[3]]:
                    slot(what)
            values(len(STEPS) - 1)
            for what in LAST_SLOTS:
                slot(what)

            def route1(c):
                pe.wait_ge(ln_h, 3 * NC + c + 1)
                for t in tiles(c):
                    last = mm(ps[:, 2, t * 2 * E1:(t + 1) * 2 * E1], hT[:, PAD + t * P:PAD + (t + 1) * P], wr1[:, :],
                              start=True, stop=True)
                last.then_inc(lg1_mm, 1)

            norm(3, lambda c: route1(c - 1) if c else None)
            route1(NC - 1)
            pe.wait_ge(cw_ready, 1)
            for c in range(NC):
                for k, t in enumerate(tiles(c)):
                    last = mm(ps[:, 4 + c, k * P:(k + 1) * P], cw[:, t, 0:1].broadcast_to([P, P]), ident[:, :],
                              is_transpose=True, start=True, stop=True)
                last.then_inc(cw_tr, 1)
            for t in range(NT):
                last = nc.tensor.transpose(ps[0:E1, t // TPC, t % TPC * P:(t % TPC + 1) * P], cw[:, t, :],
                                           ident[:, :])
            last.then_inc(cw_tr, 1)
            pe.wait_ge(cwT_ready, 1)

            def look1(k, n0, w_parts, h_parts):
                e, ft, c = k // (FT * NC), k // NC % FT, k % NC
                if k % HALF == 0:
                    pe.wait_ge(w1_lo, w_parts)
                    pe.wait_ge(hc_lo, h_parts)
                if n0 is not None:
                    pe.wait_ge(ffn_prod, n0 + (k - 1))
                three(ps[:, k % 2, :], lambda i: w1(e, i, 0, ft), lambda i: hs1[:, i, chunk(c)],
                      True, True).then_inc(ffn_g, 1)
                three(ps[:, 2 + k % 2, :], lambda i: w1(e, i, 1, ft), lambda i: hcw[:, e, i, chunk(c)],
                      True, True).then_inc(ffn_u, 1)

            def sum1(n0, k, first, last_one):
                e, ft, c = k // (FT * NC), k // NC % FT, k % NC
                pe.wait_ge(ffn_lo, n0 + (k + 1))
                three(ps[:, 4 + c, :], lambda i: w1(e, i, 2, ft), lambda i: hid1[:, k % NBUF, i, :],
                      first, last_one).then_inc(ffn_down, 1)

            pe.wait_ge(hs_lo[1], NC)
            for k in range(LOOK):
                look1(k, 0 if k >= 2 else None, 3, NC)
            for k in range(MU):
                if k + LOOK < MU:
                    look1(k + LOOK, 0, 6, 2 * NC)
                else:
                    look1(k + LOOK - MU, MU, 9, 3 * NC)
                sum1(0, k, k < NC, False)
            with pe.Fori(1, N_IT1 - 1) as it:
                for k in range(MU):
                    if k + LOOK < MU:
                        look1(k + LOOK, it * MU, it * 6 + 6, it * (2 * NC) + 2 * NC)
                    else:
                        look1(k + LOOK - MU, it * MU + MU, it * 6 + 9, it * (2 * NC) + 3 * NC)
                    sum1(it * MU, k, False, False)
            for k in range(MU):
                if k + LOOK < MU:
                    look1(k + LOOK, (N_IT1 - 1) * MU, 6 * N_IT1, 2 * NC * N_IT1)
                sum1((N_IT1 - 1) * MU, k, False, k >= MU - NC)
            for c in range(NC):
                pe.wait_ge(y1_ready, c + 1)
                if c >= 2:
                    pe.wait_ge(out_ready, c - 1)
                for k in range(TPC):
                    last = nc.tensor.transpose(ps[:, 2 + c % 2, k * P:(k + 1) * P],
                                               y1T[:, c * CW + k * P:c * CW + (k + 1) * P], ident[:, :])
                last.then_inc(y1_tr, 1)

        @block.scalar
        def _(act):
            a = nc.scalar.activation
            own = [0]

            def step(ins):
                own[0] += 1
                ins.then_inc(s_a, 1)

            def settle():
                act.wait_ge(s_a, own[0])

            def norm(i, after=lambda c: None):
                l, j = i // 2, 2 * (i % 2)
                if i == 0:
                    act.wait_ge(mod_ready, 1)
                for c in range(NC + 1):
                    if c < NC:
                        act.wait_ge(ln_var, i * NC + c + 1)
                        a(sd[:, TPC * c:TPC * c + TPC], mv[:, TPC * c:TPC * c + TPC, 1], ACT.Sqrt).then_inc(ln_sd, 1)
                    if c >= 1:
                        b = c - 1
                        act.wait_ge(ln_tr, i * NC + b + 1)
                        if i % 2:
                            a((hs0, hs1)[l][:, 0, chunk(b)], ps[:, b % 2, :], ACT.Identity,
                              bias=modc[:, l, j:j + 1], scale=modc[:, l, j + 1:j + 2])
                        a(hT[:, PAD + b * CW:PAD + (b + 1) * CW], ps[:, b % 2, :], ACT.Identity,
                          bias=modc[:, l, j:j + 1], scale=modc[:, l, j + 1:j + 2]).then_inc(ln_h, 1)
                        after(b)

            act.wait_ge(ld_mod, 64)
            a(tiny[:, 2:4], tiny[:, 0:2], ACT.Silu).then_inc(silu_c, 1)
            norm(0)

            def values(c):
                act.wait_ge(zv_mm, c + 1)
                if c >= 2:
                    act.wait_ge(xv_used, c - 1)
                a(xv[:, c % 2, :], ps[:, 4, :], ACT.Identity, bias=tc("bval")).then_inc(xv_ready, 1)

            def gates(c):
                act.wait_ge(zg_mm, c + 1)
                a(gate[:, chunk(c)], ps[:, 5, :], ACT.Silu, bias=tc("bgate")).then_inc(gate_ready, 1)

            def trig(c):
                act.wait_ge(phi_ready, c + 1)
                step(a(ang[:, c % 2], phi[:, c % 2], ACT.Abs))
                settle()
                step(a(ang[:, c % 2], ang[:, c % 2], ACT.Sin, bias=nsc, scale=-TURN))
                step(a(phi[:, c % 2], phi[:, c % 2], ACT.Sin, scale=-TURN))
                settle()
                nc.scalar.activation(nsc_copy, nsc, ACT.Copy).then_inc(trig_ready, 1)

            def squares(c):
                if c >= 1:
                    act.wait_ge(ss_mm, c)
                for i in range(2):
                    act.wait_ge(num_ready, 2 * M0 * c + M0 * (i + 1))
                    a(sqs[:, M0 * i:M0 * i + M0], nums[:, c % 2, M0 * i:M0 * i + M0], ACT.Square)\
                        .then_inc(sq_ready, 1)

            def root(c):
                act.wait_ge(q_ready, c + 1)
                a(ssq, ssq, ACT.Sqrt).then_inc(rt_ready, 1)

            nsc_copy = tiny[:, 44:45]
            act.wait_ge(ld_small, 16 * 12)
            values(0)
            n_small = 16 * 12
            act.wait_ge(ld_small, n_small)
            step(a(tc("nabs"), tc("slope"), ACT.Abs))
            settle()
            a(tc("esl"), tc("nabs"), ACT.Exp, scale=-1.0).then_inc(slope_e, 1)
            act.wait_ge(slope_u, 1)
            a(tc("lsl"), tc("usl"), ACT.Ln).then_inc(slope_l, 1)
            act.wait_ge(dl_max, 1)
            a(dexp, dlog, ACT.Exp, bias=dmax, scale=1.0, accum_out=dsum).then_inc(dl_exp, 1)
            act.wait_ge(slope_ready, 1)
            act.wait_ge(ld_a, 48)
            a(tw, tw, ACT.Exp, scale=tc("nsd")).then_inc(tw_ready, 1)
            trig(0)
            for c in range(NC):
                act.wait_ge(zs_lin, c + 1)
                a(pw[:, chunk(c)], pw[:, chunk(c)], ACT.Exp).then_inc(zs_exp, 1)
            gates(0)
            act.wait_ge(rw_tr, 1)
            a(rwT[:, :], ps[:, 7, 0:E0], ACT.Copy).then_inc(rw_ready, 1)
            for c in range(NC):
                if c + 1 < NC:
                    values(c + 1)
                    gates(c + 1)
                squares(c)
                if c >= 1:
                    root(c - 1)
                if c + 1 < NC:
                    trig(c + 1)
            root(NC - 1)

            norm(1)

            def high0(slot, n, loaded):
                if loaded is not None:
                    act.wait_ge(ld_w0[slot], loaded)
                a(wsp0[:, slot, 0, piece(n)], wslot[:, slot, piece(n)], ACT.Copy).then_inc(w0_hi, 1)

            high0(0, 0, 32)
            high0(0, 1, None)
            act.wait_ge(lg_mm, NC)
            a(scores.rearrange("p (b n) e -> p b (n e)", b=2), ps[:, 4:6, :], ACT.Sigmoid).then_inc(sig_ready, 1)
            for n in range(NSH * NC):
                act.wait_ge(sh_up, n + 1)
                if n >= 2:
                    act.wait_ge(sh_down, n - 1)
                step(a(relu[:, n % 2, :], ps[:, n % 2, :], ACT.Relu))
                settle()
                a(hid[:, n % 2, :], relu[:, n % 2, :], ACT.Square).then_inc(sh_hid, 1)
            for c in range(NC):
                act.wait_ge(comb_tr, c + 1)
                a(combT[0:NCB, 1, chunk(c)], ps[0:NCB, comb_bank(c) + 1, 0:CW // 2].bitcast(BF16), ACT.Copy)\
                    .then_inc(comb_TL, 1)

            def relu0(n0, k):
                act.wait_ge(moe_up, n0 + (k + 1))
                a(relu[:, k % NBUF, :], ps[:, k % 2, :], ACT.Relu).then_inc(moe_relu, 1)

            def sq_unit(n0, k):
                act.wait_ge(moe_relu, n0 + (k + 1))
                a(sq0[:, k % NBUF, :], relu[:, k % NBUF, :], ACT.Square).then_inc(moe_sq, 1)

            def high_unit(n0, k):
                act.wait_ge(moe_prod, n0 + (k + 1))
                a(hid0[:, k % NBUF, 0, :], prod0[:, k % NBUF, :], ACT.Copy).then_inc(moe_hi, 1)

            def units0(n0, nb, loads, last_iteration):
                for k in range(MU):
                    two, one = ((n0, k + i) if k + i < MU else (nb, k + i - MU) for i in (2, 1))
                    if one[0] is not None:
                        sq_unit(*one)
                    if k % 4 != 3:
                        high_unit(n0, k)
                    if two[0] is not None:
                        relu0(*two)
                    half, u = k // HALF, k % HALF
                    if u in (4, 6) and not (last_iteration and half):
                        high0((half + 1) % 2, u // 2 - 2, loads * 16 + (32 if half == 0 else 64))

            relu0(0, 0)
            relu0(0, 1)
            sq_unit(0, 0)
            with act.Fori(0, N_IT0 - 1) as it:
                units0(it * MU, it * MU + MU, it * 2, False)
            units0((N_IT0 - 1) * MU, None, (N_IT0 - 1) * 2, True)
            for c in range(NC):
                if c == 0:
                    act.wait_ge(moe_down, N_IT0 * MU)
                a(yT[:, chunk(c)], ps[:, 4 + c, :], ACT.Copy, scale=modc[:, 0, 4:5]).then_inc(y0_ready, 1)

            def lat_copies(c):
                act.wait_ge(lat_mm, c + 1)
                a(latq[0:QL, c % 2, :], ps[0:QL, 2, :], ACT.Copy).then_inc(lat_ready, 1)
                a(latk[0:KVL, c % 2, :], ps[0:KVL, 3, :], ACT.Copy).then_inc(lat_ready, 1)

            def v_copy(c):
                act.wait_ge(v_mm, c + 1)
                act.wait_ge(vzero, 2)
                a(vaug[:, TPC * c:TPC * c + TPC, :, 0:HD],
                  ps[:, 2, 0:TPC * 32].rearrange("p (n g d) -> p n g d", g=G1, d=HD), ACT.Copy)\
                    .then_inc(v_ready, 1)

            def after_chunk(c):
                if c >= 2:
                    v_copy(c - 2)
                if c >= 1:
                    lat_copies(c - 1)

            norm(2, after_chunk)
            v_copy(NC - 2)
            lat_copies(NC - 1)
            v_copy(NC - 1)

            scale = float(HD) ** -0.5
            for s, (n, j) in enumerate(STEPS):
                off = max(0, j - TPC * (n // G1)) * P
                for pair in range(2):
                    act.wait_ge(p2_mm, 2 * s + pair + 1)
                    if s >= 2:
                        act.wait_ge(pv_mm, s - 1)
                    a(probs[:, s % 2, 2 * pair:2 * pair + 2, off:CW],
                      ps[:, 2 + 2 * pair:4 + 2 * pair, off:CW], ACT.Exp, scale=scale).then_inc(p2_exp, 1)

            norm(3)
            def high1(slot, n, loaded):
                if loaded is not None:
                    act.wait_ge(ld_w1[slot], loaded)
                a(wsp1[:, slot, 0, piece(n)], wslot[:, slot, piece(n)], ACT.Copy).then_inc(w1_hi, 1)

            for n in range(3):
                high1(0, n, 48)
            act.wait_ge(lg1_max, 1)
            a(ex, lg, ACT.Exp).then_inc(lg1_exp, 1)

            def high_stream(slot, c, n):
                act.wait_ge(hc_prod, n + 1)
                a(hcw[:, slot, 0, chunk(c)], hcf[:, c, :], ACT.Copy).then_inc(hc_hi, 1)

            def silu1(n0, k):
                act.wait_ge(ffn_g, n0 + (k + 1))
                a(silg[:, k % 2, :], ps[:, k % 2, :], ACT.Silu).then_inc(ffn_silu, 1)

            def high_hid(n0, k):
                act.wait_ge(ffn_prod, n0 + (k + 1))
                a(hid1[:, k % NBUF, 0, :], prod1[:, k % NBUF, :], ACT.Copy).then_inc(ffn_hi, 1)

            def units1(n0, nb, it2, last_iteration):
                for k in range(MU):
                    n = (n0, k + 1) if k + 1 < MU else (nb, 0)
                    if n[0] is not None:
                        silu1(*n)
                    high_hid(n0, k)
                    half, u = k // HALF, k % HALF
                    if last_iteration and half:
                        continue
                    if u in (4, 6, 8):
                        high1((half + 1) % 2, u // 2 - 2, it2 * 24 + (48 if half == 0 else 96))
                    if u in (5, 7, 9, 11):
                        c = (u - 5) // 2
                        high_stream((half + 1) % 2, c, it2 * NC + ((half + 1) * NC + c))

            for c in range(NC):
                high_stream(0, c, c)
            act.wait_ge(cw_tr, NC + 1)
            a(cwT[0:E1, :].rearrange("p (c t) -> p c t", c=NC), ps[0:E1, 0:4, :], ACT.Copy).then_inc(cwT_ready, 1)
            silu1(0, 0)
            with act.Fori(0, N_IT1 - 1) as it:
                units1(it * MU, it * MU + MU, it * 2, False)
            units1((N_IT1 - 1) * MU, None, (N_IT1 - 1) * 2, True)
            for c in range(NC):
                if c == 0:
                    act.wait_ge(ffn_down, N_IT1 * MU)
                a(y1T[:, chunk(c)], ps[:, 4 + c, :], ACT.Copy, scale=modc[:, 1, 4:5]).then_inc(y1_ready, 1)

        @block.vector
        def _(dve):
            v = nc.vector
            own = [0]

            def step(ins):
                own[0] += 1
                ins.then_inc(s_v, 1)

            def settle():
                dve.wait_ge(s_v, own[0])

            def chain(ins):
                step(ins)
                settle()

            def norm(i, ready, counted=False):
                for c in range(NC + 1):
                    if c < NC:
                        if not counted:
                            ready(c)
                            for t in tiles(c):
                                step(v.bn_stats(stats[:, t, :], xt[:, t, :]))
                        settle()
                        for t in tiles(c):
                            step(v.bn_aggr(mv[:, t, :], stats[:, t, :]))
                        settle()
                        m = mv[:, TPC * c:TPC * c + TPC, 1]
                        v.tensor_scalar(m, m, EPS, None, ALU.add).then_inc(ln_var, 1)
                    if c >= 1:
                        b = c - 1
                        ts = slice(TPC * b, TPC * b + TPC)
                        dve.wait_ge(ln_sd, i * NC + b + 1)
                        chain(v.reciprocal(rstd[:, ts], sd[:, ts]))
                        for t in tiles(b):
                            last = v.tensor_scalar(xn[:, t, :], xt[:, t, :], mv[:, t, 0:1], rstd[:, t:t + 1],
                                                   ALU.subtract, ALU.mult)
                        last.then_inc(ln_xn, 1)

            dve.wait_ge(silu_c, 1)
            for l in range(2):
                v.tensor_copy(scb[:, l, :], tiny[:, 2 + l:3 + l].broadcast_to([P, P])).then_inc(scb_ready, 1)
            dve.wait_ge(mod_mm, 1)
            for l in range(2):
                m = ps[:, 3, 8 * l:8 * l + 5]
                step(v.tensor_copy(modc[:, l, 0:5], m))
                step(v.tensor_scalar(gcol[:, 0:1], m[:, 4:5], 0.0, 2.0, ALU.is_ge, ALU.mult))
                step(v.tensor_scalar(gcol[:, 1:2], m[:, 4:5], -1.0, 0.25, ALU.mult, ALU.max))
                r = ps[:, 2, l * P:(l + 1) * P]
                step(v.tensor_scalar(gar[:, l, :], r, 0.0, 2.0, ALU.is_ge, ALU.mult))
                step(v.tensor_scalar(scb[:, l, :], r, -1.0, 0.25, ALU.mult, ALU.max))
                settle()
                step(v.tensor_tensor(gcol[:, 1:2], m[:, 4:5], gcol[:, 1:2], ALU.max))
                step(v.tensor_tensor(scb[:, l, :], r, scb[:, l, :], ALU.max))
                settle()
                step(v.tensor_scalar(modc[:, l, 1:2], modc[:, l, 1:2], 1.0, None, ALU.add))
                step(v.tensor_scalar(modc[:, l, 3:4], modc[:, l, 3:4], 1.0, None, ALU.add))
                step(v.scalar_tensor_tensor(modc[:, l, 4:5], gcol[:, 0:1], -1.0, gcol[:, 1:2], ALU.add, ALU.mult))
                chain(v.scalar_tensor_tensor(gar[:, l, :], gar[:, l, :], -1.0, scb[:, l, :], ALU.add, ALU.mult))
            v.tensor_copy(tiny[:, 45:46], tiny[:, 2:3]).then_inc(mod_ready, 1)

            def x_loaded(c):
                dve.wait_ge(ld_x[c], 16)

            n_small = 16 * 12
            dve.wait_ge(ld_a, 48)
            for grp in range(2):
                cols = slice(grp * D, (grp + 1) * D)
                v.tensor_tensor(wfold[:, :, grp, :], wcv[:, :, cols],
                                win[:, cols].unsqueeze(1).broadcast_to([P, TAPS, D]), ALU.mult)\
                    .then_inc(fold_ready, 1)
            for k in range(TAPS):
                last = v.tensor_tensor(wfold[:, k, 2, :].rearrange("p (k h) -> p k h", h=H0),
                                       wcv[:, k, 2 * D:].unsqueeze(2).broadcast_to([P, K0, H0]),
                                       win[:, 2 * D:].unsqueeze(2).broadcast_to([P, K0, H0]), ALU.mult)
            last.then_inc(fold_ready, 1)
            norm(0, x_loaded)
            dve.wait_ge(ld_small, n_small)
            step(v.tensor_scalar(theta_n, theta_c, INV_2PI, None, ALU.mult))
            step(v.tensor_tensor(tc("ssb"), tc("bs"), tc("ss"), ALU.mult))
            chain(v.memset(nsc, HALF_PI))
            def front(c):
                b = c % 2
                dve.wait_ge(xv_ready, c + 1)
                for m in range(M0):
                    step(v.tensor_scalar(phi[:, b, m, :], xv[:, b, :], theta_n[:, m:m + 1], None, ALU.mult))
                settle()
                chain(v.tensor_scalar(ang[:, b], phi[:, b], ROUND, -ROUND, ALU.add, ALU.add))
                v.tensor_tensor(phi[:, b], ang[:, b], phi[:, b], ALU.subtract).then_inc(phi_ready, 1)

            def weights(c):
                b = c % 2
                x = xv[:, b, :]
                if c == 0:
                    dve.wait_ge(pw_ready, NC)
                step(v.tensor_scalar(tmp[:, 0, :], x, dw[:, 2:3], dw[:, 1:2], ALU.mult, ALU.add))
                prev = den[:, c * CW - 1:c * CW] if c else 0.0
                step(v.tensor_tensor_scan(den[:, chunk(c)], ones_b, pw[:, chunk(c)], prev, ALU.mult, ALU.add))
                settle()
                chain(v.tensor_tensor(tmp[:, 0, :], tmp[:, 0, :], x, ALU.mult))
                chain(v.scalar_tensor_tensor(pw_poly[:, b, :], tmp[:, 0, :], dw[:, 0:1], pw[:, chunk(c)],
                                             ALU.add, ALU.mult))
                v.tensor_copy(tiny[:, 46:47], tiny[:, 45:46]).then_inc(xv_used, 1)

            def back(c):
                b = c % 2
                dve.wait_ge(trig_ready, c + 1)
                w = pw_poly[:, b, :].unsqueeze(1).broadcast_to([P, M0, CW])
                step(v.tensor_tensor(ang[:, b], ang[:, b], w, ALU.mult))
                step(v.tensor_tensor(phi[:, b], phi[:, b], w, ALU.mult))
                settle()
                if c >= 2:
                    dve.wait_ge(y_mm, c - 1)
                for n in range(2 * M0):
                    src = (ang if n < M0 else phi)[:, b, n % M0, :]
                    prev = nums[:, 1 - b, n, CW - 1:CW] if c else 0.0
                    v.tensor_tensor_scan(nums[:, b, n, :], ones_b, src, prev, ALU.mult, ALU.add)\
                        .then_inc(num_ready, 1)

            def mean_square(c):
                chain(v.tensor_scalar(tmp[:, 1, :], den[:, chunk(c)], 1e-4, None, ALU.max))
                chain(v.scalar_tensor_tensor(tmp[:, 1, :], tmp[:, 1, :], EPS, tmp[:, 1, :], ALU.mult, ALU.mult))
                dve.wait_ge(ss_mm, c + 1)
                v.scalar_tensor_tensor(ssq, ps[:, c % 2, :], 1.0 / (2 * H0 * M0), tmp[:, 1, :], ALU.mult, ALU.add)\
                    .then_inc(q_ready, 1)

            def gated(c):
                dve.wait_ge(rt_ready, c + 1)
                chain(v.reciprocal(fac[:, 0, :], ssq))
                dve.wait_ge(gate_ready, c + 1)
                chain(v.tensor_tensor(fac[:, 1, :], fac[:, 0, :], gate[:, chunk(c)], ALU.mult))
                dve.wait_ge(y_mm, c + 1)
                v.tensor_tensor(yg[:, chunk(c)], ps[:, 6 + c % 2, :], fac[:, 1, :], ALU.mult).then_inc(yg_ready, 1)

            def residual(c, bank, mm_done, done):
                dve.wait_ge(mm_done, c + 1)
                v.tensor_tensor(xt[:, TPC * c:TPC * c + TPC, :].rearrange("p n d -> p (n d)"),
                                ps[:, bank, :],
                                xt[:, TPC * c:TPC * c + TPC, :].rearrange("p n d -> p (n d)"), ALU.add)\
                    .then_inc(done, 1)

            ones_b = ones_w[:, :].broadcast_to([P, CW])
            chain(v.memset(ones_w[:, :], 1.0))
            front(0)
            dve.wait_ge(slope_e, 1)
            v.tensor_scalar(tc("usl"), tc("esl"), 1.0, None, ALU.add).then_inc(slope_u, 1)
            dve.wait_ge(slope_u, 1)
            chain(v.tensor_scalar(tc("dsl"), tc("usl"), -1.0, None, ALU.add))
            step(v.tensor_scalar(tc("zsl"), tc("dsl"), 0.0, tc("esl"), ALU.is_equal, ALU.mult))
            chain(v.tensor_scalar(tc("msl"), tc("dsl"), 1e-30, None, ALU.max))
            chain(v.reciprocal(tc("rsl"), tc("msl")))
            dve.wait_ge(slope_l, 1)
            chain(v.scalar_tensor_tensor(tc("sp"), tc("lsl"), tc("esl"), tc("rsl"), ALU.mult, ALU.mult))
            chain(v.tensor_tensor(tc("sp"), tc("sp"), tc("zsl"), ALU.add))
            chain(v.scalar_tensor_tensor(tc("sp"), tc("slope"), 0.0, tc("sp"), ALU.max, ALU.add))
            v.tensor_scalar(tc("nsd"), tc("sp"), -1.0, None, ALU.mult).then_inc(slope_ready, 1)
            v.tensor_reduce(dmax, dlog, AX_X, ALU.max, negate=True).then_inc(dl_max, 1)
            dve.wait_ge(dl_exp, 1)
            chain(v.reciprocal(dsum, dsum))
            chain(v.tensor_scalar(dw, dexp, dsum, None, ALU.mult))
            chain(v.tensor_scalar(dw[:, 2:3], dw[:, 2:3], -1.0, None, ALU.mult))
            dve.wait_ge(ld_const, 32)
            chain(v.tensor_tensor(wrows, wrows, nscale[:, :, :].unsqueeze(3).broadcast_to([P, 2, M0, H0]), ALU.mult))
            for i in range(2):
                for m in range(M0):
                    last = v.tensor_tensor(bd[:, i, m], blk[:, :].rearrange("p (k j) -> p k j", j=H0),
                                           wrows[:, i, m].unsqueeze(1).broadcast_to([P, K0, H0]), ALU.mult)
            last.then_inc(bd_ready, 1)
            dve.wait_ge(ld_b, 48)
            v.tensor_tensor(wo0[:, :], wo0[:, :], gar[:, 0, :], ALU.mult).then_inc(wo_ready, 1)

            for c in range(NC):
                dve.wait_ge(zs_mm, c + 1)
                chain(v.tensor_scalar(pw[:, chunk(c)], ps[:, 2 + c % 2, :], tc("ss"), tc("ssb"), ALU.mult, ALU.add))
                v.tensor_scalar(pw[:, chunk(c)], pw[:, chunk(c)], 20.0, -20.0, ALU.min, ALU.max).then_inc(zs_lin, 1)
            dve.wait_ge(tw_ready, 1)
            for c in range(NC):
                dve.wait_ge(zs_exp, c + 1)
                v.tensor_tensor(pw[:, chunk(c)], pw[:, chunk(c)], tw[:, chunk(c)], ALU.mult).then_inc(pw_ready, 1)
            weights(0)
            for c in range(NC):
                back(c)
                if c >= 1:
                    mean_square(c - 1)
                if c + 1 < NC:
                    front(c + 1)
                    weights(c + 1)
                if c >= 1:
                    gated(c - 1)
                if c >= 3:
                    residual(c - 3, 2 + (c - 3) % 2, o0_mm, x1_ready)
            mean_square(NC - 1)
            residual(NC - 3, 2 + (NC - 3) % 2, o0_mm, x1_ready)
            gated(NC - 1)

            def added0(c):
                if c >= NC - 2:
                    residual(c, 2 + c % 2, o0_mm, x1_ready)
                dve.wait_ge(x1_ready, c + 1)

            norm(1, added0)
            def low_h(l):
                for c in range(NC):
                    dve.wait_ge(ln_h, (2 * l + 1) * NC + c + 1)
                    hs = (hs0, hs1)[l]
                    v.tensor_tensor(hs[:, 1, chunk(c)], hT[:, PAD + c * CW:PAD + (c + 1) * CW],
                                    hs[:, 0, chunk(c)].bitcast(F32), ALU.subtract).then_inc(hs_lo[l], 1)

            def low0(slot, n, count):
                dve.wait_ge(w0_hi, count)
                v.tensor_tensor(wsp0[:, slot, 1, piece(n)], wslot[:, slot, piece(n)],
                                wsp0[:, slot, 0, piece(n)].bitcast(F32), ALU.subtract).then_inc(w0_lo, 1)

            low_h(0)
            low0(0, 0, 1)
            low0(0, 1, 2)
            dve.wait_ge(sig_ready, 1)
            chain(v.tensor_tensor(sfc, scores, cbias[:, :].unsqueeze(1).broadcast_to([P, NT, E0]), ALU.add))
            NGT = NT * NG0
            grp = sfc.rearrange("p n (g e) -> p (n g) e", e=GE0)
            b1g = b1.rearrange("p n (g e) -> p (n g) e", e=GE0)
            b2g = b2.rearrange("p n (g e) -> p (n g) e", e=GE0)
            m1, t1, u1, m2, gs, left, gm = (gsm[:, i, :] for i in range(7))

            def per_group(x):
                return x.unsqueeze(2).broadcast_to([P, NGT, GE0])

            def quarter(x, k, n):
                return x.rearrange("p n e -> p (n e)")[:, k * 2 * NGT:k * 2 * NGT + n * NGT]\
                    .rearrange("p (g e) -> p g e", e=n)

            hi4, lo4 = quarter(b1, 0, 4), quarter(b1, 2, 4)
            hi2, t2, u2, lo2 = (quarter(b2, k, 2) for k in range(4))
            step(v.tensor_tensor(hi4, grp[:, :, 0:4], grp[:, :, 4:8], ALU.max))
            step(v.tensor_tensor(lo4, grp[:, :, 0:4], grp[:, :, 4:8], ALU.min))
            settle()
            step(v.tensor_tensor(hi2, hi4[:, :, 0:2], hi4[:, :, 2:4], ALU.max))
            step(v.tensor_tensor(t2, hi4[:, :, 0:2], hi4[:, :, 2:4], ALU.min))
            step(v.tensor_tensor(u2, lo4[:, :, 0:2], lo4[:, :, 2:4], ALU.max))
            settle()
            step(v.tensor_tensor(lo2, t2, u2, ALU.max))
            step(v.tensor_tensor(m1, hi2[:, :, 0], hi2[:, :, 1], ALU.max))
            step(v.tensor_tensor(t1, hi2[:, :, 0], hi2[:, :, 1], ALU.min))
            settle()
            chain(v.tensor_tensor(u1, lo2[:, :, 0], lo2[:, :, 1], ALU.max))
            chain(v.tensor_tensor(m2, t1, u1, ALU.max))
            chain(v.tensor_tensor(gs, m1, m2, ALU.add))
            gs_v = gs.rearrange("p (n g) -> p n g", g=NG0)
            left_v = left.rearrange("p (n g) -> p n g", g=NG0)
            for t in range(NT):
                step(v.max(top8[:, t, :], gs_v[:, t, :]))
            settle()
            chain(v.memset(top8[:, :, TOPG:], BIG))
            for t in range(NT):
                step(v.match_replace(left_v[:, t, :], top8[:, t, :], gs_v[:, t, :], -BIG))
            settle()
            chain(v.tensor_scalar(gm, left, -BIG / 2, None, ALU.is_lt))
            chain(v.tensor_tensor(msk.rearrange("p n (g e) -> p (n g) e", e=GE0), grp, per_group(gm), ALU.mult))
            for t in range(NT):
                step(v.max(top8[:, t, :], msk[:, t, :]))
            settle()
            for t in range(NT):
                step(v.match_replace(b1[:, t, :], top8[:, t, :], msk[:, t, :], -BIG))
            settle()
            chain(v.scalar_tensor_tensor(b2, b1, -BIG / 2, scores, ALU.is_lt, ALU.mult))
            chain(v.tensor_reduce(wsum[:, 0, :], b2, AX_X, ALU.add))
            chain(v.tensor_scalar(wsum[:, 1, :], wsum[:, 0, :], 1e-20, None, ALU.add))
            chain(v.reciprocal(wsum[:, 2, :], wsum[:, 1, :]))
            chain(v.scalar_tensor_tensor(b1, b2, 2.5, wsum[:, 2, :].unsqueeze(2).broadcast_to([P, NT, E0]),
                                         ALU.mult, ALU.mult))
            def by_load(x, q):
                return x.rearrange("p n (i q x) -> p q n i x", q=2, x=2 * GP)[:, q]

            def part(q, m):
                return comb3[:, q, :, m, :].rearrange("p n (i x) -> p n i x", x=2 * GP)

            for q in range(2):
                step(v.tensor_copy(part(q, 0), by_load(b1, q)))
            settle()
            for q in range(2):
                step(v.tensor_tensor(by_load(b2, q), by_load(b1, q), part(q, 0), ALU.subtract))
            settle()
            for q in range(2):
                step(v.tensor_copy(part(q, 1), by_load(b2, q)))
            settle()
            for q in range(2):
                v.tensor_tensor(part(q, 2), by_load(b2, q), part(q, 1), ALU.subtract).then_inc(comb_ready, 1)

            dve.wait_ge(ld_c, 16 * 11)
            swap = wqb[:, 1, :].rearrange("p (n two) -> p n two", two=2)
            plain = wqb[:, 0, :].rearrange("p (n two) -> p n two", two=2)
            kv = wkvb[:, :].rearrange("p (n two kv) -> p n two kv", two=2, kv=2)
            wk0 = wkk[:, 0, :].rearrange("p (n two) -> p n two", two=2)
            wk1 = wkk[:, 1, :].rearrange("p (n two) -> p n two", two=2)
            wv = wkk[:, 2, :].rearrange("p (n two) -> p n two", two=2)
            v.tensor_copy(swap[:, :, 0], plain[:, :, 1])
            v.tensor_copy(swap[:, :, 1], plain[:, :, 0])
            v.tensor_copy(wk0, kv[:, :, :, 0])
            v.tensor_copy(wk1[:, :, 0], kv[:, :, 1, 0])
            v.tensor_copy(wk1[:, :, 1], kv[:, :, 0, 0])
            v.tensor_copy(wv, kv[:, :, :, 1]).then_inc(wk_ready, 1)
            step(v.tensor_tensor(wo1[:, :], wo1[:, :], gar[:, 1, :], ALU.mult))
            chain(v.tensor_tensor(bo1[:, :], bo1[:, :], gar[:, 1, :], ALU.mult))

            def prod_unit(n0, k):
                dve.wait_ge(moe_sq, n0 + (k + 1))
                dve.wait_ge(moe_cb, n0 + (k + 1))
                v.tensor_tensor(prod0[:, k % NBUF, :], ps[:, 2 + k % 2, :], sq0[:, k % NBUF, :], ALU.mult)\
                    .then_inc(moe_prod, 1)

            def low_unit(n0, h0, k):
                if k % 4 == 3:
                    dve.wait_ge(moe_prod, n0 + (k + 1))
                    v.tensor_copy(hid0[:, k % NBUF, 0, :], prod0[:, k % NBUF, :]).then_inc(moe_hi_own, 1)
                    dve.wait_ge(moe_hi_own, h0 + (k // 4 + 1))
                else:
                    dve.wait_ge(moe_hi, h0 * 3 + (k + 1 - (k + 1) // 4))
                v.tensor_tensor(hid0[:, k % NBUF, 1, :], prod0[:, k % NBUF, :],
                                hid0[:, k % NBUF, 0, :].bitcast(F32), ALU.subtract).then_inc(moe_lo, 1)

            def units0(n0, nb, h0, loads, last_iteration):
                for k in range(MU):
                    n = (n0, k + 1) if k + 1 < MU else (nb, 0)
                    if n[0] is not None:
                        prod_unit(*n)
                    low_unit(n0, h0, k)
                    half, u = k // HALF, k % HALF
                    if u in (5, 7) and not (last_iteration and half):
                        m = (u - 5) // 2
                        low0((half + 1) % 2, m, loads * 2 + (2 * half + 3 + m))

            for c in range(NC):
                dve.wait_ge(comb_tr, c + 1)
                v.tensor_copy(combT[0:NCB, 0, chunk(c)], ps[0:NCB, comb_bank(c), 0:CW // 2].bitcast(BF16))\
                    .then_inc(comb_T, 1)
            prod_unit(0, 0)
            with dve.Fori(0, N_IT0 - 1) as it:
                units0(it * MU, it * MU + MU, it * (MU // 4), it * 2, False)
            units0((N_IT0 - 1) * MU, None, (N_IT0 - 1) * MU // 4, (N_IT0 - 1) * 2, True)

            def added1(c):
                residual(c, 2 + c % 2, y0_tr, x2_ready)
                dve.wait_ge(x2_ready, c + 1)

            norm(2, added1)
            dve.wait_ge(ln_xn, 3 * NC)
            chain(v.tensor_tensor(xt[:, :, :], xt[:, :, :], bo1[:, :].unsqueeze(1).broadcast_to([P, NT, D]), ALU.add))
            dve.wait_ge(ld_rope, 32)

            def rope_and_split(c):
                dve.wait_ge(qk_mm, c + 1)
                b = c % 2
                cs, sn = ropec[:, chunk(c)], ropes[:, chunk(c)]
                KR = G1 * HD
                v.tensor_tensor(ra[:, b, :], ps[:, 4, :], cs, ALU.mult).then_inc(rope_done, 1)
                v.tensor_tensor(rb[:, b, :], ps[:, 5, :], sn, ALU.mult).then_inc(rope_done, 1)
                v.tensor_tensor(rk[0:KR, b, :], ps[0:KR, 6, :], cs[0:KR, :], ALU.mult).then_inc(rope_done, 1)
                v.tensor_tensor(rl[0:KR, b, :], ps[0:KR, 7, :], sn[0:KR, :], ALU.mult).then_inc(rope_done, 1)
                dve.wait_ge(rope_done, 4 * c + 4)
                step(v.tensor_tensor(ra[:, b, :], ra[:, b, :], rb[:, b, :], ALU.add))
                step(v.tensor_tensor(rk[0:KR, b, :], rk[0:KR, b, :], rl[0:KR, b, :], ALU.add))
                settle()
                if c >= 2:
                    dve.wait_ge(st_qk[b], 32 * (c // 2))
                step(v.tensor_copy(q3[:, b, 0, :], ra[:, b, :]))
                step(v.tensor_copy(k3[0:KR, b, 0, :], rk[0:KR, b, :]))
                settle()
                step(v.tensor_tensor(ra[:, b, :], ra[:, b, :], q3[:, b, 0, :], ALU.subtract))
                step(v.tensor_tensor(rk[0:KR, b, :], rk[0:KR, b, :], k3[0:KR, b, 0, :], ALU.subtract))
                settle()
                step(v.tensor_copy(q3[:, b, 1, :], ra[:, b, :]))
                step(v.tensor_copy(k3[0:KR, b, 1, :], rk[0:KR, b, :]))
                settle()
                v.tensor_tensor(q3[:, b, 2, :], ra[:, b, :], q3[:, b, 1, :], ALU.subtract).then_inc(split_ready, 1)
                v.tensor_tensor(k3[0:KR, b, 2, :], rk[0:KR, b, :], k3[0:KR, b, 1, :], ALU.subtract)\
                    .then_inc(split_ready, 1)

            def copy_out(n, steps):
                dve.wait_ge(pv_mm, steps)
                if n >= 2:
                    dve.wait_ge(slot_read, READ["out", n - 2])
                v.tensor_copy(oT[:, n % 2, :], ps[:, 6, :]).then_inc(o_copy, 1)

            slot_at = [0]

            def slot(what):
                m = slot_at[0]
                slot_at[0] += 1
                dve.wait_ge(slot_mm, m + 1)
                b = ps[:, slot_bank(m), :]
                if what[0] == "scores":
                    _, n, t, u, i, fit = what
                    w = (t % TPC + 1) * P if u == t // TPC else CW
                    v.tensor_reduce(mx[:, n % 2, i:i + fit, t % TPC, u],
                                    b[:, 0:fit * w].rearrange("p (h k) -> p h k", k=w), AX_X, ALU.max)\
                        .then_inc(slot_read, 1)
                    if t % TPC == TPC - 1 and u == t // TPC and i == HPG - 1:
                        maxima(n, m + 1)
                elif what[0] == "maxima":
                    n = what[1]
                    if n >= 2:
                        dve.wait_ge(ld_nm[(n - 2) % G1], 32 * ((n - 2) // G1 + 1))
                    v.tensor_copy(nrow[0:2 * HPG * TPC, n % 2, :], b[0:2 * HPG * TPC, 0:P // 2].bitcast(BF16))\
                        .then_inc(slot_read, 1)
                elif what[0] == "out":
                    n = what[1]
                    c, g = n // G1, n % G1
                    o = b.rearrange("p (n h w) -> p n h w", h=HPG, w=32)
                    chain(v.reciprocal(rden, o[:, :, :, HD]))
                    for k in range(TPC):
                        last = v.tensor_tensor(otok[:, TPC * c + k, g * HPG * HD:(g + 1) * HPG * HD]
                                               .rearrange("p (h d) -> p h d", d=HD),
                                               o[:, k, :, 0:HD],
                                               rden[:, k, :].unsqueeze(2).broadcast_to([P, HPG, HD]), ALU.mult)
                        if k < TPC - 1:
                            step(last)
                    last.then_inc(slot_read, 1)
                elif what[0] == "turned":
                    v.tensor_copy(oTT[:, what[1] % 2, :], b).then_inc(slot_read, 1)
                else:
                    c = what[1]
                    x = xt[:, TPC * c:TPC * c + TPC, :].rearrange("p n d -> p (n d)")
                    v.tensor_tensor(x, b, x, ALU.add).then_inc(slot_read, 1)
                    dve.wait_ge(slot_read, m + 1)
                    for t in tiles(c):
                        step(v.bn_stats(stats[:, t, :], xt[:, t, :]))

            def maxima(n, count):
                c = n // G1
                dve.wait_ge(slot_read, count)
                chain(v.tensor_reduce(nmx, mx[:, n % 2, :, :, 0:c + 1].rearrange("p h t u -> p (h t) u"), AX_X,
                                      ALU.max, negate=True))
                chain(v.tensor_copy(nm2[:, 0, :], nmx))
                chain(v.tensor_tensor(nres, nmx, nm2[:, 0, :], ALU.subtract))
                v.tensor_copy(nm2[:, 1, :], nres).then_inc(nm_ready, 1)

            for c in range(NC):
                if c >= NC - 2:
                    for what in FIRST[c - 2]:
                        slot(what)
                rope_and_split(c)
            for s, (n, j) in enumerate(STEPS):
                for what in SLOTS[s + 1]:
                    slot(what)
                if s >= 1 and STEPS[s - 1][0] != n:
                    copy_out(n - 1, s)
            copy_out(NITEM - 1, len(STEPS))
            for what in LAST_SLOTS:
                slot(what)

            norm(3, None, counted=True)
            low_h(1)

            def low1(slot, n, count):
                dve.wait_ge(w1_hi, count)
                v.tensor_tensor(wsp1[:, slot, 1, piece(n)], wslot[:, slot, piece(n)],
                                wsp1[:, slot, 0, piece(n)].bitcast(F32), ALU.subtract).then_inc(w1_lo, 1)

            for n in range(3):
                low1(0, n, n + 1)
            dve.wait_ge(lg1_mm, NC)
            l4 = ps[:, 2, 0:NT * 2 * E1].rearrange("p (n e) -> p n e", e=E1)
            lgv = lg.rearrange("p n (a e) -> p (n a) e", a=2)
            chain(v.tensor_reduce(sm[:, 0, :], l4, AX_X, ALU.max))
            chain(v.tensor_tensor(lgv, l4, sm[:, 0, :].unsqueeze(2).broadcast_to([P, 2 * NT, E1]), ALU.subtract))
            v.tensor_scalar(lg[:, :, E1:2 * E1], lg[:, :, E1:2 * E1], 10.0, None, ALU.mult).then_inc(lg1_max, 1)
            dve.wait_ge(lg1_exp, 1)
            exv = ex.rearrange("p n (a e) -> p (n a) e", a=2)
            chain(v.tensor_reduce(sm[:, 1, :], exv, AX_X, ALU.add))
            chain(v.reciprocal(sm[:, 2, :], sm[:, 1, :]))
            chain(v.tensor_tensor(exv, exv, sm[:, 2, :].unsqueeze(2).broadcast_to([P, 2 * NT, E1]), ALU.mult))
            chain(v.tensor_tensor(cw, ex[:, :, 0:E1], ex[:, :, E1:2 * E1], ALU.mult))
            chain(v.tensor_reduce(sm[:, 3, 0:NT], cw, AX_X, ALU.add))
            chain(v.tensor_scalar(sm[:, 3, 0:NT], sm[:, 3, 0:NT], 1e-9, None, ALU.add))
            chain(v.reciprocal(sm[:, 4, 0:NT], sm[:, 3, 0:NT]))
            v.tensor_tensor(cw, cw, sm[:, 4, 0:NT].unsqueeze(2).broadcast_to([P, NT, E1]), ALU.mult)\
                .then_inc(cw_ready, 1)

            def prod_stream(slot, c, loaded):
                dve.wait_ge(ld_cwb[slot], loaded)
                v.tensor_tensor(hcf[:, c, :], hT[:, PAD + c * CW:PAD + (c + 1) * CW], cwb[:, slot, chunk(c)],
                                ALU.mult).then_inc(hc_prod, 1)

            def low_stream(slot, c, n):
                dve.wait_ge(hc_hi, n + 1)
                v.tensor_tensor(hcw[:, slot, 1, chunk(c)], hcf[:, c, :],
                                hcw[:, slot, 0, chunk(c)].bitcast(F32), ALU.subtract).then_inc(hc_lo, 1)

            def prod_hid(n0, k):
                dve.wait_ge(ffn_silu, n0 + (k + 1))
                dve.wait_ge(ffn_u, n0 + (k + 1))
                v.tensor_tensor(prod1[:, k % NBUF, :], ps[:, 2 + k % 2, :], silg[:, k % 2, :], ALU.mult)\
                    .then_inc(ffn_prod, 1)

            def low_hid(n0, k):
                dve.wait_ge(ffn_hi, n0 + (k + 1))
                v.tensor_tensor(hid1[:, k % NBUF, 1, :], prod1[:, k % NBUF, :],
                                hid1[:, k % NBUF, 0, :].bitcast(F32), ALU.subtract).then_inc(ffn_lo, 1)

            def units1(n0, nb, it1, last_iteration):
                for k in range(MU):
                    n = (n0, k + 1) if k + 1 < MU else (nb, 0)
                    if n[0] is not None:
                        prod_hid(*n)
                    low_hid(n0, k)
                    half, u = k // HALF, k % HALF
                    if last_iteration and half:
                        continue
                    to = (half + 1) % 2
                    if u in (6, 8, 10, 12):
                        c = (u - 6) // 2
                        low_stream(to, c, it1 * (2 * NC) + ((half + 1) * NC + c))
                    if u in (4, 6, 8, 10):
                        prod_stream(to, (u - 4) // 2, it1 * 16 + 16)
                    if u in (5, 7, 9):
                        m = (u - 5) // 2
                        low1(to, m, it1 * 6 + (3 * half + 4 + m))

            for c in range(NC):
                dve.wait_ge(cw_tr, c + 1)
                v.tensor_tensor(hcf[:, c, :], ps[:, 4 + c, :], hT[:, PAD + c * CW:PAD + (c + 1) * CW], ALU.mult)\
                    .then_inc(hc_prod, 1)
            for c in range(NC):
                low_stream(0, c, c)
            prod_hid(0, 0)
            with dve.Fori(0, N_IT1 - 1) as it:
                units1(it * MU, it * MU + MU, it, False)
            units1((N_IT1 - 1) * MU, None, N_IT1 - 1, True)
            for c in range(NC):
                dve.wait_ge(y1_tr, c + 1)
                v.tensor_tensor(obuf[:, TPC * c:TPC * c + TPC, :].rearrange("p n d -> p (n d)"), ps[:, 2 + c % 2, :],
                                xt[:, TPC * c:TPC * c + TPC, :].rearrange("p n d -> p (n d)"), ALU.add)\
                    .then_inc(out_ready, 1)


_INS = ['L0_attn_x', 'L0_attn_W_in', 'L0_attn_w_conv', 'L0_attn_b_conv', 'L0_attn_theta', 'L0_attn_decay_slopes',
        'L0_attn_anchor_slopes', 'L0_attn_score_scale', 'L0_attn_deriv_logits', 'L0_attn_norm_scale', 'L0_attn_W_re',
        'L0_attn_W_im', 'L0_attn_W_out', 'L0_ffn_router_w', 'L0_ffn_correction_bias', 'L0_ffn_up_w',
        'L0_ffn_down_w', 'L0_ffn_shared_up_w', 'L0_ffn_shared_down_w', 'L0_c', 'L0_wmod', 'L1_attn_Wqa',
        'L1_attn_Wqb', 'L1_attn_Wkva', 'L1_attn_Wkvb', 'L1_attn_Wout', 'L1_attn_bout', 'L1_ffn_w_router',
        'L1_ffn_w_gating', 'L1_ffn_w_gate', 'L1_ffn_w_up', 'L1_ffn_w_down', 'L1_c', 'L1_wmod']


def _constants():
    import numpy as np

    f32 = np.float32

    def bf16_bits(x):
        return (x.astype(f32).view(np.uint32) >> 16).astype(np.uint16)

    ident = np.eye(P, dtype=f32)
    i = np.arange(P)
    later = (i[None, :] > i[:, None])
    pos = np.arange(T, dtype=f32)
    dist = np.broadcast_to(pos[None, :], (P, T)).copy()
    n_anchor = 4
    dist[0:(K0 - n_anchor) * H0] = (T - 1 - pos)[None, :]
    freq = (1.0 / np.float32(10000.0) ** (np.arange(0, HD, 2, dtype=f32) / f32(HD))).astype(f32)
    ang = (pos[:, None] * freq[None, :]).astype(f32).astype(np.float64)
    d = i % HD
    cos = np.cos(ang).astype(f32).T[d // 2]
    sin = np.sin(ang).astype(f32).T[d // 2] * np.where(d % 2 == 0, -1.0, 1.0).astype(f32)[:, None]
    sel = np.zeros((P, NPAIR // 2, P), f32)
    for n in range(NPAIR // 2):
        for j in range(2):
            for m in range(3):
                sel[m * EH + 2 * n + j, n, j * I0:(j + 1) * I0] = 1.0
    return {
        "ident": ident, "identb": bf16_bits(ident),
        "maskqk": bf16_bits(np.where(later, -BIG, 0.0)), "maskkq": bf16_bits(np.where(later.T, -BIG, 0.0)),
        "blk": (i[:, None] // H0 == i[None, :] // H0).astype(f32), "dist": dist,
        "ropec": np.ascontiguousarray(cos, dtype=f32), "ropes": np.ascontiguousarray(sin, dtype=f32),
        "sel": bf16_bits(sel.reshape(P, NPAIR // 2 * P)),
    }


def kernel(**inputs):
    import numpy as np
    import concourse.bacc as bacc
    from concourse.bass_utils import run_bass_kernel_spmd

    nc = bacc.Bacc("TRN2", target_bir_lowering=False, num_devices=1)
    arrays, aps = {}, {}
    every = {name: np.ascontiguousarray(inputs[name]) for name in _INS}
    every.update(_constants())
    for name, a in every.items():
        arrays[f"in_{name}"] = a
        aps[name] = nc.dram_tensor(f"in_{name}", a.shape, mybir.dt.from_np(a.dtype), kind="ExternalInput").ap()
        if a.dtype == np.uint16:
            aps[name] = aps[name].bitcast(BF16)
    out = nc.dram_tensor("out_0", (1, T, D), F32, kind="ExternalOutput").ap()
    adaln_two_layers(nc, aps, out)
    r = run_bass_kernel_spmd(nc, [arrays], core_ids=[0])
    return r.results[0]["out_0"]
```
